# Optimizing a Trainium2 kernel written in Bass

```python
import numpy as np
import jax
import jax.numpy as jnp

def _softmax(x, axis=-1):
    return jax.nn.softmax(x, axis=axis)

def _gelu(x):
    return jax.nn.gelu(x, approximate=True)

def _silu(x):
    return jax.nn.silu(x)

def _sigmoid(x):
    return jax.nn.sigmoid(x)

def _layernorm(x, axis=-1, eps=1e-05):
    m = jnp.mean(x, axis=axis, keepdims=True)
    v = jnp.var(x, axis=axis, keepdims=True)
    return (x - m) / jnp.sqrt(v + eps)

def _scatter_add(tgt, idx, src, axis=0):
    return tgt.at[idx].add(src)

def _segment_sum(src, seg, n):
    return jax.ops.segment_sum(src, seg, n)
kernel_name = 'mk_xattn_ffn_d4_seqx_r8_42974d'

def setup_inputs(seed: int=0):
    np.random.seed(seed)
    _w = jnp.asarray

    def _rec_inputs():
        import jax
        import jax.numpy as jnp
        _rk = jax.random.key(seed)
        x = -0.0003929 + 0.9999 * jax.random.normal(jax.random.fold_in(_rk, 1), (8, 256, 128), jnp.float32)
        _lenS = 256 - jax.random.randint(jax.random.fold_in(_rk, 7), (8,), 0, max(1, 256 // 4) + 1, jnp.int32)
        _lenS2 = 1601 - jax.random.randint(jax.random.fold_in(_rk, 8), (8,), 0, max(1, 1601 // 4) + 1, jnp.int32)
        _ctx_512P = jax.random.normal(jax.random.fold_in(_rk, 11), (8, 16, 64), jnp.float32)
        _ctx_512c = jax.random.dirichlet(jax.random.fold_in(_rk, 511), 0.3 * jnp.ones((16,), jnp.float32), (8, 1601))
        _ctx_512t = jnp.einsum('bsk,bkd->bsd', _ctx_512c, _ctx_512P)
        _ctx_512t = _ctx_512t * jax.lax.rsqrt(jnp.mean(jnp.square(_ctx_512t)) + 1e-12) * 0.953939
        ctx_512 = -1.39393e-06 + 0.999914 * (_ctx_512t + 0.3 * jax.random.normal(jax.random.fold_in(_rk, 611), (8, 1601, 64), jnp.float32))
        return (x, ctx_512)
    x, ctx_512 = _rec_inputs()

    def _L0_xattn_setup():
        import jax, jax.numpy as jnp
        import numpy as np
        HEADS = 16
        D_MODEL = 128
        IMG_MODEL = 64
        D_K = D_MODEL // HEADS
        key = jax.random.key(seed)
        ks = jax.random.split(key, 12)
        B, LQ, LKV = (8, 256, 128)
        s_dm = 1.0 / np.sqrt(D_MODEL)
        s_im = 1.0 / np.sqrt(IMG_MODEL)
        return {'q': jax.random.normal(ks[0], (B, LQ, D_MODEL), jnp.float32), 'k': jax.random.normal(ks[1], (B, LKV, IMG_MODEL), jnp.float32), 'v': jax.random.normal(ks[2], (B, LKV, IMG_MODEL), jnp.float32), 'Wq': jax.random.normal(ks[3], (D_MODEL, D_MODEL), jnp.float32) * s_dm, 'bq': jnp.zeros((D_MODEL,), jnp.float32), 'Wk': jax.random.normal(ks[4], (IMG_MODEL, D_MODEL), jnp.float32) * s_im, 'bk': jnp.zeros((D_MODEL,), jnp.float32), 'Wv': jax.random.normal(ks[5], (IMG_MODEL, D_MODEL), jnp.float32) * s_im, 'bv': jnp.zeros((D_MODEL,), jnp.float32), 'Wo': jax.random.normal(ks[6], (D_MODEL, D_MODEL), jnp.float32) * s_dm, 'bo': jnp.zeros((D_MODEL,), jnp.float32)}
    _L0_xattn_all = _L0_xattn_setup()
    _L0_xattn_in = {k: v for k, v in _L0_xattn_all.items() if k in ('Wq', 'bq', 'Wk', 'bk', 'Wv', 'bv', 'Wo', 'bo')}
    del _L0_xattn_all

    def _L0_ffn_setup():
        import jax, jax.numpy as jnp
        import numpy as np
        D = 128
        H = 16
        HD = D // H
        L = 64
        E = 8
        B, T = (4, 256)
        EPS = 1e-06

        def _glorot(k, shape):
            fan_in, fan_out = (shape[-2], shape[-1])
            lim = np.sqrt(6.0 / (fan_in + fan_out)).astype(np.float32)
            return jax.random.uniform(k, shape, jnp.float32, -lim, lim)

        def _rmsnorm(x, gamma):
            return gamma * x * jax.lax.rsqrt(jnp.mean(x * x, axis=-1, keepdims=True) + EPS)
        key = jax.random.key(seed)
        ks = jax.random.split(key, 8)
        return {'x': jax.random.normal(ks[0], (B, T, D), jnp.float32), 'gamma1': jnp.ones((D,), jnp.float32), 'Wq': _glorot(ks[1], (D, D)), 'bq': jnp.zeros((D,), jnp.float32), 'Wdown': _glorot(ks[2], (D, L)), 'bdown': jnp.zeros((L,), jnp.float32), 'Wup': _glorot(ks[3], (L, 2 * D)), 'bup': jnp.zeros((2 * D,), jnp.float32), 'Wo': _glorot(ks[4], (D, D)), 'bo': jnp.zeros((D,), jnp.float32), 'gamma2': jnp.ones((D,), jnp.float32), 'Wg': _glorot(ks[5], (D, E)), 'bg': jnp.zeros((E,), jnp.float32), 'We': _glorot(ks[6], (E, D, D))}
    _L0_ffn_all = _L0_ffn_setup()
    _L0_ffn_in = {k: v for k, v in _L0_ffn_all.items() if k in ('gamma1', 'Wq', 'bq', 'Wdown', 'bdown', 'Wup', 'bup', 'Wo', 'bo', 'gamma2', 'Wg', 'bg', 'We')}
    del _L0_ffn_all

    def _L1_xattn_setup():
        import jax, jax.numpy as jnp
        import numpy as np
        NUM_HEADS = 16
        HEAD_DIM = 64
        Q_DIM = 128
        KV_DIM = 64
        INNER = NUM_HEADS * HEAD_DIM
        key = jax.random.key(seed)
        ks = jax.random.split(key, 7)
        B, N, M = (32, 128, 256)
        q = jax.random.normal(ks[0], (B, N, Q_DIM), dtype=jnp.float32)
        kv = jax.random.normal(ks[1], (B, M, KV_DIM), dtype=jnp.float32)
        Wq = jax.random.normal(ks[2], (Q_DIM, INNER), dtype=jnp.float32) / np.sqrt(Q_DIM)
        Wk = jax.random.normal(ks[3], (KV_DIM, INNER), dtype=jnp.float32) / np.sqrt(KV_DIM)
        Wv = jax.random.normal(ks[4], (KV_DIM, INNER), dtype=jnp.float32) / np.sqrt(KV_DIM)
        Wo = jax.random.normal(ks[5], (INNER, Q_DIM), dtype=jnp.float32) / np.sqrt(INNER)
        bo = jax.random.normal(ks[6], (Q_DIM,), dtype=jnp.float32) * 0.01
        return {'q': q, 'kv': kv, 'Wq': Wq, 'Wk': Wk, 'Wv': Wv, 'Wo': Wo, 'bo': bo}
    _L1_xattn_all = _L1_xattn_setup()
    _L1_xattn_in = {k: v for k, v in _L1_xattn_all.items() if k in ('Wq', 'Wk', 'Wv', 'Wo', 'bo')}
    del _L1_xattn_all

    def _L1_ffn_setup():
        import jax, jax.numpy as jnp
        import numpy as np
        B, S, D_MODEL, D_HIDDEN = (4, 256, 128, 512)

        def act_quant(x):
            scale = 127.0 / jnp.clip(jnp.max(jnp.abs(x), axis=-1, keepdims=True), 1e-05)
            return jnp.clip(jnp.round(x * scale), -128, 127) / scale

        def weight_quant(w):
            scale = 1.0 / jnp.clip(jnp.mean(jnp.abs(w)), 1e-05)
            return jnp.clip(jnp.round(w * scale), -1, 1) / scale

        def bit_linear(x, w):
            xq = x + jax.lax.stop_gradient(act_quant(x) - x)
            wq = w + jax.lax.stop_gradient(weight_quant(w) - w)
            return jnp.einsum('bsd,hd->bsh', xq, wq)

        def depthwise_conv1d(x_bcl, w, b):
            y = jax.lax.conv_general_dilated(x_bcl, w, window_strides=(1,), padding=[(1, 1)], dimension_numbers=('NCH', 'OIH', 'NCH'), feature_group_count=x_bcl.shape[1])
            return y + b[None, :, None]
        key = jax.random.key(seed)
        ks = jax.random.split(key, 5)
        lim1 = 1.0 / np.sqrt(D_MODEL)
        lim2 = 1.0 / np.sqrt(D_HIDDEN)
        limc = 1.0 / np.sqrt(3.0)
        return {'x': jax.random.normal(ks[0], (B, S, D_MODEL), dtype=jnp.float32), 'w1': jax.random.uniform(ks[1], (D_HIDDEN, D_MODEL), jnp.float32, -lim1, lim1), 'conv_w': jax.random.uniform(ks[2], (D_HIDDEN, 1, 3), jnp.float32, -limc, limc), 'conv_b': jax.random.uniform(ks[3], (D_HIDDEN,), jnp.float32, -limc, limc), 'w2': jax.random.uniform(ks[4], (D_MODEL, D_HIDDEN), jnp.float32, -lim2, lim2)}
    _L1_ffn_all = _L1_ffn_setup()
    _L1_ffn_in = {k: v for k, v in _L1_ffn_all.items() if k in ('w1', 'conv_w', 'conv_b', 'w2')}
    del _L1_ffn_all

    def _L2_xattn_setup():
        import jax, jax.numpy as jnp
        import numpy as np
        B, LQ, LK = (8, 256, 256)
        QD, KD, VD = (128, 64, 64)
        key = jax.random.key(seed)
        ks = jax.random.split(key, 9)
        s = 0.02
        return {'query': jax.random.normal(ks[0], (B, LQ, QD), jnp.float32), 'key': jax.random.normal(ks[1], (B, LK, KD), jnp.float32), 'value': jax.random.normal(ks[2], (B, LK, VD), jnp.float32), 'Wq': jax.random.normal(ks[3], (QD, QD), jnp.float32) * s, 'bq': jnp.zeros((QD,), jnp.float32), 'Wk': jax.random.normal(ks[4], (KD, QD), jnp.float32) * s, 'bk': jnp.zeros((QD,), jnp.float32), 'Wv': jax.random.normal(ks[5], (VD, QD), jnp.float32) * s, 'bv': jnp.zeros((QD,), jnp.float32)}
    _L2_xattn_all = _L2_xattn_setup()
    _L2_xattn_in = {k: v for k, v in _L2_xattn_all.items() if k in ('Wq', 'bq', 'Wk', 'bk', 'Wv', 'bv')}
    del _L2_xattn_all

    def _L2_ffn_setup():
        import jax, jax.numpy as jnp
        import numpy as np
        D_MODEL = 128
        FFN_DIM = 256
        NUM_EXPERTS = 8
        NUM_GROUPS = 4
        EXPERTS_PER_GROUP = NUM_EXPERTS // NUM_GROUPS
        TOP_K = 2
        GROUPS_TOP_K = 1
        EPS = 1e-09

        def _topk_normalized(scores, k):
            vals, idx = jax.lax.top_k(scores, k)
            vals = vals / (jnp.sum(vals, axis=-1, keepdims=True) + EPS)
            return (vals, idx)
        key = jax.random.key(seed)
        ks = jax.random.split(key, 6)
        B, S = (2, 128)
        x = jax.random.normal(ks[0], (B, S, D_MODEL), dtype=jnp.float32)
        sd = 0.02
        macro_w = jax.random.normal(ks[1], (D_MODEL, NUM_GROUPS), dtype=jnp.float32) * sd
        micro_w = jax.random.normal(ks[2], (NUM_GROUPS, D_MODEL, EXPERTS_PER_GROUP), dtype=jnp.float32) * sd
        gate_w = jax.random.normal(ks[3], (NUM_EXPERTS, D_MODEL, FFN_DIM), dtype=jnp.float32) * sd
        up_w = jax.random.normal(ks[4], (NUM_EXPERTS, D_MODEL, FFN_DIM), dtype=jnp.float32) * sd
        down_w = jax.random.normal(ks[5], (NUM_EXPERTS, FFN_DIM, D_MODEL), dtype=jnp.float32) * sd
        return {'x': x, 'macro_w': macro_w, 'micro_w': micro_w, 'gate_w': gate_w, 'up_w': up_w, 'down_w': down_w}
    _L2_ffn_all = _L2_ffn_setup()
    _L2_ffn_in = {k: v for k, v in _L2_ffn_all.items() if k in ('macro_w', 'micro_w', 'gate_w', 'up_w', 'down_w')}
    del _L2_ffn_all

    def _L3_xattn_setup():
        import jax, jax.numpy as jnp
        import numpy as np
        DIM = 128
        LATENT_DIM = 64
        NUM_HEADS = 16
        HEAD_DIM = DIM // NUM_HEADS
        SCALE = HEAD_DIM ** (-0.5)
        key = jax.random.key(seed)
        k1, k2, k3, k4, k5 = jax.random.split(key, 5)
        B, xN, zN = (2, 256, 256)
        x = jax.random.normal(k1, (B, xN, DIM), dtype=jnp.float32)
        z = jax.random.normal(k2, (B, zN, LATENT_DIM), dtype=jnp.float32)
        Wq = jax.random.normal(k3, (DIM, DIM), dtype=jnp.float32) * DIM ** (-0.5)
        Wkv = jax.random.normal(k4, (2 * DIM, LATENT_DIM), dtype=jnp.float32) * LATENT_DIM ** (-0.5)
        Wo = jax.random.normal(k5, (DIM, DIM), dtype=jnp.float32) * DIM ** (-0.5)
        return {'x': x, 'z': z, 'Wq': Wq, 'Wkv': Wkv, 'Wo': Wo}
    _L3_xattn_all = _L3_xattn_setup()
    _L3_xattn_in = {k: v for k, v in _L3_xattn_all.items() if k in ('Wq', 'Wkv', 'Wo')}
    del _L3_xattn_all

    def _L3_ffn_setup():
        import jax, jax.numpy as jnp
        import numpy as np
        E = 32
        H = 128
        I = 64
        G = 8
        TKG = 4
        TOPK = 8
        NSH = 2
        SCALE = 2.5
        key = jax.random.key(seed)
        ks = jax.random.split(key, 10)
        s = 0.02
        return {'hidden_states': jax.random.normal(ks[0], (2, 128, H), jnp.float32), 'gate_w': jax.random.normal(ks[1], (E, H), jnp.float32) * s, 'gate_bias': jax.random.normal(ks[2], (E,), jnp.float32) * s, 'w_gate': jax.random.normal(ks[3], (E, I, H), jnp.float32) * s, 'w_up': jax.random.normal(ks[4], (E, I, H), jnp.float32) * s, 'w_down': jax.random.normal(ks[5], (E, H, I), jnp.float32) * s, 'sh_gate': jax.random.normal(ks[6], (I * NSH, H), jnp.float32) * s, 'sh_up': jax.random.normal(ks[7], (I * NSH, H), jnp.float32) * s, 'sh_down': jax.random.normal(ks[8], (H, I * NSH), jnp.float32) * s}
    _L3_ffn_all = _L3_ffn_setup()
    _L3_ffn_in = {k: v for k, v in _L3_ffn_all.items() if k in ('gate_w', 'gate_bias', 'w_gate', 'w_up', 'w_down', 'sh_gate', 'sh_up', 'sh_down')}
    del _L3_ffn_all
    return {'x': x, 'ctx_512': ctx_512, 'L0_xattn_Wq': _L0_xattn_in['Wq'], 'L0_xattn_bq': _L0_xattn_in['bq'], 'L0_xattn_Wk': _L0_xattn_in['Wk'], 'L0_xattn_bk': _L0_xattn_in['bk'], 'L0_xattn_Wv': _L0_xattn_in['Wv'], 'L0_xattn_bv': _L0_xattn_in['bv'], 'L0_xattn_Wo': _L0_xattn_in['Wo'], 'L0_xattn_bo': _L0_xattn_in['bo'], 'L0_ffn_gamma1': _L0_ffn_in['gamma1'], 'L0_ffn_Wq': _L0_ffn_in['Wq'], 'L0_ffn_bq': _L0_ffn_in['bq'], 'L0_ffn_Wdown': _L0_ffn_in['Wdown'], 'L0_ffn_bdown': _L0_ffn_in['bdown'], 'L0_ffn_Wup': _L0_ffn_in['Wup'], 'L0_ffn_bup': _L0_ffn_in['bup'], 'L0_ffn_Wo': _L0_ffn_in['Wo'], 'L0_ffn_bo': _L0_ffn_in['bo'], 'L0_ffn_gamma2': _L0_ffn_in['gamma2'], 'L0_ffn_Wg': _L0_ffn_in['Wg'], 'L0_ffn_bg': _L0_ffn_in['bg'], 'L0_ffn_We': _L0_ffn_in['We'], 'L1_xattn_Wq': _L1_xattn_in['Wq'], 'L1_xattn_Wk': _L1_xattn_in['Wk'], 'L1_xattn_Wv': _L1_xattn_in['Wv'], 'L1_xattn_Wo': _L1_xattn_in['Wo'], 'L1_xattn_bo': _L1_xattn_in['bo'], 'L1_ffn_w1': _L1_ffn_in['w1'], 'L1_ffn_conv_w': _L1_ffn_in['conv_w'], 'L1_ffn_conv_b': _L1_ffn_in['conv_b'], 'L1_ffn_w2': _L1_ffn_in['w2'], 'L2_xattn_Wq': _L2_xattn_in['Wq'], 'L2_xattn_bq': _L2_xattn_in['bq'], 'L2_xattn_Wk': _L2_xattn_in['Wk'], 'L2_xattn_bk': _L2_xattn_in['bk'], 'L2_xattn_Wv': _L2_xattn_in['Wv'], 'L2_xattn_bv': _L2_xattn_in['bv'], 'L2_ffn_macro_w': _L2_ffn_in['macro_w'], 'L2_ffn_micro_w': _L2_ffn_in['micro_w'], 'L2_ffn_gate_w': _L2_ffn_in['gate_w'], 'L2_ffn_up_w': _L2_ffn_in['up_w'], 'L2_ffn_down_w': _L2_ffn_in['down_w'], 'L3_xattn_Wq': _L3_xattn_in['Wq'], 'L3_xattn_Wkv': _L3_xattn_in['Wkv'], 'L3_xattn_Wo': _L3_xattn_in['Wo'], 'L3_ffn_gate_w': _L3_ffn_in['gate_w'], 'L3_ffn_gate_bias': _L3_ffn_in['gate_bias'], 'L3_ffn_w_gate': _L3_ffn_in['w_gate'], 'L3_ffn_w_up': _L3_ffn_in['w_up'], 'L3_ffn_w_down': _L3_ffn_in['w_down'], 'L3_ffn_sh_gate': _L3_ffn_in['sh_gate'], 'L3_ffn_sh_up': _L3_ffn_in['sh_up'], 'L3_ffn_sh_down': _L3_ffn_in['sh_down']}

def reference(x, ctx_512, L0_xattn_Wq, L0_xattn_bq, L0_xattn_Wk, L0_xattn_bk, L0_xattn_Wv, L0_xattn_bv, L0_xattn_Wo, L0_xattn_bo, L0_ffn_gamma1, L0_ffn_Wq, L0_ffn_bq, L0_ffn_Wdown, L0_ffn_bdown, L0_ffn_Wup, L0_ffn_bup, L0_ffn_Wo, L0_ffn_bo, L0_ffn_gamma2, L0_ffn_Wg, L0_ffn_bg, L0_ffn_We, L1_xattn_Wq, L1_xattn_Wk, L1_xattn_Wv, L1_xattn_Wo, L1_xattn_bo, L1_ffn_w1, L1_ffn_conv_w, L1_ffn_conv_b, L1_ffn_w2, L2_xattn_Wq, L2_xattn_bq, L2_xattn_Wk, L2_xattn_bk, L2_xattn_Wv, L2_xattn_bv, L2_ffn_macro_w, L2_ffn_micro_w, L2_ffn_gate_w, L2_ffn_up_w, L2_ffn_down_w, L3_xattn_Wq, L3_xattn_Wkv, L3_xattn_Wo, L3_ffn_gate_w, L3_ffn_gate_bias, L3_ffn_w_gate, L3_ffn_w_up, L3_ffn_w_down, L3_ffn_sh_gate, L3_ffn_sh_up, L3_ffn_sh_down):
    import jax
    import jax.numpy as jnp

    def _L0_xattn_ref(q, k, v, Wq, bq, Wk, bk, Wv, bv, Wo, bo):
        import jax, jax.numpy as jnp
        import numpy as np
        HEADS = 16
        D_MODEL = 128
        IMG_MODEL = 64
        D_K = D_MODEL // HEADS
        B, LQ, _ = q.shape
        LKV = k.shape[1]
        qh = (q @ Wq + bq).reshape(B, LQ, HEADS, D_K).transpose(0, 2, 1, 3)
        kh = (k @ Wk + bk).reshape(B, LKV, HEADS, D_K).transpose(0, 2, 1, 3)
        vh = (v @ Wv + bv).reshape(B, LKV, HEADS, D_K).transpose(0, 2, 1, 3)
        scale = 1.0 / np.sqrt(D_K)
        scores = jnp.einsum('bhqd,bhkd->bhqk', qh, kh) * scale
        attn = jax.nn.softmax(scores, axis=-1)
        out = jnp.einsum('bhqk,bhkd->bhqd', attn, vh)
        concat = out.transpose(0, 2, 1, 3).reshape(B, LQ, D_MODEL)
        return concat @ Wo + bo

    def _L0_ffn_ref(x, gamma1, Wq, bq, Wdown, bdown, Wup, bup, Wo, bo, gamma2, Wg, bg, We):
        import jax, jax.numpy as jnp
        import numpy as np
        D = 128
        H = 16
        HD = D // H
        L = 64
        E = 8
        B, T = (4, 256)
        EPS = 1e-06

        def _glorot(k, shape):
            fan_in, fan_out = (shape[-2], shape[-1])
            lim = np.sqrt(6.0 / (fan_in + fan_out)).astype(np.float32)
            return jax.random.uniform(k, shape, jnp.float32, -lim, lim)

        def _rmsnorm(x, gamma):
            return gamma * x * jax.lax.rsqrt(jnp.mean(x * x, axis=-1, keepdims=True) + EPS)
        b, t = (x.shape[0], x.shape[1])
        h = _rmsnorm(x, gamma1)
        q = (h @ Wq + bq).reshape(b, t, H, HD)
        kv = ((h @ Wdown + bdown) @ Wup + bup).reshape(b, t, H, 2 * HD)
        k, v = jnp.split(kv, 2, axis=-1)
        att = jnp.einsum('bthd,btgd->bthg', q, k) / np.sqrt(HD).astype(np.float32)
        att = jax.nn.softmax(att, axis=-1)
        out = jnp.einsum('bthg,btgd->bthd', att, v).reshape(b, t, D)
        x = x + (out @ Wo + bo)
        h2 = _rmsnorm(x, gamma2)
        gate = jax.nn.softmax(h2 @ Wg + bg, axis=-1)
        combined = jnp.einsum('btd,edf,bte->btf', h2, We, gate)
        return x + combined

    def _L1_xattn_ref(q, kv, Wq, Wk, Wv, Wo, bo):
        import jax, jax.numpy as jnp
        import numpy as np
        NUM_HEADS = 16
        HEAD_DIM = 64
        Q_DIM = 128
        KV_DIM = 64
        INNER = NUM_HEADS * HEAD_DIM
        B, N, _ = q.shape
        M = kv.shape[1]
        scale = HEAD_DIM ** (-0.5)
        qh = (q @ Wq).reshape(B, N, NUM_HEADS, HEAD_DIM).transpose(0, 2, 1, 3)
        kh = (kv @ Wk).reshape(B, M, NUM_HEADS, HEAD_DIM).transpose(0, 2, 1, 3)
        vh = (kv @ Wv).reshape(B, M, NUM_HEADS, HEAD_DIM).transpose(0, 2, 1, 3)
        scores = jnp.einsum('bhnd,bhmd->bhnm', qh, kh) * scale
        attn = jax.nn.softmax(scores, axis=-1)
        out = jnp.einsum('bhnm,bhmd->bhnd', attn, vh)
        out = out.transpose(0, 2, 1, 3).reshape(B, N, INNER)
        return out @ Wo + bo

    def _L1_ffn_ref(x, w1, conv_w, conv_b, w2):
        import jax, jax.numpy as jnp
        import numpy as np
        B, S, D_MODEL, D_HIDDEN = (4, 256, 128, 512)

        def act_quant(x):
            scale = 127.0 / jnp.clip(jnp.max(jnp.abs(x), axis=-1, keepdims=True), 1e-05)
            return jnp.clip(jnp.round(x * scale), -128, 127) / scale

        def weight_quant(w):
            scale = 1.0 / jnp.clip(jnp.mean(jnp.abs(w)), 1e-05)
            return jnp.clip(jnp.round(w * scale), -1, 1) / scale

        def bit_linear(x, w):
            xq = x + jax.lax.stop_gradient(act_quant(x) - x)
            wq = w + jax.lax.stop_gradient(weight_quant(w) - w)
            return jnp.einsum('bsd,hd->bsh', xq, wq)

        def depthwise_conv1d(x_bcl, w, b):
            y = jax.lax.conv_general_dilated(x_bcl, w, window_strides=(1,), padding=[(1, 1)], dimension_numbers=('NCH', 'OIH', 'NCH'), feature_group_count=x_bcl.shape[1])
            return y + b[None, :, None]
        h = bit_linear(x, w1)
        h = depthwise_conv1d(h.transpose(0, 2, 1), conv_w, conv_b)
        h = h.transpose(0, 2, 1)
        h = jax.nn.silu(h)
        return bit_linear(h, w2)

    def _L2_xattn_ref(query, key, value, Wq, bq, Wk, bk, Wv, bv):
        import jax, jax.numpy as jnp
        import numpy as np
        B, LQ, LK = (8, 256, 256)
        QD, KD, VD = (128, 64, 64)
        q = jnp.einsum('bld,de->ble', query, Wq) + bq
        k = jnp.einsum('bld,de->ble', key, Wk) + bk
        v = jnp.einsum('bld,de->ble', value, Wv) + bv
        scores = jnp.einsum('bqe,bke->bqk', q, k)
        attn = jax.nn.softmax(scores, axis=-1)
        out = jnp.einsum('bqk,bke->bqe', attn, v)
        return out

    def _L2_ffn_ref(x, macro_w, micro_w, gate_w, up_w, down_w):
        import jax, jax.numpy as jnp
        import numpy as np
        D_MODEL = 128
        FFN_DIM = 256
        NUM_EXPERTS = 8
        NUM_GROUPS = 4
        EXPERTS_PER_GROUP = NUM_EXPERTS // NUM_GROUPS
        TOP_K = 2
        GROUPS_TOP_K = 1
        EPS = 1e-09

        def _topk_normalized(scores, k):
            vals, idx = jax.lax.top_k(scores, k)
            vals = vals / (jnp.sum(vals, axis=-1, keepdims=True) + EPS)
            return (vals, idx)
        B, S, D = x.shape
        T = B * S
        xf = x.reshape(T, D)
        macro_scores = jax.nn.sigmoid(xf @ macro_w)
        mv, mi = _topk_normalized(macro_scores, GROUPS_TOP_K)
        macro_full = jnp.sum(jax.nn.one_hot(mi, NUM_GROUPS, dtype=xf.dtype) * mv[..., None], axis=1)
        micro_scores = jax.nn.sigmoid(jnp.einsum('td,gde->tge', xf, micro_w))
        uv, ui = _topk_normalized(micro_scores, TOP_K)
        micro_full = jnp.sum(jax.nn.one_hot(ui, EXPERTS_PER_GROUP, dtype=xf.dtype) * uv[..., None], axis=2)
        w = (macro_full[:, :, None] * micro_full).reshape(T, NUM_EXPERTS)
        gate = jax.nn.silu(jnp.einsum('td,edf->tef', xf, gate_w))
        up = jnp.einsum('td,edf->tef', xf, up_w)
        h = gate * up
        out = jnp.einsum('te,tef,efd->td', w, h, down_w)
        return out.reshape(B, S, D)

    def _L3_xattn_ref(x, z, Wq, Wkv, Wo):
        import jax, jax.numpy as jnp
        import numpy as np
        DIM = 128
        LATENT_DIM = 64
        NUM_HEADS = 16
        HEAD_DIM = DIM // NUM_HEADS
        SCALE = HEAD_DIM ** (-0.5)
        B, xN, _ = x.shape
        _, zN, _ = z.shape
        Q = (x @ Wq.T).reshape(B, xN, NUM_HEADS, HEAD_DIM)
        KV = (z @ Wkv.T).reshape(B, zN, 2, NUM_HEADS, HEAD_DIM)
        K = KV[:, :, 0]
        V = KV[:, :, 1]
        attn = jnp.einsum('bqhd,bkhd->bhqk', Q, K) * SCALE
        attn = jax.nn.softmax(attn, axis=-1)
        O = jnp.einsum('bhqk,bkhd->bqhd', attn, V).reshape(B, xN, DIM)
        return O @ Wo.T

    def _L3_ffn_ref(hidden_states, gate_w, gate_bias, w_gate, w_up, w_down, sh_gate, sh_up, sh_down):
        import jax, jax.numpy as jnp
        import numpy as np
        E = 32
        H = 128
        I = 64
        G = 8
        TKG = 4
        TOPK = 8
        NSH = 2
        SCALE = 2.5
        B, S, Hd = hidden_states.shape
        h = hidden_states.reshape(-1, Hd)
        logits = h.astype(jnp.float32) @ gate_w.T
        scores = jax.nn.sigmoid(logits)
        sc = scores + gate_bias
        grp = sc.reshape(-1, G, E // G)
        group_scores = jax.lax.top_k(grp, 2)[0].sum(-1)
        gidx = jax.lax.top_k(group_scores, TKG)[1]
        gmask = jnp.sum(jax.nn.one_hot(gidx, G, dtype=sc.dtype), axis=1)
        smask = jnp.repeat(gmask, E // G, axis=1)
        masked = jnp.where(smask > 0, sc, jnp.zeros_like(sc))
        tki = jax.lax.top_k(masked, TOPK)[1]
        tkw = jnp.take_along_axis(scores, tki, axis=1)
        tkw = tkw / (tkw.sum(-1, keepdims=True) + 1e-20)
        tkw = tkw * SCALE
        combine = (jax.nn.one_hot(tki, E, dtype=tkw.dtype) * tkw[..., None]).sum(1)
        g = jax.nn.silu(jnp.einsum('th,eih->tei', h, w_gate))
        u = jnp.einsum('th,eih->tei', h, w_up)
        routed = jnp.einsum('tei,ehi->th', g * u * combine[:, :, None], w_down)
        sg = jax.nn.silu(h @ sh_gate.T)
        shared = sg * (h @ sh_up.T) @ sh_down.T
        return (routed + shared).reshape(B, S, Hd)
    x = x + _L0_xattn_ref(_layernorm(x, axis=-1), ctx_512, ctx_512, L0_xattn_Wq, L0_xattn_bq, L0_xattn_Wk, L0_xattn_bk, L0_xattn_Wv, L0_xattn_bv, L0_xattn_Wo, L0_xattn_bo)
    x = x + _L0_ffn_ref(_layernorm(x, axis=-1), L0_ffn_gamma1, L0_ffn_Wq, L0_ffn_bq, L0_ffn_Wdown, L0_ffn_bdown, L0_ffn_Wup, L0_ffn_bup, L0_ffn_Wo, L0_ffn_bo, L0_ffn_gamma2, L0_ffn_Wg, L0_ffn_bg, L0_ffn_We)
    x = x + _L1_xattn_ref(_layernorm(x, axis=-1), ctx_512, L1_xattn_Wq, L1_xattn_Wk, L1_xattn_Wv, L1_xattn_Wo, L1_xattn_bo)
    x = x + _L1_ffn_ref(_layernorm(x, axis=-1), L1_ffn_w1, L1_ffn_conv_w, L1_ffn_conv_b, L1_ffn_w2)
    x = x + _L2_xattn_ref(_layernorm(x, axis=-1), ctx_512, ctx_512, L2_xattn_Wq, L2_xattn_bq, L2_xattn_Wk, L2_xattn_bk, L2_xattn_Wv, L2_xattn_bv)
    x = x + _L2_ffn_ref(_layernorm(x, axis=-1), L2_ffn_macro_w, L2_ffn_micro_w, L2_ffn_gate_w, L2_ffn_up_w, L2_ffn_down_w)
    x = x + _L3_xattn_ref(_layernorm(x, axis=-1), ctx_512, L3_xattn_Wq, L3_xattn_Wkv, L3_xattn_Wo)
    x = x + _L3_ffn_ref(_layernorm(x, axis=-1), L3_ffn_gate_w, L3_ffn_gate_bias, L3_ffn_w_gate, L3_ffn_w_up, L3_ffn_w_down, L3_ffn_sh_gate, L3_ffn_sh_up, L3_ffn_sh_down)
    return x

_drawn_inputs = setup_inputs


def setup_inputs(seed=0):
    import zlib

    import numpy as np

    out = dict(_drawn_inputs(seed))
    spreads = {'L0_xattn_bq': (0.0, 0.373),
     'L0_xattn_bk': (0.0, 0.8),
     'L0_xattn_bv': (0.0, 0.1),
     'L0_xattn_bo': (0.0, 0.1),
     'L0_ffn_gamma1': (1.0, 0.2),
     'L0_ffn_bq': (0.0, 0.8),
     'L0_ffn_bdown': (0.0, 0.661),
     'L0_ffn_bup': (0.0, 0.345),
     'L0_ffn_bo': (0.0, 0.1),
     'L0_ffn_gamma2': (1.0, 0.2),
     'L0_ffn_bg': (0.0, 0.784),
     'L2_xattn_bq': (0.0, 0.8),
     'L2_xattn_bk': (0.0, 0.8),
     'L2_xattn_bv': (0.0, 0.1)}
    factors = {'L1_xattn_bo': 8.0,
     'L2_xattn_Wq': 8.0,
     'L2_xattn_Wk': 8.0,
     'L2_ffn_macro_w': 8.0,
     'L2_ffn_micro_w': 8.0,
     'L2_ffn_gate_w': 8.0,
     'L2_ffn_up_w': 8.0,
     'L2_ffn_down_w': 8.0,
     'L3_ffn_gate_w': 8.0,
     'L3_ffn_gate_bias': 8.0,
     'L3_ffn_w_gate': 8.0,
     'L3_ffn_w_up': 8.0,
     'L3_ffn_w_down': 8.0,
     'L3_ffn_sh_gate': 8.0,
     'L3_ffn_sh_up': 8.0,
     'L3_ffn_sh_down': 8.0}
    for name, (base, spread) in spreads.items():
        noise = np.random.default_rng([zlib.crc32(name.encode()), seed]).standard_normal(out[name].shape)
        drawn = base * np.exp(spread * noise) if base else spread * noise
        out[name] = jnp.asarray(drawn.astype(out[name].dtype))
    for name, factor in factors.items():
        out[name] = (out[name] * factor).astype(out[name].dtype)
    return out
```

```python
import math
from contextlib import ExitStack

import concourse.bass as bass
from concourse import mybir

F32 = mybir.dt.float32
F16 = mybir.dt.float16
BF16 = mybir.dt.bfloat16
ALU = mybir.AluOpType
ACT = mybir.ActivationFunctionType
AX = mybir.AxisListType

P = 128
B, S, D, DC, LK = 8, 256, 128, 64, 1601
NT = B * S // P
QT = S // P
KT = -(-LK // P)
LAST = LK - (KT - 1) * P
PIECES = [(0, 401), (401, 400), (801, 400), (1201, 400)]
NP_ = len(PIECES)
LN_EPS = 1e-5


def rows(t):
    return P if t < KT - 1 else LAST


class Plan:

    def __init__(self, ahead, body, times, behind, incs, credits):
        self.ahead, self.body, self.times, self.behind, self.incs = ahead, body, times, behind, incs
        count = dict(credits)
        for op in ahead:
            self.number(op, count, None)
        start = dict(count)
        for op in body:
            self.number(op, count, None)
        self.step = {n: count[n] - start[n] for n in count}
        for n in count:
            count[n] = start[n] + times * self.step[n]
        for op in behind:
            self.number(op, count, None)

    def number(self, op, count, _):
        for n, k in self.incs[op["kind"]].items():
            count[n] += k
        op["count"] = dict(count)
        op["by"] = self.incs[op["kind"]]

    def at(self, op, name, i, less=0):
        v = op["count"][name] - less
        return v if i is None else i * self.step[name] + v

    def all(self):
        return ([(op, None) for op in self.ahead] + [(op, i) for i in range(self.times) for op in self.body]
                + [(op, None) for op in self.behind])

    def run(self, engine, emit):
        for op in self.ahead:
            emit(op, None)
        if self.times:
            with engine.Fori(0, self.times) as i:
                for op in self.body:
                    emit(op, i)
        for op in self.behind:
            emit(op, None)


def semaphores(nc, stack, name):
    taken = []

    def clear():
        first = last = None
        for k, handle in enumerate(sorted(taken, key=lambda h: h.num)):
            first = handle.num if k == 0 or handle.num != last + 1 else first
            last = handle.num
            runs[first] = last
        for first, last in runs.items():
            nc.gpsimd.sem_clear(range(first, last + 1))
        nc.all_engine_barrier()

    def sem(n):
        handle = stack.enter_context(nc.semaphore(f"{name}_{n}"))
        taken.append(handle)
        return handle

    runs = {}
    stack.callback(clear)
    return sem


def layer_norm(nc, g, name, need_xn=False):
    with ExitStack() as c:
        sem = semaphores(nc, c, name)
        sb = lambda n, s, d=F32: c.enter_context(nc.sbuf_tensor(f"{name}_{n}", s, d))
        stats = sb("stats", [P, NT, 6])
        xn = sb("xn", [P, 4, D])
        ps = c.enter_context(nc.psum_tensor(f"{name}_ps", [P, 512], F32))
        stats_done, moments_done, std_done = sem("stats_done"), sem("moments_done"), sem("std_done")
        rstd_done, xn_done, turned, xnT_done = sem("rstd_done"), sem("xn_done"), sem("turned"), sem("xnT_done")
        block = c.enter_context(nc.Block())

        @block.vector
        def _(dve):
            for t in range(NT):
                nc.vector.bn_stats(stats[:, t, :], g.x[:, t, :]).then_inc(stats_done, 1)
            for t in range(NT):
                dve.wait_ge(stats_done, t + 1)
                nc.vector.bn_aggr(g.mv[:, t, :], stats[:, t, :]).then_inc(moments_done, 1)
            dve.wait_ge(std_done, 1)
            nc.vector.reciprocal(g.rstd[:, :], g.std[:, :]).then_inc(rstd_done, 1)
            dve.wait_ge(rstd_done, 1)
            with dve.Fori(0, NT // 4) as i:
                dve.wait_ge(turned, i + 1)
                for k in range(4):
                    r = nc.vector.tensor_scalar(xn[:, k, :], g.x4[:, i, k, :], g.mean4[:, i, k:k + 1],
                                                g.rstd4[:, i, k:k + 1], ALU.subtract, ALU.mult)
                r.then_inc(xn_done, 1)

        @block.scalar
        def _(act):
            act.wait_ge(moments_done, NT)
            nc.scalar.activation(g.std[:, :], g.mv[:, :, 1], ACT.Sqrt, bias=g.cols[:, 0:1]).then_inc(std_done, 1)
            with act.Fori(0, NT // 4) as i:
                act.wait_ge(turned, i + 2)
                nc.scalar.activation(g.xnT4[:, i, :], ps[:, :], ACT.Copy).then_inc(xnT_done, 1)

        @block.tensor
        def _(pe):
            pe.sem_inc(turned, 1)
            with pe.Fori(0, NT // 4) as i:
                pe.wait_ge(xn_done, i + 1)
                pe.wait_ge(xnT_done, i + 1)
                for k in range(4):
                    r = nc.tensor.transpose(ps[:, k * P:(k + 1) * P], xn[:, k, :], g.ident[:, :])
                r.then_inc(turned, 1)

        @block.gpsimd
        def _(pool):
            pool.sem_inc(xnT_done, 1)


def small_attention(nc, g, name, w, scale, has_bo):
    H, DH, HG, W = 16, 8, 4, 32
    G = H // HG
    MROW, SUM = 24, 8
    with ExitStack() as c:
        sem = semaphores(nc, c, name)
        sb = lambda n, s, d=F32: c.enter_context(nc.sbuf_tensor(f"{name}_{n}", s, d))
        pb = lambda n, s: c.enter_context(nc.psum_tensor(f"{name}_{n}", s, F32))
        wq, wk, wv, wo = sb("wq", [P, G, P]), sb("wk", [DC + 1, G, P]), sb("wv", [DC + 1, G, P]), sb("wo", [P, G, D])
        bq = sb("bq", [P, G])
        bqs = sb("bqs", [P, G])
        bo = sb("bo", [1, D])
        ctxT = sb("ctxT", [DC + 1, LK])
        k16 = sb("k16", [P, G, LK], F16)
        kcast = sb("kcast", [P, 401], F16)
        v = sb("v", [P, G, KT, P])
        qf, qcast, q16 = sb("qf", [P, S]), sb("qcast", [P, S], F16), sb("q16", [P, S], F16)
        q_max = sb("q_max", [P, 2, HG, S], F16)
        q_exp = sb("q_exp", [P, 2, HG, S], F16)
        mx = sb("mx", [P, QT, HG, NP_])
        negm = sb("negm", [P, QT, HG, W])
        prob = sb("prob", [P, 4, HG * S])
        acc = sb("acc", [P, S])
        rec = sb("rec", [P, S])
        on = sb("on", [P, G, S])
        ps_s, ps_m = [pb(f"ps_s{i}", [P, 1024]) for i in range(2)], [pb(f"ps_m{i}", [P, 512]) for i in range(2)]
        ps_o, ps_w = pb("ps_o", [P, 512]), pb("ps_w", [P, 512])
        loaded, ctx_loaded = sem("loaded"), sem("ctx_loaded")
        qk, ex, pv, mm, mr, nm = sem("scores"), sem("exped"), sem("pv"), sem("maxmm"), sem("maxed"), sem("negmax")
        mj, mf, kc, qs, qb = sem("side"), sem("side_free"), sem("k_cast"), sem("q_split"), sem("q_blocks")
        ac, od, init = sem("acc_out"), sem("normed"), sem("init")
        qc = sem("q_out")

        def step(s, total=None):
            ok = lambda k: total is None or 0 <= s + k < total
            gr = lambda k: (s + k) % G
            db = lambda k: (s + k) // G
            pieces = [(j, q, k) for j in range(HG) for q in range(QT) for k in range(NP_)]
            side = {}
            if ok(1):
                side[1] = dict(kind="Q2", g=gr(1), db=db(1), par=(s + 1) % 2)
            if ok(3):
                side[2] = dict(kind="Q1", g=gr(3), db=db(3), par=(s + 3) % 2)
                for k in range(4):
                    side[3 + k] = dict(kind="K", g=gr(3), db=db(3), piece=k, first=gr(3) == 0 and k == 0)
                    side[7 + k] = dict(kind="V", g=gr(3), db=db(3), quad=k, last=gr(3) == G - 1 and k == 3)
            ops = []
            for t in range(KT):
                n, t2 = divmod(t + 2, KT)
                if ok(n):
                    ops.append(dict(kind="S", g=gr(n), t=t2, par=(s + n) % 2))
                if ok(0):
                    ops.append(dict(kind="PV", g=gr(0), t=t))
                if ok(2):
                    for k, (j, q, p) in enumerate(pieces[3 * t:3 * t + 3]):
                        ops.append(dict(kind="M", g=gr(2), j=j, q=q, piece=p, par=(s + 2) % 2, first=t == 0 and k == 0))
                    if t == 11:
                        ops.append(dict(kind="MF"))
                if t in side:
                    ops.append(side[t])
            if ok(0):
                ops.append(dict(kind="N", g=gr(0)))
                if gr(0) == G - 1:
                    ops.append(dict(kind="O", db=db(0)))
            return ops

        total = B * G
        ahead = [o for s in (-3, -2, -1) for o in step(s, total)]
        body = [o for s in range(G) for o in step(s)]
        behind = [o for s in range(total - G, total) for o in step(s, total)]
        incs = {"S": dict(qk=1, ex=1), "PV": dict(pv=1), "M": dict(mm=1, mr=1), "MF": dict(nm=1),
                "K": dict(mj=1, mf=1, kc=1), "V": dict(mj=1, mf=1), "Q1": dict(mj=1, mf=1, qs=1, qb=1),
                "Q2": dict(mj=1, mf=1, qs=1, qb=1), "N": dict(mj=1, mf=1, ac=1, od=1), "O": dict(mj=1, mf=1)}
        plan = Plan(ahead, body, B - 1, behind, incs,
                    dict(qk=0, ex=2, pv=4, mm=0, mr=2, nm=0, mj=0, mf=1, kc=0, qs=1, qb=0, ac=0, od=1))
        assert plan.step["ex"] % 4 == 0 and plan.step["mr"] % 2 == 0
        at = plan.at

        def batch(op, i):
            return op["db"] if i is None else i + op["db"]

        last_use = {batch(op, i): at(op, "mf", i) for op, i in plan.all() if op.get("last")}
        block = c.enter_context(nc.Block())

        @block.sync
        def _(sp):
            for dst, src in ((wq, w["wq"]), (wk, w["wk"]), (wv, w["wv"]), (wo, w["wo"])):
                sp.dma_start(dst[:, :, :], src).then_inc(loaded, 16)
            sp.dma_start(bq[:, :], w["bq"]).then_inc(loaded, 16)
            sp.dma_start(bo[:, :], w["bo"]).then_inc(loaded, 16)
            for b in range(B):
                if b:
                    sp.wait_ge(mf, last_use[b - 1])
                sp.dma_start(ctxT[0:DC, :], g.ctxT_dram[:, b, :]).then_inc(ctx_loaded, 16)

        @block.tensor
        def _(pe):
            pe.sem_inc(pv, 4)
            pe.wait_ge(loaded, 6 * 16)
            pe.wait_ge(init, 1)

            def emit(op, i):
                k = op["kind"]
                if k == "S":
                    t, n = op["t"], rows(op["t"])
                    if t == 0:
                        pe.wait_ge(qb, at(op, "qb", i))
                    pe.wait_ge(ex, at(op, "ex", i, 2))
                    slot = ps_s[op["count"]["qk"] % 2 ^ 1]
                    for h in range(2):
                        r = nc.tensor.matmul(slot[0:n, h * 512:h * 512 + 512], k16[:, op["g"], t * P:t * P + n],
                                             q_exp[:, op["par"], 2 * h:2 * h + 2, :], start=True, stop=True)
                    r.then_inc(qk, 1)
                elif k == "PV":
                    t, n = op["t"], rows(op["t"])
                    m = op["count"]["pv"] - 5
                    pe.wait_ge(ex, at(op, "pv", i, 2))
                    for j in range(HG):
                        r = nc.tensor.matmul(ps_o[W * j:W * j + W, 0:S], v[0:n, op["g"], t, W * j:W * j + W],
                                             prob[0:n, m % 4, j * S:(j + 1) * S], start=t == 0, stop=t == KT - 1)
                    r.then_inc(pv, 1)
                elif k == "M":
                    if op["first"]:
                        pe.wait_ge(qb, at(op, "qb", i))
                    pe.wait_ge(mr, at(op, "mr", i, 2))
                    k0, n = PIECES[op["piece"]]
                    q = op["q"]
                    nc.tensor.matmul(ps_m[op["count"]["mm"] % 2 ^ 1][:, 0:n], q_max[:, op["par"], op["j"], q * P:(q + 1) * P],
                                     k16[:, op["g"], k0:k0 + n], start=True, stop=True).then_inc(mm, 1)
                elif k != "MF":
                    pe.wait_ge(mf, at(op, "mf", i, 1))
                    if k == "K":
                        if op["first"]:
                            b = batch(op, i)
                            pe.wait_ge(ctx_loaded, b * 16 + 16)
                        k0, n = PIECES[op["piece"]]
                        r = nc.tensor.matmul(ps_w[:, 0:n], wk[:, op["g"], :], ctxT[:, k0:k0 + n], start=True, stop=True)
                    elif k == "V":
                        for t in range(4 * op["quad"], min(4 * op["quad"] + 4, KT)):
                            n = rows(t)
                            r = nc.tensor.matmul(ps_w[0:n, (t % 4) * P:(t % 4) * P + P], ctxT[:, t * P:t * P + n],
                                                 wv[:, op["g"], :], start=True, stop=True)
                    elif k in ("Q1", "Q2"):
                        r = nc.tensor.matmul(ps_w[:, 0:S], wq[:, op["g"], :], g.xnT[:, batch(op, i), :],
                                             start=True, stop=k == "Q1")
                        if k == "Q2":
                            pe.wait_ge(nm, at(op, "nm", i))
                            for q in range(QT):
                                r = nc.tensor.matmul(ps_w[:, q * P:(q + 1) * P], negm[:, q, :, :].rearrange("p a b -> p (a b)"),
                                                     g.ident[:, :], start=False, stop=q == QT - 1)
                    elif k == "N":
                        pe.wait_ge(ac, at(op, "ac", i))
                        r = nc.tensor.matmul(ps_w[:, 0:S], g.sel[:, :], acc[:, :], start=True, stop=True)
                    elif k == "O":
                        pe.wait_ge(od, at(op, "od", i))
                        for q in range(QT):
                            if has_bo:
                                nc.tensor.matmul(ps_w[:, q * D:(q + 1) * D], g.ones[0:1, :], bo[:, :], start=True, stop=False)
                            for gg in range(G):
                                r = nc.tensor.matmul(ps_w[:, q * D:(q + 1) * D], on[:, gg, q * P:(q + 1) * P], wo[:, gg, :],
                                                     start=gg == 0 and not has_bo, stop=gg == G - 1)
                    r.then_inc(mj, 1)

            plan.run(pe, emit)

        @block.scalar
        def _(act):
            act.sem_inc(ex, 2)
            act.wait_ge(loaded, 6 * 16)
            nc.scalar.activation(bqs[:, :], bq[:, :], ACT.Copy, scale=scale).then_inc(qc, 1)
            act.wait_ge(qc, 1)

            def emit(op, i):
                k = op["kind"]
                if k == "S":
                    t, n = op["t"], rows(op["t"])
                    act.wait_ge(qk, at(op, "qk", i))
                    act.wait_ge(pv, at(op, "qk", i))
                    nc.scalar.activation(prob[0:n, (op["count"]["qk"] - 1) % 4, :], ps_s[op["count"]["qk"] % 2 ^ 1][0:n, :],
                                         ACT.Exp).then_inc(ex, 1)
                elif k == "K":
                    act.wait_ge(mj, at(op, "mj", i))
                    n = PIECES[op["piece"]][1]
                    nc.scalar.activation(kcast[:, 0:n], ps_w[:, 0:n], ACT.Copy).then_inc(kc, 1)
                elif k == "V":
                    act.wait_ge(mj, at(op, "mj", i))
                    if op["quad"] < 3:
                        dst = v[:, op["g"], 4 * op["quad"]:4 * op["quad"] + 4, :].rearrange("p a b -> p (a b)")
                        r = nc.scalar.activation(dst, ps_w[:, :], ACT.Copy)
                    else:
                        r = nc.scalar.activation(v[0:LAST, op["g"], KT - 1, :], ps_w[0:LAST, 0:P], ACT.Copy)
                    r.then_inc(mf, 1)
                elif k in ("Q1", "Q2"):
                    act.wait_ge(mj, at(op, "mj", i))
                    act.wait_ge(qs, at(op, "qs", i, 1))
                    nc.scalar.activation(qf[:, :], ps_w[:, 0:S], ACT.Identity, bias=bqs[:, op["g"]:op["g"] + 1],
                                         scale=g.cols[:, 1:2])
                    nc.scalar.activation(qcast[:, :], ps_w[:, 0:S], ACT.Identity, bias=bqs[:, op["g"]:op["g"] + 1],
                                         scale=g.cols[:, 1:2]).then_inc(mf, 1)
                elif k == "N":
                    act.wait_ge(pv, at(op, "pv", i))
                    act.wait_ge(od, at(op, "od", i, 1))
                    nc.scalar.activation(acc[:, :], ps_o[:, 0:S], ACT.Copy).then_inc(ac, 1)

            plan.run(act, emit)

        @block.vector
        def _(dve):
            nc.vector.memset(ctxT[DC:DC + 1, :], 1.0)
            nc.vector.memset(negm[:, :, :, :], 0.0).then_inc(init, 1)
            dve.sem_inc(mr, 2)
            dve.sem_inc(mf, 1)
            dve.sem_inc(qs, 1)
            dve.sem_inc(od, 1)
            dve.wait_ge(init, 1)

            def emit(op, i):
                k = op["kind"]
                if k == "M":
                    if op["first"] and (i is not None or op["count"]["nm"] > 0):
                        dve.wait_ge(nm, at(op, "nm", i))
                    dve.wait_ge(mm, at(op, "mm", i))
                    n = PIECES[op["piece"]][1]
                    nc.vector.reduce_max(mx[:, op["q"], op["j"], op["piece"]:op["piece"] + 1],
                                         ps_m[op["count"]["mm"] % 2 ^ 1][:, 0:n], AX.X).then_inc(mr, 1)
                elif k == "MF":
                    dve.wait_ge(mr, at(op, "mr", i))
                    nc.vector.tensor_reduce(negm[:, :, :, MROW], mx[:, :, :, :], AX.X, ALU.max, negate=True).then_inc(nm, 1)
                elif k == "K":
                    dve.wait_ge(kc, at(op, "kc", i))
                    k0, n = PIECES[op["piece"]]
                    nc.vector.scalar_tensor_tensor(k16[:, op["g"], k0:k0 + n], kcast[:, 0:n], g.cols[:, 2:3], ps_w[:, 0:n],
                                                   ALU.mult, ALU.add).then_inc(mf, 1)
                elif k in ("Q1", "Q2"):
                    dve.wait_ge(mf, at(op, "mf", i))
                    if op["count"]["qb"] > 1 or i is not None:
                        dve.wait_ge(qb, at(op, "qb", i, 1))
                    nc.vector.scalar_tensor_tensor(q16[:, :], qcast[:, :], g.cols[:, 3:4], qf[:, :],
                                                   ALU.mult, ALU.add).then_inc(qs, 1)
                elif k == "N":
                    dve.wait_ge(mj, at(op, "mj", i))
                    nc.vector.reciprocal(rec[:, :], ps_w[:, 0:S]).then_inc(mf, 1)
                    dve.wait_ge(mf, at(op, "mf", i))
                    nc.vector.tensor_tensor(on[:, op["g"], :], acc[:, :], rec[:, :], ALU.mult).then_inc(od, 1)
                elif k == "O":
                    dve.wait_ge(mj, at(op, "mj", i))
                    xb = g.xb[:, batch(op, i), :]
                    nc.vector.tensor_tensor(xb, ps_w[:, 0:S], xb, ALU.add).then_inc(mf, 1)

            plan.run(dve, emit)

        @block.gpsimd
        def _(pool):
            def emit(op, i):
                if op["kind"] in ("Q1", "Q2"):
                    pool.wait_ge(qs, at(op, "qs", i))
                    dst = (q_max if op["kind"] == "Q1" else q_exp)[:, op["par"], :, :]
                    nc.gpsimd.tensor_tensor(dst, q16[:, None, :].broadcast_to([P, HG, S]), g.blocks[:, :, None].broadcast_to([P, HG, S]), ALU.mult).then_inc(qb, 1)

            plan.run(pool, emit)


def wide_attention(nc, g, name, w, H, HG, DH, scale, KB, combined, biased):
    G = H // HG
    C1 = DC + 1
    N = HG * S
    OR = HG * DC
    PB = 8
    POOLED = 8
    total = B * G
    BODY = 2 * G if G > 1 else total
    with ExitStack() as c:
        sem = semaphores(nc, c, name)
        sb = lambda n, s, d=F32: c.enter_context(nc.sbuf_tensor(f"{name}_{n}", s, d))
        pb = lambda n, s: c.enter_context(nc.psum_tensor(f"{name}_{n}", s, F32))
        wq, wk = sb("wq", [DH, H, D]), sb("wk", [DH, H, DC])
        wv = sb("wv", [DH if combined else DC, H, DC if combined else D])
        wo = sb("wo", [DH, H, D]) if combined else None
        bq = sb("bq", [DH, 1]) if biased else None
        bo = sb("bo", [1, D])
        a_max, a_exp = sb("a_max", [P, H, P]), sb("a_exp", [P, H, C1])
        b_max, b_exp = sb("b_max", [1, P]), sb("b_exp", [1, C1])
        wvo = sb("wvo", [OR, G, D])
        stage = sb("stage", [P, LK])
        kcast = sb("kcast", [P, 401], F16)
        k_a, k_b = sb("k_a", [P, KB, LK], F16), sb("k_b", [C1, KB, LK], F16)
        v = sb("v", [P, KB, KT, DC])
        q_a, q_b, qcast = sb("q_a", [P, 4, N], F16), sb("q_b", [C1, 2, N], F16), sb("qcast", [C1, N], F16)
        mx, negm = sb("mx", [P, QT, HG, NP_]), sb("negm", [P, QT, HG, C1])
        prob = sb("prob", [P, PB, N])
        sum_p, sum_v = sb("sum_p", [P, 2, N]), sb("sum_v", [P, 2, N])
        acc, rec, on = sb("acc", [OR, S]), sb("rec", [OR, S]), sb("on", [OR, G, S])
        ps_s, ps_m = [pb(f"ps_s{i}", [P, 512]) for i in range(4)], [pb(f"ps_m{i}", [P, 512]) for i in range(2)]
        ps_o, ps_w = pb("ps_o", [P, 512]), pb("ps_w", [P, 512])
        loaded, stage_in, v_in = sem("loaded"), sem("stage_in"), [sem(f"v_in{k}") for k in range(KB)]
        qk, ex, pv, mm, mr, nm = sem("scores"), sem("exped"), sem("pv"), sem("maxmm"), sem("maxed"), sem("negmax")
        mj, mf, cc, cd, qc = sem("side"), sem("side_free"), sem("ctx_cast"), sem("ctx_split"), sem("q_cast")
        ac, od, init = sem("acc_out"), sem("normed"), sem("init")
        sp_, sv = sem("sum_pool"), sem("sum_vector")
        folded, fold_out = sem("folded"), sem("fold_out")

        def step(s, total=None):
            ok = lambda k: total is None or 0 <= s + k < total
            f = lambda k: dict(s=s + k, g=(s + k) % G, db=(s + k) // G, kb=(s + k) // G % KB, par=(s + k) % 2, par4=(s + k) % 4)
            pieces = [(j, q, k) for j in range(HG) for q in range(QT) for k in range(NP_)]
            side = {}
            if ok(1):
                side[1] = [dict(kind="Q2", **f(1))]
            if ok(3):
                side[3] = [dict(kind="Q1", **f(3))]
            ahead = 3 if G == 1 else G - 2
            if (s + ahead) % G == 0 and ok(ahead):
                for k in range(NP_):
                    side.setdefault(4 + k, []).append(dict(kind="C", piece=k, **f(ahead)))
            ops = []
            for t in range(KT):
                n, t2 = divmod(t + 3, KT)
                if ok(n):
                    ops.append(dict(kind="S", t=t2, **f(n)))
                if ok(0):
                    ops.append(dict(kind="PV", t=t, **f(0)))
                if ok(2):
                    for k, (j, q, p) in enumerate(pieces[2 * t:2 * t + 2]):
                        ops.append(dict(kind="M", j=j, q=q, piece=p, first=t == 0 and k == 0, **f(2)))
                    if t == 9:
                        ops.append(dict(kind="MF"))
                ops += side.get(t, [])
            if ok(0):
                ops.append(dict(kind="N", **f(0)))
                if (s + 1) % G == 0:
                    ops.append(dict(kind="O", **f(0)))
            return ops

        first = [dict(kind="C", piece=k, s=0, g=0, db=0, kb=0) for k in range(NP_)]
        if G == 1:
            first = []
        ahead = first + [o for s in (-3, -2, -1) for o in step(s, total) if not (G > 1 and o["kind"] == "C")]
        times = total // BODY - 1
        body = [o for s in range(BODY) for o in step(s)] if times else []
        behind = [o for s in range(total - BODY, total) for o in step(s, total)]
        incs = {"S": dict(qk=1, ex=1), "PV": dict(pv=1), "M": dict(mm=1, mr=1), "MF": dict(nm=1), "C": dict(cc=1, cd=1),
                "Q1": dict(mj=1, mf=1), "Q2": dict(mj=1, mf=1, qc=1), "N": dict(mj=1, mf=1, ac=1, od=1), "O": dict(mj=1, mf=1)}
        plan = Plan(ahead, body, times, behind, incs,
                    dict(qk=0, ex=4, pv=PB, mm=0, mr=2, nm=0, mj=0, mf=1, cc=0, cd=1, qc=0, ac=0, od=1))
        at = plan.at
        if times:
            assert plan.step["ex"] % PB == 0 and plan.step["mr"] % 2 == 0

        def step_of(op, i):
            return op["s"] if i is None else i * BODY + op["s"]

        def batch(op, i):
            return op["db"] if i is None else i * (BODY // G) + op["db"]

        split = {batch(op, i): at(op, "cd", i) for op, i in plan.all() if op["kind"] == "C"}
        attended = {batch(op, i): at(op, "pv", i) for op, i in plan.all() if op["kind"] == "PV" and op["t"] == KT - 1}
        block = c.enter_context(nc.Block())

        @block.sync
        def _(sp):
            loads = [(wq, w["wq"]), (wk, w["wk"]), (wv, w["wv"])] + ([(wo, w["wo"])] if combined else [])
            for dst, src in loads:
                sp.dma_start(dst[:, :, :], src).then_inc(loaded, 16)
            for dst, src in [(bo, w["bo"])] + ([(bq, w["bq"])] if biased else []):
                sp.dma_start(dst[:, :], src).then_inc(loaded, 16)
            for b in range(B):
                if b:
                    sp.wait_ge(cd, split[b - 1])
                sp.dma_start(stage[0:DC, :], g.ctxT_dram[:, b, :]).then_inc(stage_in, 16)
                sp.dma_start(stage[DC:P, :], g.ctxT_dram[:, b, :]).then_inc(stage_in, 16)
                if b >= KB:
                    sp.wait_ge(pv, attended[b - KB])
                sp.dma_start(v[:, b % KB, :, :], g.ctxV_dram[:, b, :, :]).then_inc(v_in[b % KB], 16)

        n_loads = 16 * (4 + combined + biased)

        @block.tensor
        def _(pe):
            pe.sem_inc(pv, PB)
            pe.wait_ge(loaded, n_loads)
            pe.wait_ge(init, 1)
            for h in range(H):
                if h >= 4:
                    pe.wait_ge(fold_out, h - 3)
                bank = ps_s[h % 4]
                r = nc.tensor.matmul(bank[:, 0:DC], wq[:, h, :], wk[:, h, :], start=True, stop=True)
                if combined:
                    r = nc.tensor.matmul(bank[0:DC, 256:256 + D], wv[:, h, :], wo[:, h, :], start=True, stop=True)
                r.then_inc(folded, 1)
            if biased:
                nc.tensor.matmul(ps_m[0][0:1, 0:DC], bq[:, :], wk[:, 0, :], start=True, stop=True).then_inc(folded, 1)
            pe.wait_ge(fold_out, H + 1)

            def emit(op, i):
                k = op["kind"]
                if k == "S":
                    t, n = op["t"], rows(op["t"])
                    if t == 0:
                        pe.wait_ge(mf, at(op, "mf", i))
                    pe.wait_ge(ex, at(op, "ex", i, 4))
                    bank = ps_s[(op["count"]["qk"] - 1) % 4]
                    nc.tensor.matmul(bank[0:n, 0:N], k_a[:, op["kb"], t * P:t * P + n], q_a[:, op["par4"], :], start=True, stop=False)
                    nc.tensor.matmul(bank[0:n, 0:N], k_b[:, op["kb"], t * P:t * P + n], q_b[:, op["par"], :],
                                     start=False, stop=True).then_inc(qk, 1)
                elif k == "PV":
                    t, n = op["t"], rows(op["t"])
                    m = op["count"]["pv"] - PB - 1
                    if t == 0 and op["g"] == 0:
                        pe.wait_ge(v_in[op["kb"]], op["db"] // KB * 16 + 16 if i is None else i * 16 + (op["db"] // KB * 16 + 16))
                    pe.wait_ge(ex, at(op, "pv", i, PB - 4))
                    for j in range(HG):
                        r = nc.tensor.matmul(ps_o[DC * j:DC * j + DC, 0:S], v[0:n, op["kb"], t, :],
                                             prob[0:n, m % PB, j * S:(j + 1) * S], start=t == 0, stop=t == KT - 1)
                    r.then_inc(pv, 1)
                elif k == "M":
                    if op["first"]:
                        pe.wait_ge(mf, at(op, "mf", i))
                        pe.wait_ge(cd, at(op, "cd", i))
                    pe.wait_ge(mr, at(op, "mr", i, 2))
                    k0, n = PIECES[op["piece"]]
                    q0 = op["j"] * S + op["q"] * P
                    nc.tensor.matmul(ps_m[(op["count"]["mm"] - 1) % 2][:, 0:n], q_a[:, op["par4"], q0:q0 + P],
                                     k_a[:, op["kb"], k0:k0 + n], start=True, stop=True).then_inc(mm, 1)
                elif k in ("Q1", "Q2", "N", "O"):
                    pe.wait_ge(mf, at(op, "mf", i, 1))
                    if k in ("Q1", "Q2"):
                        a_w, b_w, m = (a_max, b_max, P) if k == "Q1" else (a_exp, b_exp, C1)
                        if k == "Q2":
                            pe.wait_ge(nm, at(op, "nm", i))
                        for j in range(HG):
                            if biased:
                                nc.tensor.matmul(ps_w[0:m, j * S:(j + 1) * S], b_w[:, :], g.ones2[0:1, :], start=True, stop=False)
                            r = nc.tensor.matmul(ps_w[0:m, j * S:(j + 1) * S], a_w[:, op["g"] * HG + j, :], g.xnT[:, batch(op, i), :],
                                                 start=not biased, stop=k == "Q1")
                            if k == "Q2":
                                for q in range(QT):
                                    r = nc.tensor.matmul(ps_w[0:m, j * S + q * P:j * S + (q + 1) * P], negm[:, q, j, :],
                                                         g.ident[:, :], start=False, stop=q == QT - 1)
                    elif k == "N":
                        pe.wait_ge(ac, at(op, "ac", i))
                        pe.wait_ge(sp_, step_of(op, i) * POOLED + 2 * POOLED)
                        pe.wait_ge(sv, step_of(op, i) * (KT - POOLED) + 2 * (KT - POOLED))
                        for j in range(HG):
                            for sums, start in ((sum_p, True), (sum_v, False)):
                                r = nc.tensor.matmul(ps_w[DC * j:DC * j + DC, 0:S], g.ones[:, 0:DC], sums[:, op["par"], j * S:(j + 1) * S],
                                                     start=start, stop=not start)
                    elif k == "O":
                        pe.wait_ge(od, at(op, "od", i))
                        for q in range(QT):
                            nc.tensor.matmul(ps_w[:, q * D:(q + 1) * D], g.ones[0:1, :], bo[:, :], start=True, stop=False)
                            for gg in range(G):
                                r = nc.tensor.matmul(ps_w[:, q * D:(q + 1) * D], on[:, gg, q * P:(q + 1) * P], wvo[:, gg, :],
                                                     start=False, stop=gg == G - 1)
                    r.then_inc(mj, 1)

            plan.run(pe, emit)

        @block.scalar
        def _(act):
            act.sem_inc(ex, 4)
            act.wait_ge(init, 1)
            for h in range(H):
                act.wait_ge(folded, h + 1)
                bank = ps_s[h % 4]
                for k in range(2):
                    nc.scalar.activation(a_max[:, h, k * DC:(k + 1) * DC], bank[:, 0:DC], ACT.Copy, scale=scale)
                if combined:
                    nc.scalar.activation(wvo[h % HG * DC:h % HG * DC + DC, h // HG, :], bank[0:DC, 256:256 + D], ACT.Copy)
                nc.scalar.activation(a_exp[:, h, 0:DC], bank[:, 0:DC], ACT.Copy, scale=scale).then_inc(fold_out, 1)
            if not combined:
                act.wait_ge(loaded, n_loads)
                nc.scalar.activation(wvo[:, 0, :], wv[:, 0, :], ACT.Copy)
            if biased:
                act.wait_ge(folded, H + 1)
                for k in range(2):
                    nc.scalar.activation(b_max[:, k * DC:(k + 1) * DC], ps_m[0][0:1, 0:DC], ACT.Copy, scale=scale)
                r = nc.scalar.activation(b_exp[:, 0:DC], ps_m[0][0:1, 0:DC], ACT.Copy, scale=scale)
            else:
                r = nc.scalar.activation(b_exp[:, 0:DC], bo[:, 0:DC], ACT.Copy, scale=0.0)
            r.then_inc(fold_out, 1)

            def emit(op, i):
                k = op["kind"]
                if k == "S":
                    t, n = op["t"], rows(op["t"])
                    act.wait_ge(qk, at(op, "qk", i))
                    act.wait_ge(pv, at(op, "qk", i))
                    st = step_of(op, i)
                    if t >= POOLED:
                        act.wait_ge(sp_, st * POOLED + t + 1)
                    elif t < 2 * POOLED - KT:
                        act.wait_ge(sp_, st * POOLED + (t + KT - POOLED + 1))
                    else:
                        act.wait_ge(sv, st * (KT - POOLED) + (t + KT - 2 * POOLED + 1))
                    m = op["count"]["qk"] - 1
                    nc.scalar.activation(prob[0:n, m % PB, :], ps_s[m % 4][0:n, 0:N], ACT.Exp).then_inc(ex, 1)
                elif k == "C":
                    act.wait_ge(stage_in, batch(op, i) * 32 + 32)
                    act.wait_ge(cd, at(op, "cd", i, 1))
                    k0, n = PIECES[op["piece"]]
                    nc.scalar.activation(k_b[0:DC, op["kb"], k0:k0 + n], stage[0:DC, k0:k0 + n], ACT.Copy)
                    nc.scalar.activation(kcast[:, 0:n], stage[:, k0:k0 + n], ACT.Copy).then_inc(cc, 1)
                elif k == "Q1":
                    act.wait_ge(mj, at(op, "mj", i))
                    nc.scalar.activation(q_a[:, op["par4"], :], ps_w[:, 0:N], ACT.Copy).then_inc(mf, 1)
                elif k == "Q2":
                    act.wait_ge(mj, at(op, "mj", i))
                    nc.scalar.activation(qcast[:, :], ps_w[0:C1, 0:N], ACT.Copy).then_inc(qc, 1)
                elif k == "N":
                    act.wait_ge(pv, at(op, "pv", i))
                    act.wait_ge(od, at(op, "od", i, 1))
                    nc.scalar.activation(acc[:, :], ps_o[0:OR, 0:S], ACT.Copy).then_inc(ac, 1)

            plan.run(act, emit)

        @block.vector
        def _(dve):
            nc.vector.memset(k_b[DC:C1, :, :], 1.0)
            nc.vector.memset(a_exp[:, :, DC:C1], 0.0)
            nc.vector.memset(b_exp[:, DC:C1], 0.0)
            nc.vector.memset(negm[:, :, :, :], 0.0).then_inc(init, 1)
            dve.sem_inc(mr, 2)
            dve.sem_inc(mf, 1)
            dve.sem_inc(cd, 1)
            dve.sem_inc(od, 1)
            dve.sem_inc(sv, KT - POOLED)
            dve.wait_ge(init, 1)

            def emit(op, i):
                k = op["kind"]
                if k == "PV" and op["t"] > POOLED:
                    t, n = op["t"], rows(op["t"])
                    m = op["count"]["pv"] - PB - 1
                    dve.wait_ge(ex, at(op, "pv", i, PB - 4))
                    dst = sum_v[0:n, op["par"], :]
                    if t == POOLED + 1:
                        nc.vector.tensor_tensor(dst, prob[:, (m - 1) % PB, :], prob[:, m % PB, :], ALU.add).then_inc(sv, 2)
                    else:
                        dve.wait_ge(sv, step_of(op, i) * (KT - POOLED) + (t - POOLED + KT - POOLED))
                        nc.vector.tensor_tensor(dst, dst, prob[0:n, m % PB, :], ALU.add).then_inc(sv, 1)
                elif k == "M":
                    if op["first"] and (i is not None or op["count"]["nm"] > 0):
                        dve.wait_ge(nm, at(op, "nm", i))
                    dve.wait_ge(mm, at(op, "mm", i))
                    n = PIECES[op["piece"]][1]
                    nc.vector.reduce_max(mx[:, op["q"], op["j"], op["piece"]:op["piece"] + 1],
                                         ps_m[(op["count"]["mm"] - 1) % 2][:, 0:n], AX.X).then_inc(mr, 1)
                elif k == "MF":
                    dve.wait_ge(mr, at(op, "mr", i))
                    nc.vector.tensor_reduce(negm[:, :, :, DC], mx[:, :, :, :], AX.X, ALU.max, negate=True).then_inc(nm, 1)
                elif k == "C":
                    dve.wait_ge(cc, at(op, "cc", i))
                    k0, n = PIECES[op["piece"]]
                    nc.vector.scalar_tensor_tensor(k_a[:, op["kb"], k0:k0 + n], kcast[:, 0:n], g.cols[:, 4:5], stage[:, k0:k0 + n],
                                                   ALU.mult, ALU.add).then_inc(cd, 1)
                elif k == "Q2":
                    dve.wait_ge(qc, at(op, "qc", i))
                    nc.vector.scalar_tensor_tensor(q_b[:, op["par"], :], qcast[:, :], g.cols[0:C1, 5:6], ps_w[0:C1, 0:N],
                                                   ALU.mult, ALU.add).then_inc(mf, 1)
                elif k == "N":
                    dve.wait_ge(mj, at(op, "mj", i))
                    nc.vector.reciprocal(rec[:, :], ps_w[0:OR, 0:S]).then_inc(mf, 1)
                    dve.wait_ge(mf, at(op, "mf", i))
                    nc.vector.tensor_tensor(on[:, op["g"], :], acc[:, :], rec[:, :], ALU.mult).then_inc(od, 1)
                elif k == "O":
                    dve.wait_ge(mj, at(op, "mj", i))
                    xb = g.xb[:, batch(op, i), :]
                    nc.vector.tensor_tensor(xb, ps_w[:, 0:S], xb, ALU.add).then_inc(mf, 1)

            plan.run(dve, emit)

        @block.gpsimd
        def _(pool):
            pool.sem_inc(sp_, POOLED)

            def emit(op, i):
                if op["kind"] == "PV" and 0 < op["t"] < POOLED:
                    m = op["count"]["pv"] - PB - 1
                    pool.wait_ge(ex, at(op, "pv", i, PB - 4))
                    dst = sum_p[:, op["par"], :]
                    if op["t"] == 1:
                        nc.gpsimd.tensor_tensor(dst, prob[:, (m - 1) % PB, :], prob[:, m % PB, :], ALU.add).then_inc(sp_, 2)
                    else:
                        pool.wait_ge(sp_, step_of(op, i) * POOLED + (op["t"] + POOLED))
                        nc.gpsimd.tensor_tensor(dst, dst, prob[:, m % PB, :], ALU.add).then_inc(sp_, 1)

            plan.run(pool, emit)


class Flow:

    def __init__(self, n, nbuf, order):
        self.n, self.nbuf, self.order = n, nbuf, order

    def run(self, engine, emit):
        n, nb = self.n, self.nbuf
        for s in range(nb):
            for kind, off in self.order:
                if 0 <= s - off < n:
                    emit(kind, s - off, (s - off) % nb)
        if n > nb:
            with engine.Fori(0, n // nb - 1) as i:
                for k in range(nb):
                    for kind, off in self.order:
                        emit(kind, i * nb + (nb + k - off), (k - off) % nb)
        for s in range(n, n + nb):
            for kind, off in self.order:
                if s - off < n:
                    emit(kind, s - off, (s - off) % nb)

    def done(self, engine, sem, t):
        engine.wait_ge(sem, t + (1 + self.nbuf))

    def free(self, engine, sem, t):
        engine.wait_ge(sem, t + 1)

    def free1(self, engine, sem, t):
        engine.wait_ge(sem, t + self.nbuf)


def moments(nc, g, name, rms=False):
    with ExitStack() as c:
        sem = semaphores(nc, c, name)
        stats = c.enter_context(nc.sbuf_tensor(f"{name}_stats", [P, NT, 6], F32))
        sq = c.enter_context(nc.sbuf_tensor(f"{name}_sq", [P, NT, 2], F32))
        stats_done, moments_done, std_done, rstd_done = sem("stats_done"), sem("moments_done"), sem("std_done"), sem("rstd_done")
        with nc.Block() as block:
            @block.vector
            def _(dve):
                for t in range(NT):
                    nc.vector.bn_stats(stats[:, t, :], g.x[:, t, :]).then_inc(stats_done, 1)
                for t in range(NT):
                    dve.wait_ge(stats_done, t + 1)
                    nc.vector.bn_aggr(g.mv[:, t, :], stats[:, t, :]).then_inc(moments_done, 1)
                dve.wait_ge(std_done, 1)
                nc.vector.reciprocal(g.rstd[:, :], g.std[:, :]).then_inc(rstd_done, 1)
                if rms:
                    dve.wait_ge(rstd_done, 1)
                    nc.vector.tensor_tensor(sq[:, :, 0], g.rstd[:, :], g.rstd[:, :], ALU.mult).then_inc(rstd_done, 1)
                    dve.wait_ge(rstd_done, 2)
                    nc.vector.tensor_tensor(sq[:, :, 1], sq[:, :, 0], g.mv[:, :, 1], ALU.mult).then_inc(rstd_done, 1)
                    dve.wait_ge(std_done, 2)
                    nc.vector.reciprocal(g.rrms[:, :], g.rms[:, :]).then_inc(rstd_done, 1)

            @block.scalar
            def _(act):
                act.wait_ge(moments_done, NT)
                nc.scalar.activation(g.std[:, :], g.mv[:, :, 1], ACT.Sqrt, bias=g.cols[:, 0:1]).then_inc(std_done, 1)
                if rms:
                    act.wait_ge(rstd_done, 3)
                    nc.scalar.activation(g.rms[:, :], sq[:, :, 1], ACT.Sqrt, bias=g.cols[:, 6:7]).then_inc(std_done, 1)


def head_mix_ffn(nc, g, name, w):
    H, DH, E = 16, 8, 8
    C3 = 3 * D
    with ExitStack() as c:
        sem = semaphores(nc, c, name)
        sb = lambda n, s, d=F32: c.enter_context(nc.sbuf_tensor(f"{name}_{n}", s, d))
        pb = lambda n, s, d=F32: c.enter_context(nc.psum_tensor(f"{name}_{n}", s, d))
        z2 = sb("z2", [P, NT, D])
        ms2, rms2, rr2 = sb("ms2", [P, NT]), sb("rms2", [P, NT]), sb("rr2", [P, NT])
        with ExitStack() as c1:
            sb1 = lambda n, s, d=F32: c1.enter_context(nc.sbuf_tensor(f"{name}_{n}", s, d))
            pb1 = lambda n, s, d=F32: c1.enter_context(nc.psum_tensor(f"{name}_{n}", s, d))
            wqkv, wdT, wup, wo = sb1("wqkv", [P, C3]), sb1("wdT", [DC, D]), sb1("wup", [DC, 2 * D]), sb1("wo", [P, D])
            bdown, bdb = sb1("bdown", [DC, 1]), sb1("bdb", [DC, P])
            brow, bo, bias = sb1("brow", [1, C3]), sb1("bo", [1, D]), sb1("bias", [P, C3])
            gamma = sb1("gamma", [P, 1])
            NB = 4
            z, zT, qkv = sb1("z", [P, NB, D]), sb1("zT", [P, NB, D]), sb1("qkv", [P, NB, C3])
            prod, att, eatt = sb1("prod", [P, NB, H * H * DH]), sb1("att", [P, NB, H * H]), sb1("eatt", [P, NB, H * H])
            top, esum, einv = sb1("top", [P, H]), sb1("esum", [P, H]), sb1("einv", [P, H])
            prod2, o_raw = sb1("prod2", [P, H * DH * H]), sb1("o_raw", [P, D])
            o, oT, zz, sqr = sb1("o", [P, NB, D]), sb1("oT", [P, NB, D]), sb1("zz", [P, D]), sb1("sqr", [P, D])
            ps_t, ps_q = [pb1(f"ps_t{k}", [P, 512]) for k in range(2)], [pb1(f"ps_q{k}", [P, 512]) for k in range(2)]
            ps_u, ps_y = [pb1(f"ps_u{k}", [P, 512]) for k in range(2)], [pb1(f"ps_y{k}", [P, 512]) for k in range(2)]
            loaded, folded, ready, biased = sem("loaded"), sem("folded"), sem("ready"), sem("biased")
            names = ["z", "turn", "zT", "qkvmm", "qkv", "prod", "att", "exp", "mix", "oturn", "oT", "omm", "z2", "sq"]
            s = {n: sem("s_" + n) for n in names}
            r_step, v_step, y_step = sem("r_step"), sem("v_step"), sem("y_step")
            order = [("omm", 4), ("z2", 4), ("sq", 4), ("mix", 3), ("oturn", 3), ("oT", 3), ("att", 2), ("exp", 2),
                     ("qkvmm", 1), ("qkv", 1), ("prod", 1), ("z", 0), ("turn", 0), ("zT", 0)]
            flow = Flow(NT, NB, order)
            done, free = flow.done, flow.free
            block = c1.enter_context(nc.Block())

            @block.sync
            def _(sp):
                for dst, src in ((wqkv[:, 0:D], w["wq"]), (wdT[:, :], w["wdT"]), (wup[:, :], w["wup"]), (wo[:, :], w["wo"]),
                                 (bdown[:, :], w["bdown"]), (brow[:, :], w["brow"]), (bo[:, :], w["bo"]), (gamma[:, :], w["gamma1"])):
                    sp.dma_start(dst, src).then_inc(loaded, 16)

            @block.tensor
            def _(pe):
                for n in ("turn", "qkvmm", "oturn", "omm"):
                    pe.sem_inc(s[n], NB)
                pe.wait_ge(loaded, 8 * 16)
                pe.wait_ge(ready, 1)
                nc.tensor.matmul(ps_q[0][:, 0:2 * D], wdT[:, :], wup[:, :], start=True, stop=True).then_inc(folded, 1)
                nc.tensor.matmul(ps_q[1][:, 0:C3], g.ones[0:1, :], brow[:, :], start=True, stop=False)
                nc.tensor.matmul(ps_q[1][:, D:C3], bdb[:, :], wup[:, :], start=False, stop=True).then_inc(folded, 1)
                pe.wait_ge(biased, 2)

                def emit(kind, t, b):
                    if kind == "turn":
                        done(pe, s["z"], t)
                        free(pe, s["zT"], t + 2)
                        nc.tensor.transpose(ps_t[b % 2][:, 0:P], z[:, b, :], g.ident[:, :]).then_inc(s[kind], 1)
                    elif kind == "qkvmm":
                        done(pe, s["zT"], t)
                        free(pe, s["qkv"], t + 2)
                        nc.tensor.matmul(ps_q[b % 2][:, 0:C3], zT[:, b, :], wqkv[:, :], start=True, stop=True).then_inc(s[kind], 1)
                    elif kind == "oturn":
                        done(pe, s["mix"], t)
                        free(pe, s["oT"], t + 2)
                        nc.tensor.transpose(ps_u[b % 2][:, 0:P], o[:, b, :], g.ident[:, :]).then_inc(s[kind], 1)
                    elif kind == "omm":
                        done(pe, s["oT"], t)
                        free(pe, s["z2"], t + 2)
                        nc.tensor.matmul(ps_y[b % 2][:, 0:D], g.ones[0:1, :], bo[:, :], start=True, stop=False)
                        nc.tensor.matmul(ps_y[b % 2][:, 0:D], oT[:, b, :], wo[:, :], start=False, stop=True).then_inc(s[kind], 1)

                flow.run(pe, emit)

            @block.scalar
            def _(act):
                for n in ("zT", "exp", "oT", "sq"):
                    act.sem_inc(s[n], NB)

                def emit(kind, t, b):
                    if kind == "zT":
                        done(act, s["turn"], t)
                        free(act, s["qkvmm"], t)
                        nc.scalar.activation(zT[:, b, :], ps_t[b % 2][:, 0:P], ACT.Copy).then_inc(s[kind], 1)
                    elif kind == "exp":
                        done(act, s["att"], t)
                        free(act, s["mix"], t)
                        nc.scalar.activation(eatt[:, b, :], att[:, b, :], ACT.Exp, scale=DH ** -0.5).then_inc(s[kind], 1)
                    elif kind == "oT":
                        done(act, s["oturn"], t)
                        free(act, s["omm"], t)
                        nc.scalar.activation(oT[:, b, :], ps_u[b % 2][:, 0:P], ACT.Copy).then_inc(s[kind], 1)
                    elif kind == "sq":
                        done(act, s["z2"], t)
                        flow.free1(act, s["sq"], t)
                        nc.scalar.activation(sqr[:, :], z2[:, t, :], ACT.Square, accum_out=ms2[:, bass.ds(t, 1)]).then_inc(s[kind], 1)

                flow.run(act, emit)

            @block.gpsimd
            def _(pool):
                pool.sem_inc(s["prod"], NB)

                def emit(kind, t, b):
                    if kind == "prod":
                        done(pool, s["qkv"], t)
                        free(pool, s["att"], t)
                        q = qkv[:, b, 0:D].rearrange("p (h d) -> p h d", d=DH)[:, :, None, :].broadcast_to([P, H, H, DH])
                        k = qkv[:, b, D:C3].rearrange("p (h d) -> p h d", d=2 * DH)[:, None, :, 0:DH].broadcast_to([P, H, H, DH])
                        nc.gpsimd.tensor_tensor(prod[:, b, :].rearrange("p (h k d) -> p h k d", h=H, k=H), q, k, ALU.mult).then_inc(s[kind], 1)

                flow.run(pool, emit)

            @block.vector
            def _(dve):
                for n in ("z", "qkv", "att", "mix", "z2"):
                    dve.sem_inc(s[n], NB)
                dve.wait_ge(loaded, 8 * 16)
                nc.vector.tensor_copy(bdb[:, :], bdown[:, 0:1].broadcast_to([DC, P])).then_inc(ready, 1)
                dve.wait_ge(folded, 2)
                nc.vector.tensor_scalar(wqkv[:, D:C3], ps_q[0][:, 0:2 * D], gamma[:, 0:1], None, ALU.mult)
                nc.vector.tensor_scalar(wqkv[:, 0:D], wqkv[:, 0:D], gamma[:, 0:1], None, ALU.mult).then_inc(biased, 1)
                nc.vector.tensor_copy(bias[:, :], ps_q[1][:, 0:C3]).then_inc(biased, 1)
                dve.wait_ge(biased, 2)

                def emit(kind, t, b):
                    if kind == "z":
                        free(dve, s["turn"], t)
                        nc.vector.tensor_scalar(z[:, b, :], g.x[:, t, :], g.mv[:, t, 0:1], g.rstd[:, bass.ds(t, 1)],
                                                ALU.subtract, ALU.mult).then_inc(s[kind], 1)
                    elif kind == "qkv":
                        done(dve, s["qkvmm"], t)
                        free(dve, s["mix"], t)
                        nc.vector.scalar_tensor_tensor(qkv[:, b, :], ps_q[b % 2][:, 0:C3], g.rrms[:, bass.ds(t, 1)], bias[:, :],
                                                       ALU.mult, ALU.add).then_inc(s[kind], 1)
                    elif kind == "att":
                        L = 3
                        done(dve, s["prod"], t)
                        free(dve, s["exp"], t)
                        a = att[:, b, :].rearrange("p (h k) -> p h k", h=H)
                        nc.vector.tensor_reduce(a, prod[:, b, :].rearrange("p (h k d) -> p h k d", h=H, k=H), AX.X, ALU.add).then_inc(r_step, 1)
                        dve.wait_ge(r_step, t * 2 + 1)
                        nc.vector.tensor_reduce(top[:, :], a, AX.X, ALU.max).then_inc(r_step, 1)
                        dve.wait_ge(r_step, t * 2 + 2)
                        nc.vector.tensor_tensor(a, a, top[:, :, None].broadcast_to([P, H, H]), ALU.subtract).then_inc(s[kind], 1)
                    elif kind == "mix":
                        done(dve, s["exp"], t)
                        free(dve, s["oturn"], t)
                        flow.free1(dve, s["mix"], t)
                        e = eatt[:, b, :].rearrange("p (h k) -> p h k", h=H)
                        v = qkv[:, b, D:C3].rearrange("p (k d) -> p d k", d=2 * DH)[:, DH:2 * DH, :]
                        pr = prod2[:, :].rearrange("p (h d k) -> p h d k", h=H, d=DH)
                        nc.vector.tensor_tensor(pr, e[:, :, None, :].broadcast_to([P, H, DH, H]),
                                                v[:, None, :, :].broadcast_to([P, H, DH, H]), ALU.mult).then_inc(v_step, 1)
                        nc.vector.tensor_reduce(esum[:, :], e, AX.X, ALU.add).then_inc(v_step, 1)
                        dve.wait_ge(v_step, t * 4 + 2)
                        nc.vector.reciprocal(einv[:, :], esum[:, :]).then_inc(v_step, 1)
                        nc.vector.tensor_reduce(o_raw[:, :].rearrange("p (h d) -> p h d", h=H), pr, AX.X, ALU.add).then_inc(v_step, 1)
                        dve.wait_ge(v_step, t * 4 + 4)
                        nc.vector.tensor_tensor(o[:, b, :].rearrange("p (h d) -> p h d", h=H), o_raw[:, :].rearrange("p (h d) -> p h d", h=H),
                                                einv[:, :, None].broadcast_to([P, H, DH]), ALU.mult).then_inc(s[kind], 1)
                    elif kind == "z2":
                        done(dve, s["omm"], t)
                        flow.free1(dve, s["z2"], t)
                        nc.vector.tensor_scalar(zz[:, :], g.x[:, t, :], g.mv[:, t, 0:1], g.rstd[:, bass.ds(t, 1)],
                                                ALU.subtract, ALU.mult).then_inc(y_step, 1)
                        dve.wait_ge(y_step, t + 1)
                        nc.vector.tensor_tensor(z2[:, t, :], ps_y[b % 2][:, 0:D], zz[:, :], ALU.add).then_inc(s[kind], 1)

                flow.run(dve, emit)

        with ExitStack() as c1:
            sb1 = lambda n, s, d=F32: c1.enter_context(nc.sbuf_tensor(f"{name}b_{n}", s, d))
            pb1 = lambda n, s, d=F32: c1.enter_context(nc.psum_tensor(f"{name}b_{n}", s, d))
            NB = 2
            wg, we, bg, gamma = sb1("wg", [P, E]), sb1("we", [P, E * D]), sb1("bg", [P, E]), sb1("gamma", [P, 1])
            zc, zT = sb1("zc", [P, NB, D]), sb1("zT", [P, NB, D])
            lg, eg = sb1("lg", [P, NB, E]), sb1("eg", [P, NB, E])
            lraw, ltop, esum, einv = sb1("lraw", [P, E]), sb1("ltop", [P, 1]), sb1("esum", [P, 1]), sb1("einv", [P, 1])
            gate, mixed, comb, xz = sb1("gate", [P, E]), sb1("mixed", [P, E, D]), sb1("comb", [P, D]), sb1("xz", [P, D])
            ps_t, ps_g = pb1("ps_t", [P, 512]), pb1("ps_g", [P, 512])
            ps_e = [pb1(f"ps_e{k}", [P, 1024]) for k in range(2)]
            loaded, rms_in, rms_out, scaled = sem("b_loaded"), sem("b_rms_in"), sem("b_rms_out"), sem("b_scaled")
            s = {n: sem("b_" + n) for n in ("copy", "turn", "zT", "mm", "logit", "exp", "mix")}
            l_step, m_step = sem("b_l_step"), sem("b_m_step")
            order = [("mix", 2), ("mm", 1), ("logit", 1), ("exp", 1), ("copy", 0), ("turn", 0), ("zT", 0)]
            flow = Flow(NT, NB, order)
            done, free, free1 = flow.done, flow.free, flow.free1
            block = c1.enter_context(nc.Block())

            @block.sync
            def _(sp):
                for dst, src in ((wg, w["wg"]), (we, w["we"]), (bg, w["bg"]), (gamma, w["gamma2"])):
                    sp.dma_start(dst[:, :], src).then_inc(loaded, 16)

            @block.tensor
            def _(pe):
                for n in ("turn", "mm"):
                    pe.sem_inc(s[n], NB)
                pe.wait_ge(scaled, 1)

                def emit(kind, t, b):
                    if kind == "turn":
                        done(pe, s["copy"], t)
                        free1(pe, s["zT"], t)
                        nc.tensor.transpose(ps_t[:, 0:P], zc[:, b, :], g.ident[:, :]).then_inc(s[kind], 1)
                    elif kind == "mm":
                        done(pe, s["zT"], t)
                        free1(pe, s["logit"], t)
                        free(pe, s["mix"], t)
                        nc.tensor.matmul(ps_g[:, 0:E], zT[:, b, :], wg[:, :], start=True, stop=True)
                        for k in range(2):
                            r = nc.tensor.matmul(ps_e[b][:, k * 512:(k + 1) * 512], zT[:, b, :], we[:, k * 512:(k + 1) * 512], start=True, stop=True)
                        r.then_inc(s[kind], 1)

                flow.run(pe, emit)

            @block.scalar
            def _(act):
                for n in ("copy", "zT", "exp"):
                    act.sem_inc(s[n], NB)
                nc.scalar.activation(rms2[:, :], ms2[:, :], ACT.Sqrt, bias=g.cols[:, 6:7], scale=1.0 / D).then_inc(rms_in, 1)

                def emit(kind, t, b):
                    if kind == "copy":
                        free(act, s["turn"], t)
                        nc.scalar.activation(zc[:, b, :], z2[:, t, :], ACT.Copy).then_inc(s[kind], 1)
                    elif kind == "zT":
                        done(act, s["turn"], t)
                        free(act, s["mm"], t)
                        nc.scalar.activation(zT[:, b, :], ps_t[:, 0:P], ACT.Copy).then_inc(s[kind], 1)
                    elif kind == "exp":
                        done(act, s["logit"], t)
                        free(act, s["mix"], t)
                        nc.scalar.activation(eg[:, b, :], lg[:, b, :], ACT.Exp).then_inc(s[kind], 1)

                flow.run(act, emit)

            @block.vector
            def _(dve):
                for n in ("logit", "mix"):
                    dve.sem_inc(s[n], NB)
                dve.wait_ge(loaded, 4 * 16)
                nc.vector.tensor_scalar(we[:, :], we[:, :], gamma[:, 0:1], None, ALU.mult)
                nc.vector.tensor_scalar(wg[:, :], wg[:, :], gamma[:, 0:1], None, ALU.mult).then_inc(scaled, 1)
                dve.wait_ge(rms_in, 1)
                nc.vector.reciprocal(rr2[:, :], rms2[:, :]).then_inc(rms_out, 1)
                dve.wait_ge(rms_out, 1)

                def emit(kind, t, b):
                    if kind == "logit":
                        done(dve, s["mm"], t)
                        free(dve, s["exp"], t)
                        free1(dve, s["logit"], t)
                        nc.vector.scalar_tensor_tensor(lraw[:, :], ps_g[:, 0:E], rr2[:, bass.ds(t, 1)], bg[:, :], ALU.mult, ALU.add).then_inc(l_step, 1)
                        dve.wait_ge(l_step, t * 2 + 1)
                        nc.vector.tensor_reduce(ltop[:, :], lraw[:, :], AX.X, ALU.max).then_inc(l_step, 1)
                        dve.wait_ge(l_step, t * 2 + 2)
                        nc.vector.tensor_scalar(lg[:, b, :], lraw[:, :], ltop[:, 0:1], None, ALU.subtract).then_inc(s[kind], 1)
                    elif kind == "mix":
                        done(dve, s["exp"], t)
                        done(dve, s["mm"], t)
                        free1(dve, s["mix"], t)
                        nc.vector.tensor_reduce(esum[:, :], eg[:, b, :], AX.X, ALU.add).then_inc(m_step, 1)
                        dve.wait_ge(m_step, t * 6 + 1)
                        nc.vector.reciprocal(einv[:, :], esum[:, :]).then_inc(m_step, 1)
                        dve.wait_ge(m_step, t * 6 + 2)
                        nc.vector.tensor_scalar(gate[:, :], eg[:, b, :], einv[:, 0:1], rr2[:, bass.ds(t, 1)], ALU.mult, ALU.mult).then_inc(m_step, 1)
                        dve.wait_ge(m_step, t * 6 + 3)
                        nc.vector.tensor_tensor(mixed[:, :, :], ps_e[b][:, :].rearrange("p (e f) -> p e f", e=E),
                                                gate[:, :, None].broadcast_to([P, E, D]), ALU.mult).then_inc(m_step, 1)
                        nc.vector.tensor_tensor(xz[:, :], g.x[:, t, :], z2[:, t, :], ALU.add).then_inc(m_step, 1)
                        dve.wait_ge(m_step, t * 6 + 5)
                        nc.vector.tensor_reduce(comb[:, :], mixed[:, :, :].rearrange("p e f -> p f e"), AX.X, ALU.add).then_inc(m_step, 1)
                        dve.wait_ge(m_step, t * 6 + 6)
                        nc.vector.tensor_tensor(g.x[:, t, :], comb[:, :], xz[:, :], ALU.add).then_inc(s[kind], 1)

                flow.run(dve, emit)


MAGIC = 1.5 * 2.0 ** 23
QMAX = 127.0


def conv_ffn(nc, g, name, w):
    F = 512
    FC = F // P
    with ExitStack() as c:
        sem = semaphores(nc, c, name)
        sb = lambda n, s, d=F32: c.enter_context(nc.sbuf_tensor(f"{name}_{n}", s, d))
        pb = lambda n, s, d=F32: c.enter_context(nc.psum_tensor(f"{name}_{n}", s, d))
        NB = 2
        wt = [sb(f"wt{k}", [P, F]) for k in range(2)]
        wa = sb("wa", [P, F])
        wb = [sb(f"wb{k}", [P, F], BF16) for k in range(2)]
        wsum, wmean, wscale = sb("wsum", [P, 2]), sb("wmean", [P, 2]), sb("wscale", [P, 2])
        convw, convb = sb("convw", [P, FC, 3]), sb("convb", [P, FC])
        z = sb("z", [P, QT, D])
        amax, inv, scl = sb("amax", [P, QT]), sb("inv", [P, NB, QT]), sb("scl", [P, QT])
        za, zi, diag = sb("za", [P, QT, D]), sb("zi", [P, NB, QT, D], BF16), sb("diag", [P, NB, QT, P])
        xiT, invb = sb("xiT", [P, NB, S], BF16), sb("invb", [P, NB, S])
        hd, y0, y1 = sb("hd", [P, FC, S + 2]), sb("y0", [P, NB, FC, S]), sb("y1", [P, NB, FC, S])
        hs = sb("hs", [P, NB, FC, S])
        amax2, inv2, scl2 = sb("amax2", [P, QT]), sb("inv2", [P, NB, QT]), sb("scl2", [P, QT])
        ha2 = sb("ha2", [P, QT, D])
        ha, hi, hiT = sb("ha", [P, QT * F]), sb("hi", [P, NB, QT * F], BF16), sb("hiT", [P, NB, FC, S], BF16)
        identb = sb("identb", [P, P], BF16)
        ps_t, ps_b = pb("ps_t", [P, 512], BF16), pb("ps_b", [P, 512])
        ps_h, ps_u, ps_v, ps_y = pb("ps_h", [P, 1024]), pb("ps_u", [P, 1024]), pb("ps_v", [P, 1024], BF16), pb("ps_y", [P, 512])
        loaded, wstep, wsummed, prepared = sem("loaded"), sem("wstep"), sem("wsummed"), sem("prepared")
        names = ["quant", "turn", "turned", "up", "deq", "conv0", "conv", "silu", "back", "quant2", "turn2", "turned2", "down", "add"]
        s = {n: sem("s_" + n) for n in names}
        q_step, c_step, r_step, a_step = sem("q_step"), sem("c_step"), sem("r_step"), sem("a_step")
        order = [("back", 2), ("quant2", 2), ("turn2", 2), ("turned2", 2), ("down", 2), ("add", 2),
                 ("up", 1), ("deq", 1), ("conv0", 1), ("conv", 1), ("silu", 1), ("quant", 0), ("turn", 0), ("turned", 0)]
        flow = Flow(B, NB, order)
        done, free, free1 = flow.done, flow.free, flow.free1
        block = c.enter_context(nc.Block())

        @block.sync
        def _(sp):
            for dst, src in ((wt[0][:, :], w["w1"]), (wt[1][:, :], w["w2"]), (convw[:, :, :], w["convw"]), (convb[:, :], w["convb"])):
                sp.dma_start(dst, src).then_inc(loaded, 16)

        @block.tensor
        def _(pe):
            for n in ("turn", "up", "back", "turn2", "down"):
                pe.sem_inc(s[n], NB)
            pe.wait_ge(wstep, 2)
            nc.tensor.matmul(ps_y[:, 0:2], g.ones[:, :], wsum[:, :], start=True, stop=True).then_inc(wsummed, 1)
            pe.wait_ge(prepared, 1)

            def emit(kind, t, b):
                if kind == "turn":
                    done(pe, s["quant"], t)
                    free1(pe, s["turned"], t)
                    for q in range(QT):
                        nc.tensor.transpose(ps_t[:, q * P:(q + 1) * P], zi[:, b, q, :], identb[:, :])
                        r = nc.tensor.matmul(ps_b[:, q * P:(q + 1) * P], g.ones[:, :], diag[:, b, q, :], start=True, stop=True)
                    r.then_inc(s[kind], 1)
                elif kind == "up":
                    done(pe, s["turned"], t)
                    free1(pe, s["deq"], t)
                    for f in range(FC):
                        r = nc.tensor.matmul(ps_h[:, f * S:(f + 1) * S], wb[0][:, f * P:(f + 1) * P], xiT[:, b, :], start=True, stop=True)
                    r.then_inc(s[kind], 1)
                elif kind == "back":
                    done(pe, s["silu"], t)
                    free1(pe, s["quant2"], t)
                    for q in range(QT):
                        for f in range(FC):
                            r = nc.tensor.transpose(ps_u[:, q * F + f * P:q * F + (f + 1) * P], hs[:, b, f, q * P:(q + 1) * P], g.ident[:, :])
                    r.then_inc(s[kind], 1)
                elif kind == "turn2":
                    done(pe, s["quant2"], t)
                    free1(pe, s["turned2"], t)
                    for q in range(QT):
                        for f in range(FC):
                            r = nc.tensor.transpose(ps_v[:, f * S + q * P:f * S + (q + 1) * P], hi[:, b, q * F + f * P:q * F + (f + 1) * P], identb[:, :])
                    r.then_inc(s[kind], 1)
                elif kind == "down":
                    done(pe, s["turned2"], t)
                    free1(pe, s["add"], t)
                    for q in range(QT):
                        for f in range(FC):
                            r = nc.tensor.matmul(ps_y[:, q * D:(q + 1) * D], hiT[:, b, f, q * P:(q + 1) * P], wb[1][:, f * D:(f + 1) * D],
                                                 start=f == 0, stop=f == FC - 1)
                    r.then_inc(s[kind], 1)

            flow.run(pe, emit)

        @block.scalar
        def _(act):
            for n in ("turned", "conv0", "silu", "turned2"):
                act.sem_inc(s[n], NB)
            act.wait_ge(prepared, 1)

            def emit(kind, t, b):
                if kind == "turned":
                    done(act, s["turn"], t)
                    free(act, s["up"], t)
                    free(act, s["deq"], t)
                    nc.scalar.activation(xiT[:, b, :], ps_t[:, 0:S], ACT.Copy)
                    nc.scalar.activation(invb[:, b, :], ps_b[:, 0:S], ACT.Copy).then_inc(s[kind], 1)
                elif kind == "conv0":
                    done(act, s["deq"], t)
                    free(act, s["conv"], t)
                    for f in range(FC):
                        r = nc.scalar.activation(y0[:, b, f, :], hd[:, f, 1:S + 1], ACT.Identity, bias=convb[:, f:f + 1], scale=convw[:, f, 1:2])
                    r.then_inc(s[kind], 1)
                elif kind == "silu":
                    done(act, s["conv"], t)
                    free(act, s["back"], t)
                    nc.scalar.activation(hs[:, b, :, :], y0[:, b, :, :], ACT.Silu).then_inc(s[kind], 1)
                elif kind == "turned2":
                    done(act, s["turn2"], t)
                    free(act, s["down"], t)
                    nc.scalar.activation(hiT[:, b, :, :].rearrange("p f s -> p (f s)"), ps_v[:, :], ACT.Copy).then_inc(s[kind], 1)

            flow.run(act, emit)

        @block.vector
        def _(dve):
            for n in ("quant", "deq", "conv", "quant2", "add"):
                dve.sem_inc(s[n], NB)
            dve.wait_ge(loaded, 64)
            nc.vector.memset(hd[:, :, :], 0.0)
            nc.vector.tensor_copy(identb[:, :], g.ident[:, :])
            for k in range(2):
                nc.vector.tensor_reduce(wsum[:, k:k + 1], wt[k][:, :], AX.X, ALU.add, apply_absolute_value=True).then_inc(wstep, 1)
            dve.wait_ge(wsummed, 1)
            nc.vector.tensor_scalar(wmean[:, :], ps_y[:, 0:2], 1.0 / (F * D), 1e-5, ALU.mult, ALU.max).then_inc(wstep, 1)
            dve.wait_ge(wstep, 3)
            nc.vector.reciprocal(wscale[:, :], wmean[:, :]).then_inc(wstep, 1)
            nc.vector.tensor_scalar(convw[:, :, :], convw[:, :, :], wmean[:, 0:1], None, ALU.mult)
            for k in range(2):
                dve.wait_ge(wstep, 4 + 3 * k)
                nc.vector.tensor_scalar(wa[:, :], wt[k][:, :], wscale[:, k:k + 1], MAGIC, ALU.mult, ALU.add).then_inc(wstep, 1)
                dve.wait_ge(wstep, 5 + 3 * k)
                nc.vector.tensor_scalar(wt[k][:, :], wa[:, :], MAGIC - 1, MAGIC + 1, ALU.max, ALU.min).then_inc(wstep, 1)
                dve.wait_ge(wstep, 6 + 3 * k)
                nc.vector.tensor_scalar(wb[k][:, :], wt[k][:, :], MAGIC, None, ALU.subtract).then_inc(wstep, 1)
            dve.wait_ge(wstep, 10)
            nc.vector.tensor_copy(wa[:, 0:1], wmean[:, 0:1]).then_inc(prepared, 1)

            def scales(src, top, i_b, scl_, step, at, width):
                nc.vector.tensor_reduce(top[:, :], src, AX.X, ALU.max, apply_absolute_value=True).then_inc(step, 1)
                dve.wait_ge(step, at(1))
                nc.vector.tensor_scalar(i_b, top[:, :], 1e-5, 1.0 / QMAX, ALU.max, ALU.mult).then_inc(step, 1)
                dve.wait_ge(step, at(2))
                nc.vector.reciprocal(scl_[:, :], i_b).then_inc(step, 1)
                dve.wait_ge(step, at(3))

            def emit(kind, t, b):
                if kind == "quant":
                    free(dve, s["turn"], t)
                    free1(dve, s["quant"], t)
                    N = 7
                    at = lambda k: t * N + k
                    for q in range(QT):
                        nc.vector.tensor_scalar(z[:, q, :], g.xt[:, q, t, :], g.meant[:, q, bass.ds(t, 1)], g.rstdt[:, q, bass.ds(t, 1)],
                                                ALU.subtract, ALU.mult).then_inc(q_step, 1)
                    dve.wait_ge(q_step, at(2))
                    scales(z[:, :, :], amax, inv[:, b, :], scl, q_step, lambda k: at(2 + k), D)
                    for q in range(QT):
                        r = nc.vector.tensor_scalar(za[:, q, :], z[:, q, :], scl[:, q:q + 1], MAGIC, ALU.mult, ALU.add)
                    r.then_inc(q_step, 1)
                    dve.wait_ge(q_step, at(6))
                    nc.vector.tensor_scalar(z[:, :, :], za[:, :, :], MAGIC - 128, MAGIC + 127, ALU.max, ALU.min).then_inc(q_step, 1)
                    dve.wait_ge(q_step, at(7))
                    for q in range(QT):
                        nc.vector.tensor_scalar(diag[:, b, q, :], g.ident[:, :], inv[:, b, q:q + 1], None, ALU.mult)
                    nc.vector.tensor_scalar(zi[:, b, :, :], z[:, :, :], MAGIC, None, ALU.subtract).then_inc(s[kind], 1)
                elif kind == "deq":
                    done(dve, s["up"], t)
                    done(dve, s["turned"], t)
                    free1(dve, s["conv0"], t)
                    free1(dve, s["conv"], t)
                    nc.vector.tensor_tensor(hd[:, :, 1:S + 1], ps_h[:, :].rearrange("p (f s) -> p f s", f=FC),
                                            invb[:, b, None, :].broadcast_to([P, FC, S]), ALU.mult).then_inc(s[kind], 1)
                elif kind == "conv":
                    done(dve, s["conv0"], t)
                    free(dve, s["silu"], t)
                    for f in range(FC):
                        r = nc.vector.scalar_tensor_tensor(y1[:, b, f, :], hd[:, f, 0:S], convw[:, f, 0:1], y0[:, b, f, :], ALU.mult, ALU.add)
                    r.then_inc(c_step, 1)
                    dve.wait_ge(c_step, t + 1)
                    for f in range(FC):
                        r = nc.vector.scalar_tensor_tensor(y0[:, b, f, :], hd[:, f, 2:S + 2], convw[:, f, 2:3], y1[:, b, f, :], ALU.mult, ALU.add)
                    r.then_inc(s[kind], 1)
                elif kind == "quant2":
                    done(dve, s["back"], t)
                    free(dve, s["turn2"], t)
                    free1(dve, s["quant2"], t)
                    N = 5
                    at = lambda k: t * N + k
                    src = ps_u[:, :].rearrange("p (q f) -> p q f", q=QT)
                    scales(src, amax2, inv2[:, b, :], scl2, r_step, at, F)
                    for q in range(QT):
                        r = nc.vector.tensor_scalar(ha[:, q * F:(q + 1) * F], src[:, q, :], scl2[:, q:q + 1], MAGIC, ALU.mult, ALU.add)
                    r.then_inc(r_step, 1)
                    dve.wait_ge(r_step, at(4))
                    nc.vector.tensor_scalar(ha[:, :], ha[:, :], MAGIC - 128, MAGIC + 127, ALU.max, ALU.min).then_inc(r_step, 1)
                    dve.wait_ge(r_step, at(5))
                    nc.vector.tensor_scalar(hi[:, b, :], ha[:, :], MAGIC, None, ALU.subtract).then_inc(s[kind], 1)
                elif kind == "add":
                    done(dve, s["down"], t)
                    free1(dve, s["add"], t)
                    for q in range(QT):
                        r = nc.vector.tensor_scalar(ha2[:, q, :], ps_y[:, q * D:(q + 1) * D], inv2[:, b, q:q + 1], wmean[:, 1:2], ALU.mult, ALU.mult)
                    r.then_inc(a_step, 1)
                    dve.wait_ge(a_step, t + 1)
                    nc.vector.tensor_tensor(g.xb3[:, t, :, :], ha2[:, :, :], g.xb3[:, t, :, :], ALU.add).then_inc(s[kind], 1)

            flow.run(dve, emit)


def expert_ffn(nc, g, name, w, NF, FE, shared, routing):
    NC = NF // P
    NR = w["wr"].shape[1]
    NE = 32 if shared else 8
    NX = NE + shared
    BLK = 512
    NBLK = B * S // BLK
    with ExitStack() as c:
        sem = semaphores(nc, c, name)
        sb = lambda n, s, d=F32: c.enter_context(nc.sbuf_tensor(f"{name}_{n}", s, d))
        pb = lambda n, s, d=F32: c.enter_context(nc.psum_tensor(f"{name}_{n}", s, d))
        wg, wu, wd = sb("wg", [P, NC, P]), sb("wu", [P, NC, P]), sb("wd", [P, NC, D])
        sel = sb("sel", [NX, NC, P])
        combT = sb("combT", [NX, NBLK, BLK])
        loaded = sem("loaded")
        with ExitStack() as c1:
            sb1 = lambda n, s, d=F32: c1.enter_context(nc.sbuf_tensor(f"{name}_{n}", s, d))
            pb1 = lambda n, s, d=F32: c1.enter_context(nc.psum_tensor(f"{name}_{n}", s, d))
            wr = sb1("wr", [P, NR])
            lT = sb1("lT", [NR, NBLK, BLK])
            lg, sg, comb = sb1("lg", [P, NT, NR]), sb1("sg", [P, NT, NR]), sb1("comb", [P, NT, NX])
            ps_l, ps_k = [pb1(f"ps_l{k}", [P, 512]) for k in range(4)], pb1("ps_k", [P, 512])
            arrived, mm, out, turned, sig = sem("arrived"), sem("mm"), sem("out"), sem("turned"), sem("sig")
            routed, back, st = sem("routed"), sem("back"), sem("route_step")
            extra = routing.tiles(sb1)
            block = c1.enter_context(nc.Block())

            @block.sync
            def _(sp):
                sp.dma_start(wr[:, :], w["wr"]).then_inc(arrived, 16)
                for dst, src in routing.loads(extra, w):
                    sp.dma_start(dst, src).then_inc(arrived, 16)
                for dst, src in ((wg, w["wg"]), (wu, w["wu"]), (wd, w["wd"]), (sel, w["sel"])):
                    sp.dma_start(dst[:, :, :], src).then_inc(loaded, 16)

            @block.tensor
            def _(pe):
                pe.wait_ge(arrived, 16 * (1 + len(routing.loads(extra, w))))
                for k in range(NBLK):
                    nc.tensor.matmul(ps_l[k][0:NR, :], wr[:, :], g.xnT[:, 2 * k:2 * k + 2, :], start=True, stop=True).then_inc(mm, 1)
                pe.wait_ge(out, NBLK)
                for t in range(NT):
                    r = nc.tensor.transpose(ps_k[:, t * NR:(t + 1) * NR], lT[:, t // 4, t % 4 * P:(t % 4 + 1) * P], g.ident[0:NR, 0:NR])
                r.then_inc(turned, 1)
                pe.wait_ge(routed, 1)
                for t in range(NT):
                    r = nc.tensor.transpose(ps_l[t // 4][0:NX, t % 4 * P:(t % 4 + 1) * P], comb[:, t, :], g.ident[:, :])
                    if t % 4 == 3:
                        r.then_inc(back, 1)

            @block.scalar
            def _(act):
                for k in range(NBLK):
                    act.wait_ge(mm, k + 1)
                    nc.scalar.activation(lT[:, k, :], ps_l[k][0:NR, :], ACT.Copy).then_inc(out, 1)
                act.wait_ge(turned, 1)
                nc.scalar.activation(sg[:, :, :], ps_k[:, 0:NT * NR].rearrange("p (t n) -> p t n", n=NR), ACT.Sigmoid).then_inc(sig, 1)
                for k in range(NBLK):
                    act.wait_ge(back, k + 1)
                    nc.scalar.activation(combT[:, k, :], ps_l[k][0:NX, :], ACT.Copy).then_inc(out, 1)

            @block.vector
            def _(dve):
                count = [0]

                def step(r):
                    r.then_inc(st, 1)
                    count[0] += 1
                    dve.wait_ge(st, count[0])

                dve.wait_ge(sig, 1)
                dve.wait_ge(arrived, 16 * (1 + len(routing.loads(extra, w))))
                routing.route(nc, step, sg, comb, extra)
                nc.vector.tensor_copy(extra["done"][:, 0:1], comb[:, 0, 0:1]).then_inc(routed, 1)

        with ExitStack() as c1:
            sb1 = lambda n, s, d=F32: c1.enter_context(nc.sbuf_tensor(f"{name}b_{n}", s, d))
            pb1 = lambda n, s, d=F32: c1.enter_context(nc.psum_tensor(f"{name}b_{n}", s, d))
            HB = 4
            sg, su, h = sb1("sg", [P, 2, BLK]), sb1("su", [P, 2, BLK]), sb1("h", [P, HB, BLK])
            oT = sb1("oT", [P, BLK])
            ps_g, ps_u, ps_c = ([pb1(f"ps_{n}{k}", [P, BLK]) for k in range(2)] for n in "guc")
            ps_o, ps_x = pb1("ps_o", [P, BLK]), pb1("ps_x", [P, BLK])
            ins, silu, su_done, hid, down = sem("b_ins"), sem("b_silu"), sem("b_su"), sem("b_hidden"), sem("b_down")
            o_out, o_turned, added = sem("b_o_out"), sem("b_o_turned"), sem("b_added")
            block = c1.enter_context(nc.Block())

            @block.tensor
            def _(pe):
                pe.sem_inc(down, HB)
                pe.wait_ge(loaded, 64)

                with pe.Fori(0, NBLK // 2) as i:
                    def front(m):
                        j, cc = divmod(m, NC)
                        x = g.xnTb[:, i * 2 + j, :]
                        pe.wait_ge(hid, i * (2 * NC) + (m + 1))
                        nc.tensor.matmul(ps_g[m % 2][:, :], wg[:, cc, :], x, start=True, stop=True)
                        nc.tensor.matmul(ps_u[m % 2][:, :], wu[:, cc, :], x, start=True, stop=True)
                        nc.tensor.matmul(ps_c[m % 2][:, :], sel[:, cc, :], combT[:, i * 2 + j, :], start=True, stop=True).then_inc(ins, 1)

                    front(0)
                    for m in range(2 * NC):
                        j, cc = divmod(m, NC)
                        if m + 1 < 2 * NC:
                            front(m + 1)
                        pe.wait_ge(hid, i * (2 * NC) + (m + 3))
                        if cc == 0:
                            pe.wait_ge(o_out, i * 2 + (j + 1))
                        nc.tensor.matmul(ps_o[:, :], wd[:, cc, :], h[:, m % HB, :], start=cc == 0, stop=cc == NC - 1).then_inc(down, 1)
                        if cc == NC - 1:
                            pe.wait_ge(o_out, i * 2 + (j + 2))
                            pe.wait_ge(added, i * 2 + (j + 1))
                            for q in range(BLK // P):
                                r = nc.tensor.transpose(ps_x[:, q * P:(q + 1) * P], oT[:, q * P:(q + 1) * P], g.ident[:, :])
                            r.then_inc(o_turned, 1)

            @block.scalar
            def _(act):
                act.sem_inc(o_out, 1)
                with act.Fori(0, NBLK // 2) as i:
                    for m in range(2 * NC):
                        act.wait_ge(ins, i * (2 * NC) + (m + 1))
                        act.wait_ge(su_done, i * (2 * NC) + (m + 1))
                        nc.scalar.activation(sg[:, m % 2, :], ps_g[m % 2][:, :], ACT.Silu).then_inc(silu, 1)
                        if m % NC == NC - 1:
                            j = m // NC
                            act.wait_ge(down, i * (2 * NC) + (m + 1 + HB))
                            nc.scalar.activation(oT[:, :], ps_o[:, :], ACT.Copy).then_inc(o_out, 1)

            @block.vector
            def _(dve):
                dve.sem_inc(hid, 2)
                dve.sem_inc(su_done, 2)
                dve.sem_inc(added, 1)
                with dve.Fori(0, NBLK // 2) as i:
                    for m in range(2 * NC):
                        dve.wait_ge(silu, i * (2 * NC) + (m + 1))
                        nc.vector.tensor_tensor(su[:, m % 2, :], sg[:, m % 2, :], ps_u[m % 2][:, :], ALU.mult).then_inc(su_done, 1)
                        dve.wait_ge(su_done, i * (2 * NC) + (m + 3))
                        dve.wait_ge(down, i * (2 * NC) + (m + 1))
                        nc.vector.tensor_tensor(h[:, m % HB, :], su[:, m % 2, :], ps_c[m % 2][:, :], ALU.mult).then_inc(hid, 1)
                        if m % NC == NC - 1:
                            j = m // NC
                            dve.wait_ge(o_turned, i * 2 + (j + 1))
                            xb = g.xb4[:, i * 2 + j, :]
                            nc.vector.tensor_tensor(xb, ps_x[:, :], xb, ALU.add).then_inc(added, 1)


class PairedRouting:

    G, EPS = 4, 1e-9

    @staticmethod
    def tiles(sb):
        return dict(top=sb("r_top", [P, NT]), eq=sb("r_eq", [P, NT, 4]), den=sb("r_den", [P, NT]), inv=sb("r_inv", [P, NT]),
                    us=sb("r_us", [P, NT, 4]), ui=sb("r_ui", [P, NT, 4]), order=sb("r_order", [P, 4]), done=sb("r_done", [P, 1]))

    @staticmethod
    def loads(x, w):
        return [(x["order"][:, :], w["order"])]

    @staticmethod
    def route(nc, step, sg, comb, x):
        G = PairedRouting.G
        v, T = nc.vector, [P, NT, G]
        macro, micro = sg[:, :, 0:G], sg[:, :, G:3 * G].rearrange("p t (g e) -> p t g e", e=2)
        step(v.tensor_reduce(x["top"][:, :], macro, AX.X, ALU.max))
        step(v.tensor_tensor(x["eq"][:, :, :], macro, x["top"][:, :, None].broadcast_to(T), ALU.is_equal))
        step(v.tensor_tensor(x["eq"][:, :, :], x["eq"][:, :, :], x["order"][:, None, :].broadcast_to(T), ALU.mult))
        step(v.tensor_reduce(x["inv"][:, :], x["eq"][:, :, :], AX.X, ALU.max))
        step(v.tensor_tensor(x["eq"][:, :, :], x["eq"][:, :, :], x["inv"][:, :, None].broadcast_to(T), ALU.is_equal))
        step(v.tensor_scalar(x["den"][:, :], x["top"][:, :], PairedRouting.EPS, None, ALU.add))
        step(v.reciprocal(x["inv"][:, :], x["den"][:, :]))
        step(v.tensor_tensor(x["top"][:, :], x["top"][:, :], x["inv"][:, :], ALU.mult))
        step(v.tensor_tensor(x["eq"][:, :, :], x["eq"][:, :, :], x["top"][:, :, None].broadcast_to(T), ALU.mult))
        step(v.tensor_tensor(x["us"][:, :, :], micro[:, :, :, 0], micro[:, :, :, 1], ALU.add))
        step(v.tensor_scalar(x["us"][:, :, :], x["us"][:, :, :], PairedRouting.EPS, None, ALU.add))
        step(v.reciprocal(x["ui"][:, :, :], x["us"][:, :, :]))
        step(v.tensor_tensor(x["ui"][:, :, :], x["ui"][:, :, :], x["eq"][:, :, :], ALU.mult))
        for e in range(2):
            step(v.tensor_tensor(comb[:, :, :].rearrange("p t (g e) -> p t g e", e=2)[:, :, :, e], micro[:, :, :, e], x["ui"][:, :, :], ALU.mult))


class GroupedRouting:

    G, PER, TOPG, SCALE, TAKEN = 8, 4, 4, 2.5, -3.0e38

    @staticmethod
    def tiles(sb):
        E = 32
        return dict(bias=sb("r_bias", [P, E]), sc=sb("r_sc", [P, NT, E]), hi=sb("r_hi", [P, NT, 8, 2]), lo=sb("r_lo", [P, NT, 8, 2]),
                    a=sb("r_a", [P, NT, 8]), b=sb("r_b", [P, NT, 8]), gs=sb("r_gs", [P, NT, 8]),
                    gt=sb("r_gt", [P, NT, 8, 8]), eq=sb("r_eq", [P, NT, 8, 8]), before=sb("r_before", [P, 8, 8]),
                    m8=sb("r_m8", [P, NT, 8]), left=sb("r_left", [P, NT, E]), w=sb("r_w", [P, NT, E]), sum=sb("r_sum", [P, NT]),
                    inv=sb("r_inv", [P, NT]), done=sb("r_done", [P, 1]))

    @staticmethod
    def loads(x, w):
        return [(x["bias"][:, :], w["bias"]), (x["before"][:, :, :], w["before"])]

    @staticmethod
    def route(nc, step, sg, comb, x):
        R, v, E = GroupedRouting, nc.vector, 32
        step(v.tensor_tensor(x["sc"][:, :, :], sg[:, :, :], x["bias"][:, None, :].broadcast_to([P, NT, E]), ALU.add))
        sc = x["sc"][:, :, :].rearrange("p t (g k two) -> p (t g) k two", g=R.G, two=2)
        hi, lo = (x[n][:, :, :, :].rearrange("p t g k -> p (t g) k") for n in ("hi", "lo"))
        step(v.tensor_tensor(hi, sc[:, :, :, 0], sc[:, :, :, 1], ALU.max))
        step(v.tensor_tensor(lo, sc[:, :, :, 0], sc[:, :, :, 1], ALU.min))
        a, b, gs = (x[n][:, :, :].rearrange("p t g -> p (t g)") for n in ("a", "b", "gs"))
        step(v.tensor_tensor(a, hi[:, :, 0], hi[:, :, 1], ALU.min))
        step(v.tensor_tensor(b, lo[:, :, 0], lo[:, :, 1], ALU.max))
        step(v.tensor_tensor(b, a, b, ALU.max))
        step(v.tensor_tensor(a, hi[:, :, 0], hi[:, :, 1], ALU.max))
        step(v.tensor_tensor(gs, a, b, ALU.add))
        mine = x["gs"][:, :, :, None].broadcast_to([P, NT, 8, 8])
        other = x["gs"][:, :, None, :].broadcast_to([P, NT, 8, 8])
        step(v.tensor_tensor(x["gt"][:, :, :, :], other, mine, ALU.is_gt))
        step(v.tensor_tensor(x["eq"][:, :, :, :], other, mine, ALU.is_equal))
        step(v.tensor_tensor(x["eq"][:, :, :, :], x["eq"][:, :, :, :], x["before"][:, None, :, :].broadcast_to([P, NT, 8, 8]), ALU.mult))
        step(v.tensor_tensor(x["gt"][:, :, :, :], x["gt"][:, :, :, :], x["eq"][:, :, :, :], ALU.add))
        step(v.tensor_reduce(x["a"][:, :, :], x["gt"][:, :, :, :], AX.X, ALU.add))
        step(v.tensor_scalar(x["b"][:, :, :], x["a"][:, :, :], float(R.TOPG) - 0.5, None, ALU.is_lt))
        step(v.tensor_tensor(x["sc"][:, :, :].rearrange("p t (g k) -> p (t g) k", k=R.PER), x["sc"][:, :, :].rearrange("p t (g k) -> p (t g) k", k=R.PER),
                             b[:, :, None].broadcast_to([P, NT * 8, R.PER]), ALU.mult))
        for t in range(NT):
            r = v.max(x["m8"][:, t, :], x["sc"][:, t, :])
        step(r)
        for t in range(NT):
            r = v.match_replace(x["left"][:, t, :], x["m8"][:, t, :], x["sc"][:, t, :], R.TAKEN)
        step(r)
        step(v.tensor_scalar(x["left"][:, :, :], x["left"][:, :, :], R.TAKEN / 2, None, ALU.is_lt))
        step(v.tensor_tensor(x["w"][:, :, :], x["left"][:, :, :], sg[:, :, :], ALU.mult))
        step(v.tensor_reduce(x["sum"][:, :], x["w"][:, :, :], AX.X, ALU.add))
        step(v.tensor_scalar(x["sum"][:, :], x["sum"][:, :], 1e-20, 1.0 / R.SCALE, ALU.add, ALU.mult))
        step(v.reciprocal(x["inv"][:, :], x["sum"][:, :]))
        step(v.tensor_tensor(comb[:, :, 0:E], x["w"][:, :, :], x["inv"][:, :, None].broadcast_to([P, NT, E]), ALU.mult))
        step(v.memset(comb[:, :, E:E + 1], 1.0))


ONLY = None


class Resident:
    pass


def network(nc, a, out, stop=99):
    with ExitStack() as c:
        sb = lambda n, s, d=F32: c.enter_context(nc.sbuf_tensor(n, s, d))
        g = Resident()
        g.x = sb("x_sb", [P, NT, D])
        g.x4 = g.x[:, :, :].rearrange("p (i k) d -> p i k d", k=4)
        g.xb = g.x[:, :, :].rearrange("p (b q) d -> p b (q d)", q=QT)
        g.xnT = sb("xnT", [P, B, S])
        g.xnT4 = g.xnT[:, :, :].rearrange("p (i k) s -> p i (k s)", k=2)
        g.mv = sb("mv", [P, NT, 2])
        g.mean4 = g.mv[:, :, 0].rearrange("p (i k) -> p i k", k=4)
        g.std, g.rstd = sb("std", [P, NT]), sb("rstd", [P, NT])
        g.rstd4 = g.rstd[:, :].rearrange("p (i k) -> p i k", k=4)
        g.ident, g.sel, g.ones = sb("ident", [P, P]), sb("sel", [P, P]), sb("ones", [P, P])
        g.cols = sb("cols", [P, 8])
        g.blocks32 = sb("blocks32", [P, 4])
        g.blocks = sb("blocks", [P, 4], F16)
        g.xt = g.x[:, :, :].rearrange("p (b q) d -> p q b d", q=QT)
        g.xb3 = g.x[:, :, :].rearrange("p (b q) d -> p b q d", q=QT)
        g.xb4 = g.x[:, :, :].rearrange("p (j k) d -> p j (k d)", k=4)
        g.xnTb = g.xnT4
        g.meant = g.mv[:, :, 0].rearrange("p (b q) -> p q b", q=QT)
        g.rstdt = g.rstd[:, :].rearrange("p (b q) -> p q b", q=QT)
        g.rms, g.rrms = sb("rms", [P, NT]), sb("rrms", [P, NT])
        g.ones2 = sb("ones2", [1, S])
        g.ctxT_dram, g.ctxV_dram = a["ctxT"], a["ctxV"]
        arrived, made, copied = (c.enter_context(nc.semaphore(n)) for n in ("arrived", "made", "copied"))
        with nc.Block() as block:
            @block.sync
            def _(sp):
                sp.dma_start(g.x[:, :, :], a["x"]).then_inc(arrived, 16)
                sp.dma_start(g.ident[:, :], a["ident"]).then_inc(arrived, 16)
                sp.dma_start(g.sel[:, :], a["sel"]).then_inc(arrived, 16)
                sp.dma_start(g.cols[:, :], a["cols"]).then_inc(arrived, 16)
                sp.dma_start(g.blocks32[:, :], a["blocks"]).then_inc(arrived, 16)
                sp.wait_ge(arrived, 80)

            @block.vector
            def _(dve):
                nc.vector.memset(g.ones2[:, :], 1.0)
                nc.vector.memset(g.ones[:, :], 1.0).then_inc(made, 1)
                dve.wait_ge(arrived, 80)
                nc.vector.tensor_copy(g.blocks[:, :], g.blocks32[:, :]).then_inc(made, 1)
                dve.wait_ge(made, 2)
        phases = [
            lambda: (layer_norm(nc, g, "n0"), small_attention(nc, g, "a0", a["a0"], 8 ** -0.5, True)),
            lambda: (moments(nc, g, "n1", rms=True), head_mix_ffn(nc, g, "f0", a["f0"])),
            lambda: (layer_norm(nc, g, "n2"), wide_attention(nc, g, "a1", a["a1"], 16, 2, 64, 64 ** -0.5, 2, True, False)),
            lambda: (moments(nc, g, "n3"), conv_ffn(nc, g, "f1", a["f1"])),
            lambda: (layer_norm(nc, g, "n4"), wide_attention(nc, g, "a2", a["a2"], 1, 1, 128, 1.0, 4, False, True)),
            lambda: (layer_norm(nc, g, "n5"), expert_ffn(nc, g, "f2", a["f2"], 2048, 256, False, PairedRouting)),
            lambda: (layer_norm(nc, g, "n6"), small_attention(nc, g, "a3", a["a3"], 8 ** -0.5, False)),
            lambda: (layer_norm(nc, g, "n7"), expert_ffn(nc, g, "f3", a["f3"], 2176, 64, True, GroupedRouting)),
        ]
        if ONLY is not None:
            phases = [phases[k] for k in ONLY]
        for p in phases[:stop]:
            p()
        with nc.Block() as block:
            @block.sync
            def _(sp):
                sp.dma_start(out, g.x[:, :, :]).then_inc(copied, 16)
                sp.wait_ge(copied, 16)


def laid_out(inputs):
    import numpy as np
    f = {k: np.asarray(v) for k, v in inputs.items()}
    a = {}
    a["x"] = f["x"].reshape(NT, P, D).transpose(1, 0, 2)
    ctx = f["ctx_512"]
    a["ctxT"] = ctx.transpose(2, 0, 1)
    ctxv = np.zeros((B, KT * P, DC), np.float32)
    ctxv[:, :LK] = ctx
    a["ctxV"] = ctxv.reshape(B, KT, P, DC).transpose(2, 0, 1, 3)
    a["ident"] = np.eye(P, dtype=np.float32)
    part = np.arange(P)
    a["sel"] = (part[:, None] == part[None, :] // 32 * 32 + 8).astype(np.float32)
    cols = np.zeros((P, 8), np.float32)
    cols[:, 0] = LN_EPS
    cols[:, 1] = np.where(part % 32 == 24, 1.0, 8 ** -0.5)
    cols[:, 2] = np.where(part % 32 // 8 == 1, -1.0, 0.0)
    cols[:, 3] = np.where(part % 32 // 8 == 2, -1.0, 0.0)
    cols[:, 4] = np.where(part < DC, 0.0, -1.0)
    cols[:, 5] = np.where(part < DC, -1.0, 0.0)
    cols[:, 6] = 1e-6
    a["cols"] = cols
    a["blocks"] = (part[:, None] // 32 == np.arange(4)[None, :]).astype(np.float32)

    def small(name, Wq, bq, Wk, bk, Wv, bv, Wo, bo):
        wq = np.zeros((P, 16, 32), np.float32)
        wk = np.zeros((DC + 1, 16, 32), np.float32)
        wv = np.zeros((DC + 1, 16, 32), np.float32)
        wo = np.zeros((4, 32, 4, D), np.float32)
        b = np.zeros((4, 32, 4), np.float32)
        for r in range(3):
            wq[:, :, 8 * r:8 * r + 8] = Wq.reshape(D, 16, 8)
            wk[:DC, :, 8 * r:8 * r + 8] = Wk.reshape(DC, 16, 8)
            if bk is not None:
                wk[DC, :, 8 * r:8 * r + 8] = bk.reshape(16, 8)
                b[:, 8 * r:8 * r + 8, :] = bq.reshape(4, 4, 8).transpose(1, 2, 0)
        wk[DC, :, 24] = 1
        wv[:DC, :, 0:8] = Wv.reshape(DC, 16, 8)
        if bv is not None:
            wv[DC, :, 0:8] = bv.reshape(16, 8)
        wv[DC, :, 8] = 1
        wo[:, 0:8] = Wo.reshape(4, 4, 8, D).transpose(1, 2, 0, 3)
        for n, v, s in (("wq", wq, (P, 4, P)), ("wk", wk, (DC + 1, 4, P)), ("wv", wv, (DC + 1, 4, P)), ("wo", wo, (P, 4, D)),
                        ("bq", b, (P, 4)), ("bo", bo if bo is not None else np.zeros(D, np.float32), (1, D))):
            a[f"{name}.{n}"] = v.reshape(s)

    small("a0", *(f[f"L0_xattn_{n}"] for n in ("Wq", "bq", "Wk", "bk", "Wv", "bv", "Wo", "bo")))
    Wkv = f["L3_xattn_Wkv"]
    small("a3", f["L3_xattn_Wq"].T, None, Wkv[:D].T, None, Wkv[D:].T, None, f["L3_xattn_Wo"].T, None)
    heads = lambda m: m.reshape(m.shape[0], 16, 64).transpose(2, 1, 0)
    a["a1.wq"], a["a1.wk"], a["a1.wv"] = (heads(f["L1_xattn_" + n]) for n in ("Wq", "Wk", "Wv"))
    a["a1.wo"] = f["L1_xattn_Wo"].reshape(16, 64, D).transpose(1, 0, 2)
    a["a1.bo"] = f["L1_xattn_bo"][None]
    a["a2.wq"], a["a2.wk"] = f["L2_xattn_Wq"].T[:, None], f["L2_xattn_Wk"].T[:, None]
    a["a2.wv"] = f["L2_xattn_Wv"][:, None]
    a["a2.bq"], a["a2.bo"] = f["L2_xattn_bq"][:, None], f["L2_xattn_bv"][None]
    h = {k[7:]: v for k, v in f.items() if k.startswith("L0_ffn_")}
    a["f0.wq"], a["f0.wdT"], a["f0.wup"], a["f0.wo"] = h["Wq"], h["Wdown"].T, h["Wup"], h["Wo"]
    a["f0.bdown"], a["f0.bo"] = h["bdown"][:, None], h["bo"][None]
    a["f0.brow"] = np.concatenate([h["bq"], h["bup"]])[None]
    a["f0.gamma1"], a["f0.gamma2"] = h["gamma1"][:, None], h["gamma2"][:, None]
    a["f0.wg"], a["f0.bg"] = h["Wg"], np.broadcast_to(h["bg"], (P, 8))
    a["f0.we"] = h["We"].transpose(1, 0, 2).reshape(D, 8 * D)
    h = {k[7:]: v for k, v in f.items() if k.startswith("L1_ffn_")}
    a["f1.w1"] = h["w1"].T
    a["f1.w2"] = h["w2"].T.reshape(4, P, D).transpose(1, 0, 2).reshape(P, 512)
    a["f1.convw"] = h["conv_w"].reshape(4, P, 3).transpose(1, 0, 2)
    a["f1.convb"] = h["conv_b"].reshape(4, P).T
    h = {k[7:]: v for k, v in f.items() if k.startswith("L2_ffn_")}
    a["f2.wr"] = np.concatenate([h["macro_w"], h["micro_w"].transpose(1, 0, 2).reshape(D, 8)], 1)
    a["f2.wg"], a["f2.wu"] = (h[n].transpose(1, 0, 2).reshape(D, 16, P) for n in ("gate_w", "up_w"))
    a["f2.wd"] = h["down_w"].reshape(16, P, D).transpose(1, 0, 2)
    a["f2.sel"] = (np.arange(8)[:, None] == np.arange(2048)[None] // 256).astype(np.float32).reshape(8, 16, P)
    a["f2.order"] = np.broadcast_to(np.arange(4, 0, -1, dtype=np.float32), (P, 4))
    h = {k[7:]: v for k, v in f.items() if k.startswith("L3_ffn_")}
    a["f3.wr"] = h["gate_w"].T
    a["f3.wg"], a["f3.wu"] = (np.concatenate([h[n].reshape(2048, D), h[m]]).T.reshape(D, 17, P)
                              for n, m in (("w_gate", "sh_gate"), ("w_up", "sh_up")))
    a["f3.wd"] = np.concatenate([h["w_down"].transpose(0, 2, 1).reshape(2048, D), h["sh_down"].T]).reshape(17, P, D).transpose(1, 0, 2)
    a["f3.sel"] = (np.arange(33)[:, None] == np.minimum(np.arange(2176)[None] // 64, 32)).astype(np.float32).reshape(33, 17, P)
    a["f3.bias"] = np.broadcast_to(h["gate_bias"], (P, 32))
    a["f3.before"] = np.broadcast_to(np.tril(np.ones((8, 8), np.float32), -1), (P, 8, 8))
    return a


def kernel(**inputs):
    import numpy as np
    import concourse.bacc as bacc
    from concourse.bass_utils import run_bass_kernel_spmd

    nc = bacc.Bacc("TRN2", target_bir_lowering=False, num_devices=1)
    arrays, a = {}, {}
    for name, v in laid_out(inputs).items():
        v = np.ascontiguousarray(v)
        arrays["in_" + name.replace(".", "_")] = v
        t = nc.dram_tensor("in_" + name.replace(".", "_"), v.shape, F32, kind="ExternalInput").ap()
        if "." in name:
            a.setdefault(name.split(".")[0], {})[name.split(".")[1]] = t
        else:
            a[name] = t
    out = nc.dram_tensor("out", (P, NT, D), F32, kind="ExternalOutput").ap()
    network(nc, a, out)
    r = run_bass_kernel_spmd(nc, [arrays], core_ids=[0])
    return r.results[0]["out"].transpose(1, 0, 2).reshape(B, S, D)
```

```python
import math
from contextlib import ExitStack

import concourse.bass as bass
from concourse import mybir

F32 = mybir.dt.float32
F16 = mybir.dt.float16
BF16 = mybir.dt.bfloat16
ALU = mybir.AluOpType
ACT = mybir.ActivationFunctionType
AX = mybir.AxisListType

P = 128
B, S, D, DC, LK = 8, 256, 128, 64, 1601
NT = B * S // P
QT = S // P
KT = -(-LK // P)
LAST = LK - (KT - 1) * P
PIECES = [(0, 401), (401, 400), (801, 400), (1201, 400)]
NP_ = len(PIECES)
CB = DC + 2
LN_EPS = 1e-5


def rows(t):
    return P if t < KT - 1 else LAST


class Plan:

    def __init__(self, ahead, body, times, behind, incs, credits):
        self.ahead, self.body, self.times, self.behind, self.incs = ahead, body, times, behind, incs
        count = dict(credits)
        for op in ahead:
            self.number(op, count, None)
        start = dict(count)
        for op in body:
            self.number(op, count, None)
        self.step = {n: count[n] - start[n] for n in count}
        for n in count:
            count[n] = start[n] + times * self.step[n]
        for op in behind:
            self.number(op, count, None)

    def number(self, op, count, _):
        for n, k in self.incs[op["kind"]].items():
            count[n] += k
        op["count"] = dict(count)
        op["by"] = self.incs[op["kind"]]

    def at(self, op, name, i, less=0):
        v = op["count"][name] - less
        return v if i is None else i * self.step[name] + v

    def all(self):
        return ([(op, None) for op in self.ahead] + [(op, i) for i in range(self.times) for op in self.body]
                + [(op, None) for op in self.behind])

    def run(self, engine, emit):
        for op in self.ahead:
            emit(op, None)
        if self.times:
            with engine.Fori(0, self.times) as i:
                for op in self.body:
                    emit(op, i)
        for op in self.behind:
            emit(op, None)


def semaphores(nc, stack, name):
    taken = []

    def clear():
        first = last = None
        for k, handle in enumerate(sorted(taken, key=lambda h: h.num)):
            first = handle.num if k == 0 or handle.num != last + 1 else first
            last = handle.num
            runs[first] = last
        for first, last in runs.items():
            nc.gpsimd.sem_clear(range(first, last + 1))
        nc.all_engine_barrier()

    def sem(n):
        handle = stack.enter_context(nc.semaphore(f"{name}_{n}"))
        taken.append(handle)
        return handle

    runs = {}
    stack.callback(clear)
    return sem


def layer_norm(nc, g, name, need_xn=False):
    with ExitStack() as c:
        sem = semaphores(nc, c, name)
        sb = lambda n, s, d=F32: c.enter_context(nc.sbuf_tensor(f"{name}_{n}", s, d))
        stats = sb("stats", [P, NT, 6])
        xn = sb("xn", [P, 4, D])
        ps = c.enter_context(nc.psum_tensor(f"{name}_ps", [P, 512], F32))
        stats_done, moments_done, std_done = sem("stats_done"), sem("moments_done"), sem("std_done")
        rstd_done, xn_done, turned, xnT_done = sem("rstd_done"), sem("xn_done"), sem("turned"), sem("xnT_done")
        block = c.enter_context(nc.Block())

        @block.vector
        def _(dve):
            for t in range(NT):
                nc.vector.bn_stats(stats[:, t, :], g.x[:, t, :]).then_inc(stats_done, 1)
            for t in range(NT):
                dve.wait_ge(stats_done, t + 1)
                nc.vector.bn_aggr(g.mv[:, t, :], stats[:, t, :]).then_inc(moments_done, 1)
            dve.wait_ge(std_done, 1)
            nc.vector.reciprocal(g.rstd[:, :], g.std[:, :]).then_inc(rstd_done, 1)
            dve.wait_ge(rstd_done, 1)
            with dve.Fori(0, NT // 4) as i:
                dve.wait_ge(turned, i + 1)
                for k in range(4):
                    r = nc.vector.tensor_scalar(xn[:, k, :], g.x4[:, i, k, :], g.mean4[:, i, k:k + 1],
                                                g.rstd4[:, i, k:k + 1], ALU.subtract, ALU.mult)
                r.then_inc(xn_done, 1)

        @block.scalar
        def _(act):
            act.wait_ge(moments_done, NT)
            nc.scalar.activation(g.std[:, :], g.mv[:, :, 1], ACT.Sqrt, bias=g.cols[:, 0:1]).then_inc(std_done, 1)
            with act.Fori(0, NT // 4) as i:
                act.wait_ge(turned, i + 2)
                nc.scalar.activation(g.xnT4[:, i, :], ps[:, :], ACT.Copy).then_inc(xnT_done, 1)

        @block.tensor
        def _(pe):
            pe.sem_inc(turned, 1)
            with pe.Fori(0, NT // 4) as i:
                pe.wait_ge(xn_done, i + 1)
                pe.wait_ge(xnT_done, i + 1)
                for k in range(4):
                    r = nc.tensor.transpose(ps[:, k * P:(k + 1) * P], xn[:, k, :], g.ident[:, :])
                r.then_inc(turned, 1)

        @block.gpsimd
        def _(pool):
            pool.sem_inc(xnT_done, 1)


def split_context(nc, g, name):
    with ExitStack() as c:
        sem = semaphores(nc, c, name)
        stage = c.enter_context(nc.sbuf_tensor(f"{name}_stage", [P, 2, LK], F32))
        cast = c.enter_context(nc.sbuf_tensor(f"{name}_cast", [P, 2, LK], F16))
        c_a = c.enter_context(nc.sbuf_tensor(f"{name}_a", [P, 2, LK], F16))
        c_b = c.enter_context(nc.sbuf_tensor(f"{name}_b", [CB, 2, LK], F16))
        landed, cast_done, split_done, ones_done = sem("landed0"), sem("cast"), sem("split"), sem("ones")
        landed = [landed, sem("landed1")]
        stored = [sem("stored0"), sem("stored1")]
        block = c.enter_context(nc.Block())

        @block.sync
        def _(sp):
            for b in range(B):
                if b >= 2:
                    sp.wait_ge(split_done, b - 1)
                sp.dma_start(stage[0:DC, b % 2, :], g.ctxT_dram[:, b, :]).then_inc(landed[b % 2], 16)
                sp.dma_start(stage[DC:P, b % 2, :], g.ctxT_dram[:, b, :]).then_inc(landed[b % 2], 16)

        @block.scalar
        def _(act):
            act.wait_ge(ones_done, 1)

            def store(b):
                act.wait_ge(split_done, b + 1)
                act.dma_start(g.ctx_a[:, b, :], c_a[:, b % 2, :]).then_inc(stored[b % 2], 16)
                act.dma_start(g.ctx_b[:, b, :], c_b[:, b % 2, :]).then_inc(stored[b % 2], 16)

            for b in range(B):
                act.wait_ge(landed[b % 2], b // 2 * 32 + 32)
                if b >= 2:
                    act.wait_ge(stored[b % 2], b // 2 * 32)
                nc.scalar.activation(c_b[0:DC, b % 2, :], stage[0:DC, b % 2, :], ACT.Copy)
                nc.scalar.activation(cast[:, b % 2, :], stage[:, b % 2, :], ACT.Copy).then_inc(cast_done, 1)
                if b:
                    store(b - 1)
            store(B - 1)
            act.wait_ge(stored[0], B // 2 * 32)
            act.wait_ge(stored[1], B // 2 * 32)

        @block.vector
        def _(dve):
            nc.vector.memset(c_b[DC:CB, :, :], 1.0).then_inc(ones_done, 1)
            for b in range(B):
                dve.wait_ge(cast_done, b + 1)
                if b >= 2:
                    dve.wait_ge(stored[b % 2], b // 2 * 32)
                nc.vector.scalar_tensor_tensor(c_a[:, b % 2, :], cast[:, b % 2, :], g.cols[:, 4:5], stage[:, b % 2, :],
                                               ALU.mult, ALU.add).then_inc(split_done, 1)


def small_attention(nc, g, name, w, scale, has_bo):
    H, DH, HG, W = 16, 8, 4, 32
    G = H // HG
    MROW, SUM = 24, 8
    with ExitStack() as c:
        sem = semaphores(nc, c, name)
        sb = lambda n, s, d=F32: c.enter_context(nc.sbuf_tensor(f"{name}_{n}", s, d))
        pb = lambda n, s: c.enter_context(nc.psum_tensor(f"{name}_{n}", s, F32))
        wq, wo = sb("wq", [P, G, P]), sb("wo", [P, D])
        wk_a, wk_b, wv_a, wv_b = (sb(n, [r, G, P], F16) for n, r in (("wk_a", P), ("wk_b", CB), ("wv_a", P), ("wv_b", CB)))
        raw_a, raw_b = [sb(f"raw_a{k}", [P, G, P]) for k in range(2)], [sb(f"raw_b{k}", [CB, G, P]) for k in range(2)]
        wcast = sb("wcast", [CB, 2, G, P], F16)
        bq = sb("bq", [P, G])
        bqs = sb("bqs", [P, G])
        bo = sb("bo", [1, D])
        ctx_a, ctx_b = sb("ctx_a", [P, LK], F16), sb("ctx_b", [CB, LK], F16)
        k16 = sb("k16", [P, G, LK], F16)
        kcast = sb("kcast", [P, 401], F16)
        v = sb("v", [P, G, KT, P])
        qf, qcast, q16 = sb("qf", [P, S]), sb("qcast", [P, S], F16), sb("q16", [P, S], F16)
        q_max = sb("q_max", [P, 2, HG, S], F16)
        q_exp = sb("q_exp", [P, 2, HG, S], F16)
        mx = sb("mx", [P, QT, HG, NP_])
        negm = sb("negm", [P, QT, HG, W], F16)
        prob = sb("prob", [P, 4, HG * S])
        acc = sb("acc", [P, G, S])
        rec, on, onT = sb("rec", [P, QT, H]), sb("on", [P, QT, D]), sb("onT", [P, S])
        ps_s, ps_m = [pb(f"ps_s{i}", [P, 1024]) for i in range(2)], [pb(f"ps_m{i}", [P, 512]) for i in range(2)]
        ps_o, ps_w = pb("ps_o", [P, 512]), pb("ps_w", [P, 512])
        loaded, ctx_loaded = sem("loaded"), sem("ctx_loaded")
        qk, ex, pv, mm, mr, nm = sem("scores"), sem("exped"), sem("pv"), sem("maxmm"), sem("maxed"), sem("negmax")
        mj, mf, kc, qs, qb = sem("side"), sem("side_free"), sem("k_cast"), sem("q_split"), sem("q_blocks")
        ac, init, wsplit, rc = sem("acc_out"), sem("init"), sem("wsplit"), sem("recip")
        qc = sem("q_out")

        def step(s, total=None):
            ok = lambda k: total is None or 0 <= s + k < total
            gr = lambda k: (s + k) % G
            db = lambda k: (s + k) // G
            pieces = [(j, q, k) for j in range(HG) for q in range(QT) for k in range(NP_)]
            side = {}
            if ok(1):
                side[1] = dict(kind="Q2", g=gr(1), db=db(1), par=(s + 1) % 2)
            if ok(3):
                side[6] = dict(kind="Q1", g=gr(3), db=db(3), par=(s + 3) % 2)
                for k in range(4):
                    side[2 + k] = dict(kind="K", g=gr(3), db=db(3), piece=k, first=gr(3) == 0 and k == 0)
                    side[7 + k] = dict(kind="V", g=gr(3), db=db(3), quad=k, last=gr(3) == G - 1 and k == 3)
            if gr(0) == 0 and (total is None or s > 0) and s >= G:
                side[0] = dict(kind="T", q=0, db=db(0) - 1)
                side[11] = dict(kind="T", q=1, db=db(0) - 1)
                side[12] = dict(kind="W", db=db(0) - 1)
            ops = []
            split = None
            for t in range(KT):
                n, t2 = divmod(t + 2, KT)
                m = []
                if ok(2):
                    for k, (j, q, p) in enumerate(pieces[3 * t:3 * t + 3]):
                        m.append(dict(kind="M", g=gr(2), j=j, q=q, piece=p, par=(s + 2) % 2, first=t == 0 and k == 0))
                ops += m[0:1]
                if ok(n):
                    ops.append(dict(kind="S", g=gr(n), t=t2, par=(s + n) % 2))
                if split:
                    ops.append(split)
                split = dict(K="KD", Q1="Q1D", Q2="Q2D").get(side.get(t, {}).get("kind"))
                split = split and dict(side[t], kind=split)
                ops += m[1:2]
                if ok(0):
                    ops.append(dict(kind="PV", g=gr(0), t=t))
                ops += m[2:3]
                if t == 11 and ok(2):
                    ops.append(dict(kind="MF"))
                if t in side:
                    ops.append(side[t])
            if ok(0):
                ops.append(dict(kind="N", g=gr(0)))
            if side.get(12, {}).get("kind") == "W":
                ops.append(dict(kind="O", db=db(0) - 1))
            return ops

        total = B * G
        ahead = [o for s in (-3, -2, -1, 0) for o in step(s, total)]
        body = [o for s in range(1, G + 1) for o in step(s)]
        behind = [o for s in range(total - G + 1, total) for o in step(s, total)]
        behind += [dict(kind="T", q=0, db=B - 1), dict(kind="T", q=1, db=B - 1), dict(kind="W", db=B - 1), dict(kind="O", db=B - 1)]
        incs = {"S": dict(qk=1, ex=1), "PV": dict(pv=1), "M": dict(mm=1, mr=1), "MF": dict(nm=1),
                "K": dict(mj=1, mf=1, kc=1), "KD": {}, "V": dict(mj=1, mf=1), "Q1": dict(mj=1, mf=1), "Q2": dict(mj=1, mf=1),
                "Q1D": dict(qs=1, qb=1), "Q2D": dict(qs=1, qb=1), "N": dict(ac=1),
                "T": dict(mj=1, mf=1, rc=1), "W": dict(mj=1, mf=1), "O": dict(mj=1, mf=1)}
        plan = Plan(ahead, body, B - 1, behind, incs,
                    dict(qk=0, ex=2, pv=4, mm=0, mr=2, nm=0, mj=0, mf=1, kc=0, qs=1, qb=0, ac=0, rc=0))
        assert plan.step["ex"] % 4 == 0 and plan.step["mr"] % 2 == 0
        at = plan.at

        def batch(op, i):
            return op["db"] if i is None else i + op["db"]

        last_use = {batch(op, i): at(op, "mf", i) for op, i in plan.all() if op.get("last")}
        block = c.enter_context(nc.Block())

        @block.sync
        def _(sp):
            for dst, src in ((wq, w["wq"]), (raw_a[0], w["wk_a"]), (raw_b[0], w["wk_b"]), (raw_a[1], w["wv_a"]), (raw_b[1], w["wv_b"])):
                sp.dma_start(dst[:, :, :], src).then_inc(loaded, 16)
            for dst, src in ((wo, w["wo"]), (bq, w["bq"]), (bo, w["bo"])):
                sp.dma_start(dst[:, :], src).then_inc(loaded, 16)
            for b in range(B):
                if b:
                    sp.wait_ge(mf, last_use[b - 1])
                sp.dma_start(ctx_a[:, :], g.ctx_a[:, b, :]).then_inc(ctx_loaded, 16)
                sp.dma_start(ctx_b[:, :], g.ctx_b[:, b, :]).then_inc(ctx_loaded, 16)

        @block.tensor
        def _(pe):
            pe.sem_inc(pv, 4)
            pe.wait_ge(loaded, 8 * 16)
            pe.wait_ge(wsplit, 2)

            def emit(op, i):
                k = op["kind"]
                if k == "S":
                    t, n = op["t"], rows(op["t"])
                    if t == 0:
                        pe.wait_ge(qb, at(op, "qb", i))
                    pe.wait_ge(ex, at(op, "ex", i, 2))
                    slot = ps_s[op["count"]["qk"] % 2 ^ 1]
                    for h in range(2):
                        r = nc.tensor.matmul(slot[0:n, h * 512:h * 512 + 512], k16[:, op["g"], t * P:t * P + n],
                                             q_exp[:, op["par"], 2 * h:2 * h + 2, :], start=True, stop=True)
                    r.then_inc(qk, 1)
                elif k == "PV":
                    t, n = op["t"], rows(op["t"])
                    m = op["count"]["pv"] - 5
                    if t == 0 and (i is not None or op["count"]["ac"] > 0):
                        pe.wait_ge(ac, at(op, "ac", i))
                    pe.wait_ge(ex, at(op, "pv", i, 2))
                    for j in range(HG):
                        r = nc.tensor.matmul(ps_o[W * j:W * j + W, 0:S], v[0:n, op["g"], t, W * j:W * j + W],
                                             prob[0:n, m % 4, j * S:(j + 1) * S], start=t == 0, stop=t == KT - 1)
                    r.then_inc(pv, 1)
                elif k == "M":
                    if op["first"]:
                        pe.wait_ge(qb, at(op, "qb", i))
                    pe.wait_ge(mr, at(op, "mr", i, 2))
                    k0, n = PIECES[op["piece"]]
                    q = op["q"]
                    nc.tensor.matmul(ps_m[op["count"]["mm"] % 2 ^ 1][:, 0:n], q_max[:, op["par"], op["j"], q * P:(q + 1) * P],
                                     k16[:, op["g"], k0:k0 + n], start=True, stop=True).then_inc(mm, 1)
                elif k not in ("MF", "N", "KD", "Q1D", "Q2D"):
                    pe.wait_ge(mf, at(op, "mf", i, 1))
                    if k == "K":
                        if op["first"]:
                            b = batch(op, i)
                            pe.wait_ge(ctx_loaded, b * 32 + 32)
                        k0, n = PIECES[op["piece"]]
                        nc.tensor.matmul(ps_w[:, 0:n], wk_a[:, op["g"], :], ctx_a[:, k0:k0 + n], start=True, stop=False)
                        r = nc.tensor.matmul(ps_w[:, 0:n], wk_b[:, op["g"], :], ctx_b[:, k0:k0 + n], start=False, stop=True)
                    elif k == "V":
                        for t in range(4 * op["quad"], min(4 * op["quad"] + 4, KT)):
                            n = rows(t)
                            o = ps_w[0:n, (t % 4) * P:(t % 4) * P + P]
                            nc.tensor.matmul(o, ctx_a[:, t * P:t * P + n], wv_a[:, op["g"], :], start=True, stop=False)
                            r = nc.tensor.matmul(o, ctx_b[:, t * P:t * P + n], wv_b[:, op["g"], :], start=False, stop=True)
                    elif k in ("Q1", "Q2"):
                        r = nc.tensor.matmul(ps_w[:, 0:S], wq[:, op["g"], :], g.xnT[:, batch(op, i), :],
                                             start=True, stop=k == "Q1")
                        if k == "Q2":
                            pe.wait_ge(nm, at(op, "nm", i))
                            for q in range(QT):
                                r = nc.tensor.matmul(ps_w[:, q * P:(q + 1) * P], negm[:, q, :, :].rearrange("p a b -> p (a b)"),
                                                     g.ident16[:, :], start=False, stop=q == QT - 1)
                    elif k == "T":
                        pe.wait_ge(ac, at(op, "ac", i))
                        for gg in range(G):
                            r = nc.tensor.transpose(ps_w[:, gg * P:(gg + 1) * P], acc[:, gg, op["q"] * P:(op["q"] + 1) * P], g.ident[:, :])
                    elif k == "W":
                        for q in range(QT):
                            r = nc.tensor.transpose(ps_w[:, q * P:(q + 1) * P], on[:, q, :], g.ident[:, :])
                    elif k == "O":
                        for q in range(QT):
                            if has_bo:
                                nc.tensor.matmul(ps_w[:, q * D:(q + 1) * D], g.ones[0:1, :], bo[:, :], start=True, stop=False)
                            r = nc.tensor.matmul(ps_w[:, q * D:(q + 1) * D], onT[:, q * P:(q + 1) * P], wo[:, :], start=not has_bo, stop=True)
                    r.then_inc(mj, 1)

            plan.run(pe, emit)

        @block.scalar
        def _(act):
            act.sem_inc(ex, 2)
            act.wait_ge(loaded, 8 * 16)
            nc.scalar.activation(bqs[:, :], bq[:, :], ACT.Copy, scale=scale).then_inc(qc, 1)
            act.wait_ge(qc, 1)

            def emit(op, i):
                k = op["kind"]
                if k == "S":
                    t, n = op["t"], rows(op["t"])
                    act.wait_ge(qk, at(op, "qk", i))
                    act.wait_ge(pv, at(op, "qk", i))
                    nc.scalar.activation(prob[0:n, (op["count"]["qk"] - 1) % 4, :], ps_s[op["count"]["qk"] % 2 ^ 1][0:n, :],
                                         ACT.Exp).then_inc(ex, 1)
                elif k == "K":
                    act.wait_ge(mj, at(op, "mj", i))
                    n = PIECES[op["piece"]][1]
                    nc.scalar.activation(kcast[:, 0:n], ps_w[:, 0:n], ACT.Copy).then_inc(kc, 1)
                elif k == "V":
                    act.wait_ge(mj, at(op, "mj", i))
                    if op["quad"] < 3:
                        dst = v[:, op["g"], 4 * op["quad"]:4 * op["quad"] + 4, :].rearrange("p a b -> p (a b)")
                        r = nc.scalar.activation(dst, ps_w[:, :], ACT.Copy)
                    else:
                        r = nc.scalar.activation(v[0:LAST, op["g"], KT - 1, :], ps_w[0:LAST, 0:P], ACT.Copy)
                    r.then_inc(mf, 1)
                elif k in ("Q1", "Q2"):
                    act.wait_ge(mj, at(op, "mj", i))
                    act.wait_ge(qs, at(op, "qs", i))
                    nc.scalar.activation(qf[:, :], ps_w[:, 0:S], ACT.Identity, bias=bqs[:, op["g"]:op["g"] + 1],
                                         scale=g.cols[:, 1:2])
                    nc.scalar.activation(qcast[:, :], ps_w[:, 0:S], ACT.Identity, bias=bqs[:, op["g"]:op["g"] + 1],
                                         scale=g.cols[:, 1:2]).then_inc(mf, 1)
                elif k == "N":
                    act.wait_ge(pv, at(op, "pv", i))
                    act.wait_ge(mj, at(op, "mj", i))
                    nc.scalar.activation(acc[:, op["g"], :], ps_o[:, 0:S], ACT.Copy).then_inc(ac, 1)
                elif k == "W":
                    act.wait_ge(mj, at(op, "mj", i))
                    nc.scalar.activation(onT[:, :], ps_w[:, 0:S], ACT.Copy).then_inc(mf, 1)

            plan.run(act, emit)

        @block.vector
        def _(dve):
            nc.vector.memset(negm[:, :, :, :], 0.0).then_inc(init, 1)
            dve.sem_inc(mr, 2)
            dve.sem_inc(mf, 1)
            dve.sem_inc(qs, 1)
            dve.wait_ge(loaded, 8 * 16)
            for k, (w_a, w_b) in enumerate(((wk_a, wk_b), (wv_a, wv_b))):
                nc.vector.tensor_copy(w_a[:, :, :], raw_a[k][:, :, :])
                nc.vector.tensor_copy(wcast[:, k, :, :], raw_b[k][:, :, :]).then_inc(init, 1)
            dve.wait_ge(init, 3)
            for k, w_b in enumerate((wk_b, wv_b)):
                nc.vector.scalar_tensor_tensor(w_b[:, :, :], wcast[:, k, :, :], g.cols[0:CB, 7:8], raw_b[k][:, :, :], ALU.mult, ALU.add).then_inc(wsplit, 1)

            def emit(op, i):
                k = op["kind"]
                if k == "M":
                    if op["first"] and (i is not None or op["count"]["nm"] > 0):
                        dve.wait_ge(nm, at(op, "nm", i))
                    dve.wait_ge(mm, at(op, "mm", i))
                    n = PIECES[op["piece"]][1]
                    nc.vector.reduce_max(mx[:, op["q"], op["j"], op["piece"]:op["piece"] + 1],
                                         ps_m[op["count"]["mm"] % 2 ^ 1][:, 0:n], AX.X).then_inc(mr, 1)
                elif k == "MF":
                    dve.wait_ge(mr, at(op, "mr", i))
                    nc.vector.tensor_reduce(negm[:, :, :, MROW], mx[:, :, :, :], AX.X, ALU.max, negate=True).then_inc(nm, 1)
                elif k == "KD":
                    dve.wait_ge(kc, at(op, "kc", i))
                    k0, n = PIECES[op["piece"]]
                    nc.vector.scalar_tensor_tensor(k16[:, op["g"], k0:k0 + n], kcast[:, 0:n], g.cols[:, 2:3], ps_w[:, 0:n],
                                                   ALU.mult, ALU.add).then_inc(mf, 1)
                elif k in ("Q1D", "Q2D"):
                    dve.wait_ge(mf, at(op, "mf", i))
                    if op["count"]["qb"] > 1 or i is not None:
                        dve.wait_ge(qb, at(op, "qb", i, 1))
                    nc.vector.scalar_tensor_tensor(q16[:, :], qcast[:, :], g.cols[:, 3:4], qf[:, :],
                                                   ALU.mult, ALU.add).then_inc(qs, 1)
                elif k == "T":
                    dve.wait_ge(mj, at(op, "mj", i))
                    heads = ps_w[:, :].rearrange("p (h r) -> p h r", r=W)
                    nc.vector.reciprocal(rec[:, op["q"], :], heads[:, :, SUM]).then_inc(rc, 1)
                    dve.wait_ge(rc, at(op, "rc", i))
                    nc.vector.tensor_tensor(on[:, op["q"], :].rearrange("p (h d) -> p h d", d=DH), heads[:, :, 0:DH],
                                            rec[:, op["q"], :, None].broadcast_to([P, H, DH]), ALU.mult).then_inc(mf, 1)
                elif k == "O":
                    dve.wait_ge(mj, at(op, "mj", i))
                    xb = g.xb[:, batch(op, i), :]
                    nc.vector.tensor_tensor(xb, ps_w[:, 0:S], xb, ALU.add).then_inc(mf, 1)

            plan.run(dve, emit)

        @block.gpsimd
        def _(pool):
            def emit(op, i):
                if op["kind"] in ("Q1D", "Q2D"):
                    pool.wait_ge(qs, at(op, "qs", i))
                    dst = (q_max if op["kind"] == "Q1D" else q_exp)[:, op["par"], :, :]
                    nc.gpsimd.tensor_tensor(dst, q16[:, None, :].broadcast_to([P, HG, S]), g.blocks[:, :, None].broadcast_to([P, HG, S]), ALU.mult).then_inc(qb, 1)

            plan.run(pool, emit)


def wide_attention(nc, g, name, w, H, HG, DH, scale, KB, combined, biased):
    G = H // HG
    C1 = DC + 1
    N = HG * S
    OR = HG * DC
    PB = 8
    POOLED = 9
    SV = KT - POOLED + 1
    total = B * G
    BODY = 2 * G if G > 1 else total
    with ExitStack() as c:
        sem = semaphores(nc, c, name)
        sb = lambda n, s, d=F32: c.enter_context(nc.sbuf_tensor(f"{name}_{n}", s, d))
        pb = lambda n, s: c.enter_context(nc.psum_tensor(f"{name}_{n}", s, F32))
        wq, wk = sb("wq", [DH, H, D]), sb("wk", [DH, H, DC])
        wv = sb("wv", [DH if combined else DC, H, DC if combined else D])
        wo = sb("wo", [DH, H, D]) if combined else None
        bq = sb("bq", [DH, 1]) if biased else None
        bo = sb("bo", [1, D])
        wqk = sb("wqk", [P, H, P])
        bqk = sb("bqk", [1, P]) if biased else None
        wvo = sb("wvo", [OR, G, D])
        k_a, k_b = sb("k_a", [P, KB, LK], F16), sb("k_b", [C1, KB, LK], F16)
        v = sb("v", [P, KB, KT, DC])
        q_a, q_b = sb("q_a", [P, 4, N], F16), sb("q_b", [C1, 4, N], F16)
        mx, negm = sb("mx", [P, QT, HG, NP_]), sb("negm", [P, QT, HG], F16)
        prob = sb("prob", [P, PB, N])
        sum_p, sum_v = sb("sum_p", [P, 2, N]), sb("sum_v", [P, 2, N])
        acc, rec, on = sb("acc", [OR, S]), sb("rec", [OR, S]), sb("on", [OR, G, S])
        ps_s, ps_m = [pb(f"ps_s{i}", [P, 512]) for i in range(4)], [pb(f"ps_m{i}", [P, 512]) for i in range(2)]
        ps_o, ps_w = pb("ps_o", [P, 512]), pb("ps_w", [P, 512])
        loaded, ctx_in = sem("loaded"), [sem(f"ctx_in{k}") for k in range(KB)]
        qk, ex, pv, mm, mr, nm = sem("scores"), sem("exped"), sem("pv"), sem("maxmm"), sem("maxed"), sem("negmax")
        mj, mf, qc = sem("side"), sem("side_free"), sem("q_cast")
        ac, od = sem("acc_out"), sem("normed")
        sp_, sv = sem("sum_pool"), sem("sum_vector")
        folded, fold_out = sem("folded"), sem("fold_out")

        def step(s, total=None):
            ok = lambda k: total is None or 0 <= s + k < total
            f = lambda k: dict(s=s + k, g=(s + k) % G, db=(s + k) // G, kb=(s + k) // G % KB, par=(s + k) % 2, par4=(s + k) % 4)
            pieces = [(j, q, k) for j in range(HG) for q in range(QT) for k in range(NP_)]
            side = {}
            if ok(1):
                side[1] = [dict(kind="Q2", **f(1))]
            if ok(3):
                side[3] = [dict(kind="Q1", **f(3))]
                side[4] = [dict(kind="Q1D", **f(3))]
            if (total is None or s > 0) and ok(-1):
                side[2] = [dict(kind="C", **f(-1))]
                side[8] = [dict(kind="N", **f(-1))]
                side[9] = [dict(kind="ND", **f(-1))]
                if s % G == 0:
                    side[11] = [dict(kind="O", **f(-1))]
                    side[12] = [dict(kind="OD", **f(-1))]
            since = 0 if s < 2 else 1 + ((s - 1) % G == 0)
            ops = []
            for t in range(KT):
                n, t2 = divmod(t + 3, KT)
                m = []
                if ok(2):
                    for k, (j, q, p) in enumerate(pieces[2 * t - 2:2 * t] if t else []):
                        m.append(dict(kind="M", j=j, q=q, piece=p, first=t == 1 and k == 0, since=since, **f(2)))
                ops += m[0:1]
                if ok(n):
                    ops.append(dict(kind="S", t=t2, queries=side[1][0] if n and t2 == 0 else None, **f(n)))
                ops += [o for o in side.get(t, []) if o["kind"] in ("Q1D", "ND", "OD", "C")]
                ops += m[1:2]
                if ok(0):
                    ops.append(dict(kind="PV", t=t, **f(0)))
                if t == 9 and ok(2):
                    ops.append(dict(kind="MF"))
                ops += [o for o in side.get(t, []) if o["kind"] not in ("Q1D", "ND", "OD", "C")]
            if ok(0):
                ops.append(dict(kind="A", **f(0)))
            return ops

        ahead = [o for s in (-3, -2, -1, 0) for o in step(s, total)]
        times = total // BODY - 1
        body = [o for s in range(1, BODY + 1) for o in step(s)] if times else []
        behind = [o for s in range(total - BODY + 1, total) for o in step(s, total)]
        behind += [dict(kind=k, s=total - 1, g=G - 1, db=B - 1, par=(total - 1) % 2) for k in ("C", "N", "ND", "O", "OD")]
        incs = {"S": dict(qk=1, ex=1), "PV": dict(pv=1), "M": dict(mm=1, mr=1), "MF": dict(nm=1),
                "Q1": dict(mj=1, mf=1, qc=1), "Q1D": {}, "Q2": dict(mj=1, mf=1), "A": dict(ac=1),
                "N": dict(mj=1, mf=1), "ND": dict(od=1), "C": {}, "O": dict(mj=1, mf=1), "OD": {}}
        plan = Plan(ahead, body, times, behind, incs,
                    dict(qk=0, ex=4, pv=PB, mm=0, mr=2, nm=0, mj=0, mf=1, qc=0, ac=0, od=1))
        at = plan.at
        if times:
            assert plan.step["ex"] % PB == 0 and plan.step["mr"] % 2 == 0

        def step_of(op, i):
            return op["s"] if i is None else i * BODY + op["s"]

        def batch(op, i):
            return op["db"] if i is None else i * (BODY // G) + op["db"]

        attended = {batch(op, i): at(op, "pv", i) for op, i in plan.all() if op["kind"] == "PV" and op["t"] == KT - 1}
        block = c.enter_context(nc.Block())

        @block.sync
        def _(sp):
            loads = [(wq, w["wq"]), (wk, w["wk"]), (wv, w["wv"])] + ([(wo, w["wo"])] if combined else [])
            for dst, src in loads:
                sp.dma_start(dst[:, :, :], src).then_inc(loaded, 16)
            for dst, src in [(bo, w["bo"])] + ([(bq, w["bq"])] if biased else []):
                sp.dma_start(dst[:, :], src).then_inc(loaded, 16)
            for b in range(B):
                if b >= KB:
                    sp.wait_ge(pv, attended[b - KB])
                sp.dma_start(k_a[:, b % KB, :], g.ctx_a[:, b, :]).then_inc(ctx_in[b % KB], 16)
                sp.dma_start(k_b[:, b % KB, :], g.ctx_b[0:C1, b, :]).then_inc(ctx_in[b % KB], 16)
                sp.dma_start(v[:, b % KB, :, :], g.ctxV_dram[:, b, :, :]).then_inc(ctx_in[b % KB], 16)

        n_loads = 16 * (4 + combined + biased)

        @block.tensor
        def _(pe):
            pe.sem_inc(pv, PB)
            pe.wait_ge(loaded, n_loads)
            for h in range(H):
                if h >= 4:
                    pe.wait_ge(fold_out, h - 3)
                bank = ps_s[h % 4]
                r = nc.tensor.matmul(bank[:, 0:DC], wq[:, h, :], wk[:, h, :], start=True, stop=True)
                if combined:
                    r = nc.tensor.matmul(bank[0:DC, 256:256 + D], wv[:, h, :], wo[:, h, :], start=True, stop=True)
                r.then_inc(folded, 1)
            if biased:
                nc.tensor.matmul(ps_m[0][0:1, 0:DC], bq[:, :], wk[:, 0, :], start=True, stop=True).then_inc(folded, 1)
            pe.wait_ge(fold_out, H + biased + (not combined))

            def emit(op, i):
                k = op["kind"]
                if k == "S":
                    t, n = op["t"], rows(op["t"])
                    if t == 0:
                        q2 = op["queries"] or op
                        pe.wait_ge(mf, at(q2, "mf", i))
                    pe.wait_ge(ex, at(op, "ex", i, 4))
                    bank = ps_s[(op["count"]["qk"] - 1) % 4]
                    nc.tensor.matmul(bank[0:n, 0:N], k_a[:, op["kb"], t * P:t * P + n], q_a[:, op["par4"], :], start=True, stop=False)
                    nc.tensor.matmul(bank[0:n, 0:N], k_b[:, op["kb"], t * P:t * P + n], q_b[:, op["par4"], :],
                                     start=False, stop=True).then_inc(qk, 1)
                elif k == "PV":
                    t, n = op["t"], rows(op["t"])
                    m = op["count"]["pv"] - PB - 1
                    if t == 0 and (i is not None or op["count"]["ac"] > 0):
                        pe.wait_ge(ac, at(op, "ac", i))
                    pe.wait_ge(ex, at(op, "pv", i, PB - 4))
                    for j in range(HG):
                        r = nc.tensor.matmul(ps_o[DC * j:DC * j + DC, 0:S], v[0:n, op["kb"], t, :],
                                             prob[0:n, m % PB, j * S:(j + 1) * S], start=t == 0, stop=t == KT - 1)
                    r.then_inc(pv, 1)
                elif k == "M":
                    if op["first"]:
                        pe.wait_ge(mf, at(op, "mf", i, op["since"]))
                        if op["g"] == 0:
                            n = op["db"] // KB * 48 + 48
                            pe.wait_ge(ctx_in[op["kb"]], n if i is None else i * (BODY // G // KB * 48) + n)
                    pe.wait_ge(mr, at(op, "mr", i, 2))
                    k0, n = PIECES[op["piece"]]
                    q0 = op["j"] * S + op["q"] * P
                    nc.tensor.matmul(ps_m[(op["count"]["mm"] - 1) % 2][:, 0:n], q_a[:, op["par4"], q0:q0 + P],
                                     k_a[:, op["kb"], k0:k0 + n], start=True, stop=True).then_inc(mm, 1)
                elif k in ("Q1", "Q2", "N", "O"):
                    pe.wait_ge(mf, at(op, "mf", i, 1))
                    if k == "Q1":
                        for j in range(HG):
                            if biased:
                                nc.tensor.matmul(ps_w[:, j * S:(j + 1) * S], bqk[:, :], g.ones2[0:1, :], start=True, stop=False)
                            r = nc.tensor.matmul(ps_w[:, j * S:(j + 1) * S], wqk[:, op["g"] * HG + j, :], g.xnT[:, batch(op, i), :],
                                                 start=not biased, stop=True)
                    elif k == "Q2":
                        pe.wait_ge(nm, at(op, "nm", i))
                        for j in range(HG):
                            for q in range(QT):
                                c0 = j * S + q * P
                                r = nc.tensor.matmul(ps_w[DC:C1, c0:c0 + P], negm[:, q, j:j + 1], g.ident16[:, :], start=True, stop=True)
                    elif k == "N":
                        pe.wait_ge(sv, step_of(op, i) * SV + 2 * SV)
                        for j in range(HG):
                            r = nc.tensor.matmul(ps_w[DC * j:DC * j + DC, 0:S], g.ones[:, 0:DC], sum_v[:, op["par"], j * S:(j + 1) * S],
                                                 start=True, stop=True)
                    elif k == "O":
                        pe.wait_ge(od, at(op, "od", i))
                        for q in range(QT):
                            nc.tensor.matmul(ps_w[:, q * D:(q + 1) * D], g.ones[0:1, :], bo[:, :], start=True, stop=False)
                            for gg in range(G):
                                r = nc.tensor.matmul(ps_w[:, q * D:(q + 1) * D], on[:, gg, q * P:(q + 1) * P], wvo[:, gg, :],
                                                     start=False, stop=gg == G - 1)
                    r.then_inc(mj, 1)

            plan.run(pe, emit)

        @block.scalar
        def _(act):
            act.sem_inc(ex, 4)
            for h in range(H):
                act.wait_ge(folded, h + 1)
                bank = ps_s[h % 4]
                if combined:
                    nc.scalar.activation(wvo[h % HG * DC:h % HG * DC + DC, h // HG, :], bank[0:DC, 256:256 + D], ACT.Copy)
                for k in range(2):
                    r = nc.scalar.activation(wqk[:, h, k * DC:(k + 1) * DC], bank[:, 0:DC], ACT.Copy, scale=scale)
                r.then_inc(fold_out, 1)
            if not combined:
                act.wait_ge(loaded, n_loads)
                nc.scalar.activation(wvo[:, 0, :], wv[:, 0, :], ACT.Copy).then_inc(fold_out, 1)
            if biased:
                act.wait_ge(folded, H + 1)
                for k in range(2):
                    r = nc.scalar.activation(bqk[:, k * DC:(k + 1) * DC], ps_m[0][0:1, 0:DC], ACT.Copy, scale=scale)
                r.then_inc(fold_out, 1)

            def emit(op, i):
                k = op["kind"]
                if k == "S":
                    t, n = op["t"], rows(op["t"])
                    act.wait_ge(qk, at(op, "qk", i))
                    act.wait_ge(pv, at(op, "qk", i))
                    st = step_of(op, i)
                    if t >= PB:
                        act.wait_ge(sp_, st * POOLED + (POOLED + t - PB + 1))
                    elif t + KT - PB < POOLED:
                        act.wait_ge(sp_, st * POOLED + (t + KT - PB + 1))
                    else:
                        act.wait_ge(sv, st * SV + (t + KT - PB - POOLED + 1))
                    m = op["count"]["qk"] - 1
                    nc.scalar.activation(prob[0:n, m % PB, :], ps_s[m % 4][0:n, 0:N], ACT.Exp).then_inc(ex, 1)
                elif k == "Q1":
                    act.wait_ge(mj, at(op, "mj", i))
                    nc.scalar.activation(q_a[:, op["par4"], :], ps_w[:, 0:N], ACT.Copy).then_inc(qc, 1)
                elif k == "Q2":
                    act.wait_ge(mj, at(op, "mj", i))
                    nc.scalar.activation(q_b[DC:C1, op["par4"], :], ps_w[DC:C1, 0:N], ACT.Copy).then_inc(mf, 1)
                elif k == "A":
                    act.wait_ge(pv, at(op, "pv", i))
                    act.wait_ge(od, at(op, "od", i))
                    nc.scalar.activation(acc[:, :], ps_o[0:OR, 0:S], ACT.Copy).then_inc(ac, 1)

            plan.run(act, emit)

        @block.vector
        def _(dve):
            dve.sem_inc(mr, 2)
            dve.sem_inc(mf, 1)
            dve.sem_inc(od, 1)
            dve.sem_inc(sv, SV)

            def emit(op, i):
                k = op["kind"]
                if k == "PV" and op["t"] > POOLED:
                    t, n = op["t"], rows(op["t"])
                    m = op["count"]["pv"] - PB - 1
                    dve.wait_ge(ex, at(op, "pv", i, PB - 4))
                    dst = sum_v[0:n, op["par"], :]
                    if t == POOLED + 1:
                        nc.vector.tensor_tensor(dst, prob[:, (m - 1) % PB, :], prob[:, m % PB, :], ALU.add).then_inc(sv, 2)
                    else:
                        dve.wait_ge(sv, step_of(op, i) * SV + (t - POOLED + SV))
                        nc.vector.tensor_tensor(dst, dst, prob[0:n, m % PB, :], ALU.add).then_inc(sv, 1)
                elif k == "C":
                    dve.wait_ge(sp_, step_of(op, i) * POOLED + 2 * POOLED)
                    dve.wait_ge(sv, step_of(op, i) * SV + 2 * SV - 1)
                    dst = sum_v[:, op["par"], :]
                    nc.vector.tensor_tensor(dst, dst, sum_p[:, op["par"], :], ALU.add).then_inc(sv, 1)
                elif k == "M":
                    if op["first"] and (i is not None or op["count"]["nm"] > 0):
                        dve.wait_ge(nm, at(op, "nm", i))
                    dve.wait_ge(mm, at(op, "mm", i))
                    n = PIECES[op["piece"]][1]
                    nc.vector.reduce_max(mx[:, op["q"], op["j"], op["piece"]:op["piece"] + 1],
                                         ps_m[(op["count"]["mm"] - 1) % 2][:, 0:n], AX.X).then_inc(mr, 1)
                elif k == "MF":
                    dve.wait_ge(mr, at(op, "mr", i))
                    nc.vector.tensor_reduce(negm[:, :, :], mx[:, :, :, :], AX.X, ALU.max, negate=True).then_inc(nm, 1)
                elif k == "Q1D":
                    dve.wait_ge(qc, at(op, "qc", i))
                    nc.vector.scalar_tensor_tensor(q_b[0:DC, op["par4"], :], q_a[0:DC, op["par4"], :], g.cols[0:DC, 5:6],
                                                   ps_w[0:DC, 0:N], ALU.mult, ALU.add).then_inc(mf, 1)
                elif k == "ND":
                    dve.wait_ge(mj, at(op, "mj", i))
                    nc.vector.reciprocal(rec[:, :], ps_w[0:OR, 0:S]).then_inc(mf, 1)
                    dve.wait_ge(mf, at(op, "mf", i))
                    dve.wait_ge(ac, at(op, "ac", i))
                    nc.vector.tensor_tensor(on[:, op["g"], :], acc[:, :], rec[:, :], ALU.mult).then_inc(od, 1)
                elif k == "OD":
                    dve.wait_ge(mj, at(op, "mj", i))
                    xb = g.xb[:, batch(op, i), :]
                    nc.vector.tensor_tensor(xb, ps_w[:, 0:S], xb, ALU.add).then_inc(mf, 1)

            plan.run(dve, emit)

        @block.gpsimd
        def _(pool):
            pool.sem_inc(sp_, POOLED)

            def emit(op, i):
                if op["kind"] == "PV" and 0 < op["t"] < POOLED:
                    m = op["count"]["pv"] - PB - 1
                    pool.wait_ge(ex, at(op, "pv", i, PB - 4))
                    dst = sum_p[:, op["par"], :]
                    if op["t"] == 1:
                        if op["s"] >= 2 or i is not None:
                            pool.wait_ge(sv, step_of(op, i) * SV)
                        nc.gpsimd.tensor_tensor(dst, prob[:, (m - 1) % PB, :], prob[:, m % PB, :], ALU.add).then_inc(sp_, 2)
                    else:
                        pool.wait_ge(sp_, step_of(op, i) * POOLED + (op["t"] + POOLED))
                        nc.gpsimd.tensor_tensor(dst, dst, prob[:, m % PB, :], ALU.add).then_inc(sp_, 1)

            plan.run(pool, emit)


class Flow:

    def __init__(self, n, nbuf, order):
        self.n, self.nbuf, self.order = n, nbuf, order

    def run(self, engine, emit):
        n, nb = self.n, self.nbuf
        for s in range(nb):
            for kind, off in self.order:
                if 0 <= s - off < n:
                    emit(kind, s - off, (s - off) % nb)
        if n > nb:
            with engine.Fori(0, n // nb - 1) as i:
                for k in range(nb):
                    for kind, off in self.order:
                        emit(kind, i * nb + (nb + k - off), (k - off) % nb)
        for s in range(n, n + nb):
            for kind, off in self.order:
                if s - off < n:
                    emit(kind, s - off, (s - off) % nb)

    def done(self, engine, sem, t):
        engine.wait_ge(sem, t + (1 + self.nbuf))

    def free(self, engine, sem, t):
        engine.wait_ge(sem, t + 1)

    def free1(self, engine, sem, t):
        engine.wait_ge(sem, t + self.nbuf)


def moments(nc, g, name, rms=False):
    with ExitStack() as c:
        sem = semaphores(nc, c, name)
        stats = c.enter_context(nc.sbuf_tensor(f"{name}_stats", [P, NT, 6], F32))
        sq = c.enter_context(nc.sbuf_tensor(f"{name}_sq", [P, NT, 2], F32))
        stats_done, moments_done, std_done, rstd_done = sem("stats_done"), sem("moments_done"), sem("std_done"), sem("rstd_done")
        with nc.Block() as block:
            @block.vector
            def _(dve):
                for t in range(NT):
                    nc.vector.bn_stats(stats[:, t, :], g.x[:, t, :]).then_inc(stats_done, 1)
                for t in range(NT):
                    dve.wait_ge(stats_done, t + 1)
                    nc.vector.bn_aggr(g.mv[:, t, :], stats[:, t, :]).then_inc(moments_done, 1)
                dve.wait_ge(std_done, 1)
                nc.vector.reciprocal(g.rstd[:, :], g.std[:, :]).then_inc(rstd_done, 1)
                if rms:
                    dve.wait_ge(rstd_done, 1)
                    nc.vector.tensor_tensor(sq[:, :, 0], g.rstd[:, :], g.rstd[:, :], ALU.mult).then_inc(rstd_done, 1)
                    dve.wait_ge(rstd_done, 2)
                    nc.vector.tensor_tensor(sq[:, :, 1], sq[:, :, 0], g.mv[:, :, 1], ALU.mult).then_inc(rstd_done, 1)
                    dve.wait_ge(std_done, 2)
                    nc.vector.reciprocal(g.rrms[:, :], g.rms[:, :]).then_inc(rstd_done, 1)

            @block.scalar
            def _(act):
                act.wait_ge(moments_done, NT)
                nc.scalar.activation(g.std[:, :], g.mv[:, :, 1], ACT.Sqrt, bias=g.cols[:, 0:1]).then_inc(std_done, 1)
                if rms:
                    act.wait_ge(rstd_done, 3)
                    nc.scalar.activation(g.rms[:, :], sq[:, :, 1], ACT.Sqrt, bias=g.cols[:, 6:7]).then_inc(std_done, 1)


def head_mix_ffn(nc, g, name, w):
    H, DH, E = 16, 8, 8
    C3 = 3 * D
    with ExitStack() as c:
        sem = semaphores(nc, c, name)
        sb = lambda n, s, d=F32: c.enter_context(nc.sbuf_tensor(f"{name}_{n}", s, d))
        pb = lambda n, s, d=F32: c.enter_context(nc.psum_tensor(f"{name}_{n}", s, d))
        z2 = sb("z2", [P, NT, D])
        ms2, rms2, rr2 = sb("ms2", [P, NT]), sb("rms2", [P, NT]), sb("rr2", [P, NT])
        with ExitStack() as c1:
            sb1 = lambda n, s, d=F32: c1.enter_context(nc.sbuf_tensor(f"{name}_{n}", s, d))
            pb1 = lambda n, s, d=F32: c1.enter_context(nc.psum_tensor(f"{name}_{n}", s, d))
            wqkv, wdT, wup, wo = sb1("wqkv", [P, C3]), sb1("wdT", [DC, D]), sb1("wup", [DC, 2 * D]), sb1("wo", [P, D])
            bdown, bdb = sb1("bdown", [DC, 1]), sb1("bdb", [DC, P])
            brow, bo, bias = sb1("brow", [1, C3]), sb1("bo", [1, D]), sb1("bias", [P, C3])
            gamma = sb1("gamma", [P, 1])
            NB = 4
            z, zT, qkv = sb1("z", [P, NB, D]), sb1("zT", [P, NB, D]), sb1("qkv", [P, NB, C3])
            prod, att, eatt = sb1("prod", [P, NB, H * H * DH]), sb1("att", [P, NB, H * H]), sb1("eatt", [P, NB, H * H])
            top, esum, einv = sb1("top", [P, H]), sb1("esum", [P, H]), sb1("einv", [P, H])
            prod2, o_raw = sb1("prod2", [P, H * DH * H]), sb1("o_raw", [P, D])
            o, oT, zz, sqr = sb1("o", [P, NB, D]), sb1("oT", [P, NB, D]), sb1("zz", [P, D]), sb1("sqr", [P, D])
            ps_t, ps_q = [pb1(f"ps_t{k}", [P, 512]) for k in range(2)], [pb1(f"ps_q{k}", [P, 512]) for k in range(2)]
            ps_u, ps_y = [pb1(f"ps_u{k}", [P, 512]) for k in range(2)], [pb1(f"ps_y{k}", [P, 512]) for k in range(2)]
            loaded, folded, ready, biased = sem("loaded"), sem("folded"), sem("ready"), sem("biased")
            names = ["z", "turn", "zT", "qkvmm", "qkv", "prod", "att", "exp", "mix", "oturn", "oT", "omm", "z2", "sq"]
            s = {n: sem("s_" + n) for n in names}
            r_step, v_step, y_step = sem("r_step"), sem("v_step"), sem("y_step")
            order = [("omm", 4), ("z2", 4), ("sq", 4), ("mix", 3), ("oturn", 3), ("oT", 3), ("att", 2), ("exp", 2),
                     ("qkvmm", 1), ("qkv", 1), ("prod", 1), ("z", 0), ("turn", 0), ("zT", 0)]
            flow = Flow(NT, NB, order)
            done, free = flow.done, flow.free
            block = c1.enter_context(nc.Block())

            @block.sync
            def _(sp):
                for dst, src in ((wqkv[:, 0:D], w["wq"]), (wdT[:, :], w["wdT"]), (wup[:, :], w["wup"]), (wo[:, :], w["wo"]),
                                 (bdown[:, :], w["bdown"]), (brow[:, :], w["brow"]), (bo[:, :], w["bo"]), (gamma[:, :], w["gamma1"])):
                    sp.dma_start(dst, src).then_inc(loaded, 16)

            @block.tensor
            def _(pe):
                for n in ("turn", "qkvmm", "oturn", "omm"):
                    pe.sem_inc(s[n], NB)
                pe.wait_ge(loaded, 8 * 16)
                pe.wait_ge(ready, 1)
                nc.tensor.matmul(ps_q[0][:, 0:2 * D], wdT[:, :], wup[:, :], start=True, stop=True).then_inc(folded, 1)
                nc.tensor.matmul(ps_q[1][:, 0:C3], g.ones[0:1, :], brow[:, :], start=True, stop=False)
                nc.tensor.matmul(ps_q[1][:, D:C3], bdb[:, :], wup[:, :], start=False, stop=True).then_inc(folded, 1)
                pe.wait_ge(biased, 2)

                def emit(kind, t, b):
                    if kind == "turn":
                        done(pe, s["z"], t)
                        free(pe, s["zT"], t + 2)
                        nc.tensor.transpose(ps_t[b % 2][:, 0:P], z[:, b, :], g.ident[:, :]).then_inc(s[kind], 1)
                    elif kind == "qkvmm":
                        done(pe, s["zT"], t)
                        free(pe, s["qkv"], t + 2)
                        nc.tensor.matmul(ps_q[b % 2][:, 0:C3], zT[:, b, :], wqkv[:, :], start=True, stop=True).then_inc(s[kind], 1)
                    elif kind == "oturn":
                        done(pe, s["mix"], t)
                        free(pe, s["oT"], t + 2)
                        nc.tensor.transpose(ps_u[b % 2][:, 0:P], o[:, b, :], g.ident[:, :]).then_inc(s[kind], 1)
                    elif kind == "omm":
                        done(pe, s["oT"], t)
                        free(pe, s["z2"], t + 2)
                        nc.tensor.matmul(ps_y[b % 2][:, 0:D], g.ones[0:1, :], bo[:, :], start=True, stop=False)
                        nc.tensor.matmul(ps_y[b % 2][:, 0:D], oT[:, b, :], wo[:, :], start=False, stop=True).then_inc(s[kind], 1)

                flow.run(pe, emit)

            @block.scalar
            def _(act):
                for n in ("zT", "exp", "oT", "sq"):
                    act.sem_inc(s[n], NB)

                def emit(kind, t, b):
                    if kind == "zT":
                        done(act, s["turn"], t)
                        free(act, s["qkvmm"], t)
                        nc.scalar.activation(zT[:, b, :], ps_t[b % 2][:, 0:P], ACT.Copy).then_inc(s[kind], 1)
                    elif kind == "exp":
                        done(act, s["att"], t)
                        free(act, s["mix"], t)
                        nc.scalar.activation(eatt[:, b, :], att[:, b, :], ACT.Exp, scale=DH ** -0.5).then_inc(s[kind], 1)
                    elif kind == "oT":
                        done(act, s["oturn"], t)
                        free(act, s["omm"], t)
                        nc.scalar.activation(oT[:, b, :], ps_u[b % 2][:, 0:P], ACT.Copy).then_inc(s[kind], 1)
                    elif kind == "sq":
                        done(act, s["z2"], t)
                        flow.free1(act, s["sq"], t)
                        nc.scalar.activation(sqr[:, :], z2[:, t, :], ACT.Square, accum_out=ms2[:, bass.ds(t, 1)]).then_inc(s[kind], 1)

                flow.run(act, emit)

            @block.gpsimd
            def _(pool):
                pool.sem_inc(s["prod"], NB)

                def emit(kind, t, b):
                    if kind == "prod":
                        done(pool, s["qkv"], t)
                        free(pool, s["att"], t)
                        q = qkv[:, b, 0:D].rearrange("p (h d) -> p h d", d=DH)[:, :, None, :].broadcast_to([P, H, H, DH])
                        k = qkv[:, b, D:C3].rearrange("p (h d) -> p h d", d=2 * DH)[:, None, :, 0:DH].broadcast_to([P, H, H, DH])
                        nc.gpsimd.tensor_tensor(prod[:, b, :].rearrange("p (h k d) -> p h k d", h=H, k=H), q, k, ALU.mult).then_inc(s[kind], 1)

                flow.run(pool, emit)

            @block.vector
            def _(dve):
                for n in ("z", "qkv", "att", "mix", "z2"):
                    dve.sem_inc(s[n], NB)
                dve.wait_ge(loaded, 8 * 16)
                nc.vector.tensor_copy(bdb[:, :], bdown[:, 0:1].broadcast_to([DC, P])).then_inc(ready, 1)
                dve.wait_ge(folded, 2)
                nc.vector.tensor_scalar(wqkv[:, D:C3], ps_q[0][:, 0:2 * D], gamma[:, 0:1], None, ALU.mult)
                nc.vector.tensor_scalar(wqkv[:, 0:D], wqkv[:, 0:D], gamma[:, 0:1], None, ALU.mult).then_inc(biased, 1)
                nc.vector.tensor_copy(bias[:, :], ps_q[1][:, 0:C3]).then_inc(biased, 1)
                dve.wait_ge(biased, 2)

                def emit(kind, t, b):
                    if kind == "z":
                        free(dve, s["turn"], t)
                        nc.vector.tensor_scalar(z[:, b, :], g.x[:, t, :], g.mv[:, t, 0:1], g.rstd[:, bass.ds(t, 1)],
                                                ALU.subtract, ALU.mult).then_inc(s[kind], 1)
                    elif kind == "qkv":
                        done(dve, s["qkvmm"], t)
                        free(dve, s["mix"], t)
                        nc.vector.scalar_tensor_tensor(qkv[:, b, :], ps_q[b % 2][:, 0:C3], g.rrms[:, bass.ds(t, 1)], bias[:, :],
                                                       ALU.mult, ALU.add).then_inc(s[kind], 1)
                    elif kind == "att":
                        L = 3
                        done(dve, s["prod"], t)
                        free(dve, s["exp"], t)
                        a = att[:, b, :].rearrange("p (h k) -> p h k", h=H)
                        nc.vector.tensor_reduce(a, prod[:, b, :].rearrange("p (h k d) -> p h k d", h=H, k=H), AX.X, ALU.add).then_inc(r_step, 1)
                        dve.wait_ge(r_step, t * 2 + 1)
                        nc.vector.tensor_reduce(top[:, :], a, AX.X, ALU.max).then_inc(r_step, 1)
                        dve.wait_ge(r_step, t * 2 + 2)
                        nc.vector.tensor_tensor(a, a, top[:, :, None].broadcast_to([P, H, H]), ALU.subtract).then_inc(s[kind], 1)
                    elif kind == "mix":
                        done(dve, s["exp"], t)
                        free(dve, s["oturn"], t)
                        flow.free1(dve, s["mix"], t)
                        e = eatt[:, b, :].rearrange("p (h k) -> p h k", h=H)
                        v = qkv[:, b, D:C3].rearrange("p (k d) -> p d k", d=2 * DH)[:, DH:2 * DH, :]
                        pr = prod2[:, :].rearrange("p (h d k) -> p h d k", h=H, d=DH)
                        nc.vector.tensor_tensor(pr, e[:, :, None, :].broadcast_to([P, H, DH, H]),
                                                v[:, None, :, :].broadcast_to([P, H, DH, H]), ALU.mult).then_inc(v_step, 1)
                        nc.vector.tensor_reduce(esum[:, :], e, AX.X, ALU.add).then_inc(v_step, 1)
                        dve.wait_ge(v_step, t * 4 + 2)
                        nc.vector.reciprocal(einv[:, :], esum[:, :]).then_inc(v_step, 1)
                        nc.vector.tensor_reduce(o_raw[:, :].rearrange("p (h d) -> p h d", h=H), pr, AX.X, ALU.add).then_inc(v_step, 1)
                        dve.wait_ge(v_step, t * 4 + 4)
                        nc.vector.tensor_tensor(o[:, b, :].rearrange("p (h d) -> p h d", h=H), o_raw[:, :].rearrange("p (h d) -> p h d", h=H),
                                                einv[:, :, None].broadcast_to([P, H, DH]), ALU.mult).then_inc(s[kind], 1)
                    elif kind == "z2":
                        done(dve, s["omm"], t)
                        flow.free1(dve, s["z2"], t)
                        nc.vector.tensor_scalar(zz[:, :], g.x[:, t, :], g.mv[:, t, 0:1], g.rstd[:, bass.ds(t, 1)],
                                                ALU.subtract, ALU.mult).then_inc(y_step, 1)
                        dve.wait_ge(y_step, t + 1)
                        nc.vector.tensor_tensor(z2[:, t, :], ps_y[b % 2][:, 0:D], zz[:, :], ALU.add).then_inc(s[kind], 1)

                flow.run(dve, emit)

        with ExitStack() as c1:
            sb1 = lambda n, s, d=F32: c1.enter_context(nc.sbuf_tensor(f"{name}b_{n}", s, d))
            pb1 = lambda n, s, d=F32: c1.enter_context(nc.psum_tensor(f"{name}b_{n}", s, d))
            NB = 2
            wg, we, bg, gamma = sb1("wg", [P, E]), sb1("we", [P, E * D]), sb1("bg", [P, E]), sb1("gamma", [P, 1])
            zc, zT = sb1("zc", [P, NB, D]), sb1("zT", [P, NB, D])
            lg, eg = sb1("lg", [P, NB, E]), sb1("eg", [P, NB, E])
            lraw, ltop, esum, einv = sb1("lraw", [P, E]), sb1("ltop", [P, 1]), sb1("esum", [P, 1]), sb1("einv", [P, 1])
            gate, mixed, comb, xz = sb1("gate", [P, E]), sb1("mixed", [P, E, D]), sb1("comb", [P, D]), sb1("xz", [P, D])
            ps_t, ps_g = pb1("ps_t", [P, 512]), pb1("ps_g", [P, 512])
            ps_e = [pb1(f"ps_e{k}", [P, 1024]) for k in range(2)]
            loaded, rms_in, rms_out, scaled = sem("b_loaded"), sem("b_rms_in"), sem("b_rms_out"), sem("b_scaled")
            s = {n: sem("b_" + n) for n in ("copy", "turn", "zT", "mm", "logit", "exp", "mix")}
            l_step, m_step = sem("b_l_step"), sem("b_m_step")
            order = [("mix", 2), ("mm", 1), ("logit", 1), ("exp", 1), ("copy", 0), ("turn", 0), ("zT", 0)]
            flow = Flow(NT, NB, order)
            done, free, free1 = flow.done, flow.free, flow.free1
            block = c1.enter_context(nc.Block())

            @block.sync
            def _(sp):
                for dst, src in ((wg, w["wg"]), (we, w["we"]), (bg, w["bg"]), (gamma, w["gamma2"])):
                    sp.dma_start(dst[:, :], src).then_inc(loaded, 16)

            @block.tensor
            def _(pe):
                for n in ("turn", "mm"):
                    pe.sem_inc(s[n], NB)
                pe.wait_ge(scaled, 1)

                def emit(kind, t, b):
                    if kind == "turn":
                        done(pe, s["copy"], t)
                        free1(pe, s["zT"], t)
                        nc.tensor.transpose(ps_t[:, 0:P], zc[:, b, :], g.ident[:, :]).then_inc(s[kind], 1)
                    elif kind == "mm":
                        done(pe, s["zT"], t)
                        free1(pe, s["logit"], t)
                        free(pe, s["mix"], t)
                        nc.tensor.matmul(ps_g[:, 0:E], zT[:, b, :], wg[:, :], start=True, stop=True)
                        for k in range(2):
                            r = nc.tensor.matmul(ps_e[b][:, k * 512:(k + 1) * 512], zT[:, b, :], we[:, k * 512:(k + 1) * 512], start=True, stop=True)
                        r.then_inc(s[kind], 1)

                flow.run(pe, emit)

            @block.scalar
            def _(act):
                for n in ("copy", "zT", "exp"):
                    act.sem_inc(s[n], NB)
                nc.scalar.activation(rms2[:, :], ms2[:, :], ACT.Sqrt, bias=g.cols[:, 6:7], scale=1.0 / D).then_inc(rms_in, 1)

                def emit(kind, t, b):
                    if kind == "copy":
                        free(act, s["turn"], t)
                        nc.scalar.activation(zc[:, b, :], z2[:, t, :], ACT.Copy).then_inc(s[kind], 1)
                    elif kind == "zT":
                        done(act, s["turn"], t)
                        free(act, s["mm"], t)
                        nc.scalar.activation(zT[:, b, :], ps_t[:, 0:P], ACT.Copy).then_inc(s[kind], 1)
                    elif kind == "exp":
                        done(act, s["logit"], t)
                        free(act, s["mix"], t)
                        nc.scalar.activation(eg[:, b, :], lg[:, b, :], ACT.Exp).then_inc(s[kind], 1)

                flow.run(act, emit)

            @block.vector
            def _(dve):
                for n in ("logit", "mix"):
                    dve.sem_inc(s[n], NB)
                dve.wait_ge(loaded, 4 * 16)
                nc.vector.tensor_scalar(we[:, :], we[:, :], gamma[:, 0:1], None, ALU.mult)
                nc.vector.tensor_scalar(wg[:, :], wg[:, :], gamma[:, 0:1], None, ALU.mult).then_inc(scaled, 1)
                dve.wait_ge(rms_in, 1)
                nc.vector.reciprocal(rr2[:, :], rms2[:, :]).then_inc(rms_out, 1)
                dve.wait_ge(rms_out, 1)

                def emit(kind, t, b):
                    if kind == "logit":
                        done(dve, s["mm"], t)
                        free(dve, s["exp"], t)
                        free1(dve, s["logit"], t)
                        nc.vector.scalar_tensor_tensor(lraw[:, :], ps_g[:, 0:E], rr2[:, bass.ds(t, 1)], bg[:, :], ALU.mult, ALU.add).then_inc(l_step, 1)
                        dve.wait_ge(l_step, t * 2 + 1)
                        nc.vector.tensor_reduce(ltop[:, :], lraw[:, :], AX.X, ALU.max).then_inc(l_step, 1)
                        dve.wait_ge(l_step, t * 2 + 2)
                        nc.vector.tensor_scalar(lg[:, b, :], lraw[:, :], ltop[:, 0:1], None, ALU.subtract).then_inc(s[kind], 1)
                    elif kind == "mix":
                        done(dve, s["exp"], t)
                        done(dve, s["mm"], t)
                        free1(dve, s["mix"], t)
                        nc.vector.tensor_reduce(esum[:, :], eg[:, b, :], AX.X, ALU.add).then_inc(m_step, 1)
                        dve.wait_ge(m_step, t * 6 + 1)
                        nc.vector.reciprocal(einv[:, :], esum[:, :]).then_inc(m_step, 1)
                        dve.wait_ge(m_step, t * 6 + 2)
                        nc.vector.tensor_scalar(gate[:, :], eg[:, b, :], einv[:, 0:1], rr2[:, bass.ds(t, 1)], ALU.mult, ALU.mult).then_inc(m_step, 1)
                        dve.wait_ge(m_step, t * 6 + 3)
                        nc.vector.tensor_tensor(mixed[:, :, :], ps_e[b][:, :].rearrange("p (e f) -> p e f", e=E),
                                                gate[:, :, None].broadcast_to([P, E, D]), ALU.mult).then_inc(m_step, 1)
                        nc.vector.tensor_tensor(xz[:, :], g.x[:, t, :], z2[:, t, :], ALU.add).then_inc(m_step, 1)
                        dve.wait_ge(m_step, t * 6 + 5)
                        nc.vector.tensor_reduce(comb[:, :], mixed[:, :, :].rearrange("p e f -> p f e"), AX.X, ALU.add).then_inc(m_step, 1)
                        dve.wait_ge(m_step, t * 6 + 6)
                        nc.vector.tensor_tensor(g.x[:, t, :], comb[:, :], xz[:, :], ALU.add).then_inc(s[kind], 1)

                flow.run(dve, emit)


MAGIC = 1.5 * 2.0 ** 23
QMAX = 127.0


def conv_ffn(nc, g, name, w):
    F = 512
    FC = F // P
    with ExitStack() as c:
        sem = semaphores(nc, c, name)
        sb = lambda n, s, d=F32: c.enter_context(nc.sbuf_tensor(f"{name}_{n}", s, d))
        pb = lambda n, s, d=F32: c.enter_context(nc.psum_tensor(f"{name}_{n}", s, d))
        NB = 2
        wt = [sb(f"wt{k}", [P, F]) for k in range(2)]
        wa = sb("wa", [P, F])
        wb = [sb(f"wb{k}", [P, F], BF16) for k in range(2)]
        wsum, wmean, wscale = sb("wsum", [P, 2]), sb("wmean", [P, 2]), sb("wscale", [P, 2])
        convw, convb = sb("convw", [P, FC, 3]), sb("convb", [P, FC])
        z = sb("z", [P, QT, D])
        amax, inv, scl = sb("amax", [P, QT]), sb("inv", [P, NB, QT]), sb("scl", [P, QT])
        za, zi, diag = sb("za", [P, QT, D]), sb("zi", [P, NB, QT, D], BF16), sb("diag", [P, NB, QT, P])
        xiT, invb = sb("xiT", [P, NB, S], BF16), sb("invb", [P, NB, S])
        hd, y0, y1 = sb("hd", [P, FC, S + 2]), sb("y0", [P, NB, FC, S]), sb("y1", [P, NB, FC, S])
        hs = sb("hs", [P, NB, FC, S])
        amax2, inv2, scl2 = sb("amax2", [P, QT]), sb("inv2", [P, NB, QT]), sb("scl2", [P, QT])
        ha2 = sb("ha2", [P, QT, D])
        ha, hi, hiT = sb("ha", [P, QT * F]), sb("hi", [P, NB, QT * F], BF16), sb("hiT", [P, NB, FC, S], BF16)
        identb = sb("identb", [P, P], BF16)
        ps_t, ps_b = pb("ps_t", [P, 512], BF16), pb("ps_b", [P, 512])
        ps_h, ps_u, ps_v, ps_y = pb("ps_h", [P, 1024]), pb("ps_u", [P, 1024]), pb("ps_v", [P, 1024], BF16), pb("ps_y", [P, 512])
        loaded, wstep, wsummed, prepared = sem("loaded"), sem("wstep"), sem("wsummed"), sem("prepared")
        names = ["quant", "turn", "turned", "up", "deq", "conv0", "conv", "silu", "back", "quant2", "turn2", "turned2", "down", "add"]
        s = {n: sem("s_" + n) for n in names}
        q_step, c_step, r_step, a_step = sem("q_step"), sem("c_step"), sem("r_step"), sem("a_step")
        order = [("back", 2), ("quant2", 2), ("turn2", 2), ("turned2", 2), ("down", 2), ("add", 2),
                 ("up", 1), ("deq", 1), ("conv0", 1), ("conv", 1), ("silu", 1), ("quant", 0), ("turn", 0), ("turned", 0)]
        flow = Flow(B, NB, order)
        done, free, free1 = flow.done, flow.free, flow.free1
        block = c.enter_context(nc.Block())

        @block.sync
        def _(sp):
            for dst, src in ((wt[0][:, :], w["w1"]), (wt[1][:, :], w["w2"]), (convw[:, :, :], w["convw"]), (convb[:, :], w["convb"])):
                sp.dma_start(dst, src).then_inc(loaded, 16)

        @block.tensor
        def _(pe):
            for n in ("turn", "up", "back", "turn2", "down"):
                pe.sem_inc(s[n], NB)
            pe.wait_ge(wstep, 2)
            nc.tensor.matmul(ps_y[:, 0:2], g.ones[:, :], wsum[:, :], start=True, stop=True).then_inc(wsummed, 1)
            pe.wait_ge(prepared, 1)

            def emit(kind, t, b):
                if kind == "turn":
                    done(pe, s["quant"], t)
                    free1(pe, s["turned"], t)
                    for q in range(QT):
                        nc.tensor.transpose(ps_t[:, q * P:(q + 1) * P], zi[:, b, q, :], identb[:, :])
                        r = nc.tensor.matmul(ps_b[:, q * P:(q + 1) * P], g.ones[:, :], diag[:, b, q, :], start=True, stop=True)
                    r.then_inc(s[kind], 1)
                elif kind == "up":
                    done(pe, s["turned"], t)
                    free1(pe, s["deq"], t)
                    for f in range(FC):
                        r = nc.tensor.matmul(ps_h[:, f * S:(f + 1) * S], wb[0][:, f * P:(f + 1) * P], xiT[:, b, :], start=True, stop=True)
                    r.then_inc(s[kind], 1)
                elif kind == "back":
                    done(pe, s["silu"], t)
                    free1(pe, s["quant2"], t)
                    for q in range(QT):
                        for f in range(FC):
                            r = nc.tensor.transpose(ps_u[:, q * F + f * P:q * F + (f + 1) * P], hs[:, b, f, q * P:(q + 1) * P], g.ident[:, :])
                    r.then_inc(s[kind], 1)
                elif kind == "turn2":
                    done(pe, s["quant2"], t)
                    free1(pe, s["turned2"], t)
                    for q in range(QT):
                        for f in range(FC):
                            r = nc.tensor.transpose(ps_v[:, f * S + q * P:f * S + (q + 1) * P], hi[:, b, q * F + f * P:q * F + (f + 1) * P], identb[:, :])
                    r.then_inc(s[kind], 1)
                elif kind == "down":
                    done(pe, s["turned2"], t)
                    free1(pe, s["add"], t)
                    for q in range(QT):
                        for f in range(FC):
                            r = nc.tensor.matmul(ps_y[:, q * D:(q + 1) * D], hiT[:, b, f, q * P:(q + 1) * P], wb[1][:, f * D:(f + 1) * D],
                                                 start=f == 0, stop=f == FC - 1)
                    r.then_inc(s[kind], 1)

            flow.run(pe, emit)

        @block.scalar
        def _(act):
            for n in ("turned", "conv0", "silu", "turned2"):
                act.sem_inc(s[n], NB)
            act.wait_ge(prepared, 1)

            def emit(kind, t, b):
                if kind == "turned":
                    done(act, s["turn"], t)
                    free(act, s["up"], t)
                    free(act, s["deq"], t)
                    nc.scalar.activation(xiT[:, b, :], ps_t[:, 0:S], ACT.Copy)
                    nc.scalar.activation(invb[:, b, :], ps_b[:, 0:S], ACT.Copy).then_inc(s[kind], 1)
                elif kind == "conv0":
                    done(act, s["deq"], t)
                    free(act, s["conv"], t)
                    for f in range(FC):
                        r = nc.scalar.activation(y0[:, b, f, :], hd[:, f, 1:S + 1], ACT.Identity, bias=convb[:, f:f + 1], scale=convw[:, f, 1:2])
                    r.then_inc(s[kind], 1)
                elif kind == "silu":
                    done(act, s["conv"], t)
                    free(act, s["back"], t)
                    nc.scalar.activation(hs[:, b, :, :], y0[:, b, :, :], ACT.Silu).then_inc(s[kind], 1)
                elif kind == "turned2":
                    done(act, s["turn2"], t)
                    free(act, s["down"], t)
                    nc.scalar.activation(hiT[:, b, :, :].rearrange("p f s -> p (f s)"), ps_v[:, :], ACT.Copy).then_inc(s[kind], 1)

            flow.run(act, emit)

        @block.vector
        def _(dve):
            for n in ("quant", "deq", "conv", "quant2", "add"):
                dve.sem_inc(s[n], NB)
            dve.wait_ge(loaded, 64)
            nc.vector.memset(hd[:, :, :], 0.0)
            nc.vector.tensor_copy(identb[:, :], g.ident[:, :])
            for k in range(2):
                nc.vector.tensor_reduce(wsum[:, k:k + 1], wt[k][:, :], AX.X, ALU.add, apply_absolute_value=True).then_inc(wstep, 1)
            dve.wait_ge(wsummed, 1)
            nc.vector.tensor_scalar(wmean[:, :], ps_y[:, 0:2], 1.0 / (F * D), 1e-5, ALU.mult, ALU.max).then_inc(wstep, 1)
            dve.wait_ge(wstep, 3)
            nc.vector.reciprocal(wscale[:, :], wmean[:, :]).then_inc(wstep, 1)
            nc.vector.tensor_scalar(convw[:, :, :], convw[:, :, :], wmean[:, 0:1], None, ALU.mult)
            for k in range(2):
                dve.wait_ge(wstep, 4 + 3 * k)
                nc.vector.tensor_scalar(wa[:, :], wt[k][:, :], wscale[:, k:k + 1], MAGIC, ALU.mult, ALU.add).then_inc(wstep, 1)
                dve.wait_ge(wstep, 5 + 3 * k)
                nc.vector.tensor_scalar(wt[k][:, :], wa[:, :], MAGIC - 1, MAGIC + 1, ALU.max, ALU.min).then_inc(wstep, 1)
                dve.wait_ge(wstep, 6 + 3 * k)
                nc.vector.tensor_scalar(wb[k][:, :], wt[k][:, :], MAGIC, None, ALU.subtract).then_inc(wstep, 1)
            dve.wait_ge(wstep, 10)
            nc.vector.tensor_copy(wa[:, 0:1], wmean[:, 0:1]).then_inc(prepared, 1)

            def scales(src, top, i_b, scl_, step, at, width):
                nc.vector.tensor_reduce(top[:, :], src, AX.X, ALU.max, apply_absolute_value=True).then_inc(step, 1)
                dve.wait_ge(step, at(1))
                nc.vector.tensor_scalar(i_b, top[:, :], 1e-5, 1.0 / QMAX, ALU.max, ALU.mult).then_inc(step, 1)
                dve.wait_ge(step, at(2))
                nc.vector.reciprocal(scl_[:, :], i_b).then_inc(step, 1)
                dve.wait_ge(step, at(3))

            def emit(kind, t, b):
                if kind == "quant":
                    free(dve, s["turn"], t)
                    free1(dve, s["quant"], t)
                    N = 7
                    at = lambda k: t * N + k
                    for q in range(QT):
                        nc.vector.tensor_scalar(z[:, q, :], g.xt[:, q, t, :], g.meant[:, q, bass.ds(t, 1)], g.rstdt[:, q, bass.ds(t, 1)],
                                                ALU.subtract, ALU.mult).then_inc(q_step, 1)
                    dve.wait_ge(q_step, at(2))
                    scales(z[:, :, :], amax, inv[:, b, :], scl, q_step, lambda k: at(2 + k), D)
                    for q in range(QT):
                        r = nc.vector.tensor_scalar(za[:, q, :], z[:, q, :], scl[:, q:q + 1], MAGIC, ALU.mult, ALU.add)
                    r.then_inc(q_step, 1)
                    dve.wait_ge(q_step, at(6))
                    nc.vector.tensor_scalar(z[:, :, :], za[:, :, :], MAGIC - 128, MAGIC + 127, ALU.max, ALU.min).then_inc(q_step, 1)
                    dve.wait_ge(q_step, at(7))
                    for q in range(QT):
                        nc.vector.tensor_scalar(diag[:, b, q, :], g.ident[:, :], inv[:, b, q:q + 1], None, ALU.mult)
                    nc.vector.tensor_scalar(zi[:, b, :, :], z[:, :, :], MAGIC, None, ALU.subtract).then_inc(s[kind], 1)
                elif kind == "deq":
                    done(dve, s["up"], t)
                    done(dve, s["turned"], t)
                    free1(dve, s["conv0"], t)
                    free1(dve, s["conv"], t)
                    nc.vector.tensor_tensor(hd[:, :, 1:S + 1], ps_h[:, :].rearrange("p (f s) -> p f s", f=FC),
                                            invb[:, b, None, :].broadcast_to([P, FC, S]), ALU.mult).then_inc(s[kind], 1)
                elif kind == "conv":
                    done(dve, s["conv0"], t)
                    free(dve, s["silu"], t)
                    for f in range(FC):
                        r = nc.vector.scalar_tensor_tensor(y1[:, b, f, :], hd[:, f, 0:S], convw[:, f, 0:1], y0[:, b, f, :], ALU.mult, ALU.add)
                    r.then_inc(c_step, 1)
                    dve.wait_ge(c_step, t + 1)
                    for f in range(FC):
                        r = nc.vector.scalar_tensor_tensor(y0[:, b, f, :], hd[:, f, 2:S + 2], convw[:, f, 2:3], y1[:, b, f, :], ALU.mult, ALU.add)
                    r.then_inc(s[kind], 1)
                elif kind == "quant2":
                    done(dve, s["back"], t)
                    free(dve, s["turn2"], t)
                    free1(dve, s["quant2"], t)
                    N = 5
                    at = lambda k: t * N + k
                    src = ps_u[:, :].rearrange("p (q f) -> p q f", q=QT)
                    scales(src, amax2, inv2[:, b, :], scl2, r_step, at, F)
                    for q in range(QT):
                        r = nc.vector.tensor_scalar(ha[:, q * F:(q + 1) * F], src[:, q, :], scl2[:, q:q + 1], MAGIC, ALU.mult, ALU.add)
                    r.then_inc(r_step, 1)
                    dve.wait_ge(r_step, at(4))
                    nc.vector.tensor_scalar(ha[:, :], ha[:, :], MAGIC - 128, MAGIC + 127, ALU.max, ALU.min).then_inc(r_step, 1)
                    dve.wait_ge(r_step, at(5))
                    nc.vector.tensor_scalar(hi[:, b, :], ha[:, :], MAGIC, None, ALU.subtract).then_inc(s[kind], 1)
                elif kind == "add":
                    done(dve, s["down"], t)
                    free1(dve, s["add"], t)
                    for q in range(QT):
                        r = nc.vector.tensor_scalar(ha2[:, q, :], ps_y[:, q * D:(q + 1) * D], inv2[:, b, q:q + 1], wmean[:, 1:2], ALU.mult, ALU.mult)
                    r.then_inc(a_step, 1)
                    dve.wait_ge(a_step, t + 1)
                    nc.vector.tensor_tensor(g.xb3[:, t, :, :], ha2[:, :, :], g.xb3[:, t, :, :], ALU.add).then_inc(s[kind], 1)

            flow.run(dve, emit)


def expert_ffn(nc, g, name, w, NF, FE, shared, routing):
    NC = NF // P
    NR = w["wr"].shape[1]
    NE = 32 if shared else 8
    NX = NE + shared
    BLK = 512
    NBLK = B * S // BLK
    with ExitStack() as c:
        sem = semaphores(nc, c, name)
        sb = lambda n, s, d=F32: c.enter_context(nc.sbuf_tensor(f"{name}_{n}", s, d))
        pb = lambda n, s, d=F32: c.enter_context(nc.psum_tensor(f"{name}_{n}", s, d))
        wg, wu, wd = sb("wg", [P, NC, P]), sb("wu", [P, NC, P]), sb("wd", [P, NC, D])
        sel = sb("sel", [NX, NC, P])
        combT = sb("combT", [NX, NBLK, BLK])
        loaded = sem("loaded")
        with ExitStack() as c1:
            sb1 = lambda n, s, d=F32: c1.enter_context(nc.sbuf_tensor(f"{name}_{n}", s, d))
            pb1 = lambda n, s, d=F32: c1.enter_context(nc.psum_tensor(f"{name}_{n}", s, d))
            wr = sb1("wr", [P, NR])
            lT = sb1("lT", [NR, NBLK, BLK])
            lg, sg, comb = sb1("lg", [P, NT, NR]), sb1("sg", [P, NT, NR]), sb1("comb", [P, NT, NX])
            ps_l, ps_k = [pb1(f"ps_l{k}", [P, 512]) for k in range(4)], pb1("ps_k", [P, 512])
            arrived, mm, out, turned, sig = sem("arrived"), sem("mm"), sem("out"), sem("turned"), sem("sig")
            routed, back, st = sem("routed"), sem("back"), sem("route_step")
            extra = routing.tiles(sb1)
            block = c1.enter_context(nc.Block())

            @block.sync
            def _(sp):
                sp.dma_start(wr[:, :], w["wr"]).then_inc(arrived, 16)
                for dst, src in routing.loads(extra, w):
                    sp.dma_start(dst, src).then_inc(arrived, 16)
                for dst, src in ((wg, w["wg"]), (wu, w["wu"]), (wd, w["wd"]), (sel, w["sel"])):
                    sp.dma_start(dst[:, :, :], src).then_inc(loaded, 16)

            @block.tensor
            def _(pe):
                pe.wait_ge(arrived, 16 * (1 + len(routing.loads(extra, w))))
                for k in range(NBLK):
                    nc.tensor.matmul(ps_l[k][0:NR, :], wr[:, :], g.xnT[:, 2 * k:2 * k + 2, :], start=True, stop=True).then_inc(mm, 1)
                pe.wait_ge(out, NBLK)
                for t in range(NT):
                    r = nc.tensor.transpose(ps_k[:, t * NR:(t + 1) * NR], lT[:, t // 4, t % 4 * P:(t % 4 + 1) * P], g.ident[0:NR, 0:NR])
                r.then_inc(turned, 1)
                pe.wait_ge(routed, 1)
                for t in range(NT):
                    r = nc.tensor.transpose(ps_l[t // 4][0:NX, t % 4 * P:(t % 4 + 1) * P], comb[:, t, :], g.ident[:, :])
                    if t % 4 == 3:
                        r.then_inc(back, 1)

            @block.scalar
            def _(act):
                for k in range(NBLK):
                    act.wait_ge(mm, k + 1)
                    nc.scalar.activation(lT[:, k, :], ps_l[k][0:NR, :], ACT.Copy).then_inc(out, 1)
                act.wait_ge(turned, 1)
                nc.scalar.activation(sg[:, :, :], ps_k[:, 0:NT * NR].rearrange("p (t n) -> p t n", n=NR), ACT.Sigmoid).then_inc(sig, 1)
                for k in range(NBLK):
                    act.wait_ge(back, k + 1)
                    nc.scalar.activation(combT[:, k, :], ps_l[k][0:NX, :], ACT.Copy).then_inc(out, 1)

            @block.vector
            def _(dve):
                count = [0]

                def step(r):
                    r.then_inc(st, 1)
                    count[0] += 1
                    dve.wait_ge(st, count[0])

                dve.wait_ge(sig, 1)
                dve.wait_ge(arrived, 16 * (1 + len(routing.loads(extra, w))))
                routing.route(nc, step, sg, comb, extra)
                nc.vector.tensor_copy(extra["done"][:, 0:1], comb[:, 0, 0:1]).then_inc(routed, 1)

        with ExitStack() as c1:
            sb1 = lambda n, s, d=F32: c1.enter_context(nc.sbuf_tensor(f"{name}b_{n}", s, d))
            pb1 = lambda n, s, d=F32: c1.enter_context(nc.psum_tensor(f"{name}b_{n}", s, d))
            HB = 4
            sg, su, h = sb1("sg", [P, 2, BLK]), sb1("su", [P, 2, BLK]), sb1("h", [P, HB, BLK])
            oT = sb1("oT", [P, BLK])
            ps_g, ps_u, ps_c = ([pb1(f"ps_{n}{k}", [P, BLK]) for k in range(2)] for n in "guc")
            ps_o, ps_x = pb1("ps_o", [P, BLK]), pb1("ps_x", [P, BLK])
            ins, silu, su_done, hid, down = sem("b_ins"), sem("b_silu"), sem("b_su"), sem("b_hidden"), sem("b_down")
            o_out, o_turned, added = sem("b_o_out"), sem("b_o_turned"), sem("b_added")
            block = c1.enter_context(nc.Block())

            @block.tensor
            def _(pe):
                pe.sem_inc(down, HB)
                pe.wait_ge(loaded, 64)

                with pe.Fori(0, NBLK // 2) as i:
                    def front(m):
                        j, cc = divmod(m, NC)
                        x = g.xnTb[:, i * 2 + j, :]
                        pe.wait_ge(hid, i * (2 * NC) + (m + 1))
                        nc.tensor.matmul(ps_g[m % 2][:, :], wg[:, cc, :], x, start=True, stop=True)
                        nc.tensor.matmul(ps_u[m % 2][:, :], wu[:, cc, :], x, start=True, stop=True)
                        nc.tensor.matmul(ps_c[m % 2][:, :], sel[:, cc, :], combT[:, i * 2 + j, :], start=True, stop=True).then_inc(ins, 1)

                    front(0)
                    for m in range(2 * NC):
                        j, cc = divmod(m, NC)
                        if m + 1 < 2 * NC:
                            front(m + 1)
                        pe.wait_ge(hid, i * (2 * NC) + (m + 3))
                        if cc == 0:
                            pe.wait_ge(o_out, i * 2 + (j + 1))
                        nc.tensor.matmul(ps_o[:, :], wd[:, cc, :], h[:, m % HB, :], start=cc == 0, stop=cc == NC - 1).then_inc(down, 1)
                        if cc == NC - 1:
                            pe.wait_ge(o_out, i * 2 + (j + 2))
                            pe.wait_ge(added, i * 2 + (j + 1))
                            for q in range(BLK // P):
                                r = nc.tensor.transpose(ps_x[:, q * P:(q + 1) * P], oT[:, q * P:(q + 1) * P], g.ident[:, :])
                            r.then_inc(o_turned, 1)

            @block.scalar
            def _(act):
                act.sem_inc(o_out, 1)
                with act.Fori(0, NBLK // 2) as i:
                    for m in range(2 * NC):
                        act.wait_ge(ins, i * (2 * NC) + (m + 1))
                        act.wait_ge(su_done, i * (2 * NC) + (m + 1))
                        nc.scalar.activation(sg[:, m % 2, :], ps_g[m % 2][:, :], ACT.Silu).then_inc(silu, 1)
                        if m % NC == NC - 1:
                            j = m // NC
                            act.wait_ge(down, i * (2 * NC) + (m + 1 + HB))
                            nc.scalar.activation(oT[:, :], ps_o[:, :], ACT.Copy).then_inc(o_out, 1)

            @block.vector
            def _(dve):
                dve.sem_inc(hid, 2)
                dve.sem_inc(su_done, 2)
                dve.sem_inc(added, 1)
                with dve.Fori(0, NBLK // 2) as i:
                    for m in range(2 * NC):
                        dve.wait_ge(silu, i * (2 * NC) + (m + 1))
                        nc.vector.tensor_tensor(su[:, m % 2, :], sg[:, m % 2, :], ps_u[m % 2][:, :], ALU.mult).then_inc(su_done, 1)
                        dve.wait_ge(su_done, i * (2 * NC) + (m + 3))
                        dve.wait_ge(down, i * (2 * NC) + (m + 1))
                        nc.vector.tensor_tensor(h[:, m % HB, :], su[:, m % 2, :], ps_c[m % 2][:, :], ALU.mult).then_inc(hid, 1)
                        if m % NC == NC - 1:
                            j = m // NC
                            dve.wait_ge(o_turned, i * 2 + (j + 1))
                            xb = g.xb4[:, i * 2 + j, :]
                            nc.vector.tensor_tensor(xb, ps_x[:, :], xb, ALU.add).then_inc(added, 1)


class PairedRouting:

    G, EPS = 4, 1e-9

    @staticmethod
    def tiles(sb):
        return dict(top=sb("r_top", [P, NT]), eq=sb("r_eq", [P, NT, 4]), den=sb("r_den", [P, NT]), inv=sb("r_inv", [P, NT]),
                    us=sb("r_us", [P, NT, 4]), ui=sb("r_ui", [P, NT, 4]), order=sb("r_order", [P, 4]), done=sb("r_done", [P, 1]))

    @staticmethod
    def loads(x, w):
        return [(x["order"][:, :], w["order"])]

    @staticmethod
    def route(nc, step, sg, comb, x):
        G = PairedRouting.G
        v, T = nc.vector, [P, NT, G]
        macro, micro = sg[:, :, 0:G], sg[:, :, G:3 * G].rearrange("p t (g e) -> p t g e", e=2)
        step(v.tensor_reduce(x["top"][:, :], macro, AX.X, ALU.max))
        step(v.tensor_tensor(x["eq"][:, :, :], macro, x["top"][:, :, None].broadcast_to(T), ALU.is_equal))
        step(v.tensor_tensor(x["eq"][:, :, :], x["eq"][:, :, :], x["order"][:, None, :].broadcast_to(T), ALU.mult))
        step(v.tensor_reduce(x["inv"][:, :], x["eq"][:, :, :], AX.X, ALU.max))
        step(v.tensor_tensor(x["eq"][:, :, :], x["eq"][:, :, :], x["inv"][:, :, None].broadcast_to(T), ALU.is_equal))
        step(v.tensor_scalar(x["den"][:, :], x["top"][:, :], PairedRouting.EPS, None, ALU.add))
        step(v.reciprocal(x["inv"][:, :], x["den"][:, :]))
        step(v.tensor_tensor(x["top"][:, :], x["top"][:, :], x["inv"][:, :], ALU.mult))
        step(v.tensor_tensor(x["eq"][:, :, :], x["eq"][:, :, :], x["top"][:, :, None].broadcast_to(T), ALU.mult))
        step(v.tensor_tensor(x["us"][:, :, :], micro[:, :, :, 0], micro[:, :, :, 1], ALU.add))
        step(v.tensor_scalar(x["us"][:, :, :], x["us"][:, :, :], PairedRouting.EPS, None, ALU.add))
        step(v.reciprocal(x["ui"][:, :, :], x["us"][:, :, :]))
        step(v.tensor_tensor(x["ui"][:, :, :], x["ui"][:, :, :], x["eq"][:, :, :], ALU.mult))
        for e in range(2):
            step(v.tensor_tensor(comb[:, :, :].rearrange("p t (g e) -> p t g e", e=2)[:, :, :, e], micro[:, :, :, e], x["ui"][:, :, :], ALU.mult))


class GroupedRouting:

    G, PER, TOPG, SCALE, TAKEN = 8, 4, 4, 2.5, -3.0e38

    @staticmethod
    def tiles(sb):
        E = 32
        return dict(bias=sb("r_bias", [P, E]), sc=sb("r_sc", [P, NT, E]), hi=sb("r_hi", [P, NT, 8, 2]), lo=sb("r_lo", [P, NT, 8, 2]),
                    a=sb("r_a", [P, NT, 8]), b=sb("r_b", [P, NT, 8]), gs=sb("r_gs", [P, NT, 8]),
                    gt=sb("r_gt", [P, NT, 8, 8]), eq=sb("r_eq", [P, NT, 8, 8]), before=sb("r_before", [P, 8, 8]),
                    m8=sb("r_m8", [P, NT, 8]), left=sb("r_left", [P, NT, E]), w=sb("r_w", [P, NT, E]), sum=sb("r_sum", [P, NT]),
                    inv=sb("r_inv", [P, NT]), done=sb("r_done", [P, 1]))

    @staticmethod
    def loads(x, w):
        return [(x["bias"][:, :], w["bias"]), (x["before"][:, :, :], w["before"])]

    @staticmethod
    def route(nc, step, sg, comb, x):
        R, v, E = GroupedRouting, nc.vector, 32
        step(v.tensor_tensor(x["sc"][:, :, :], sg[:, :, :], x["bias"][:, None, :].broadcast_to([P, NT, E]), ALU.add))
        sc = x["sc"][:, :, :].rearrange("p t (g k two) -> p (t g) k two", g=R.G, two=2)
        hi, lo = (x[n][:, :, :, :].rearrange("p t g k -> p (t g) k") for n in ("hi", "lo"))
        step(v.tensor_tensor(hi, sc[:, :, :, 0], sc[:, :, :, 1], ALU.max))
        step(v.tensor_tensor(lo, sc[:, :, :, 0], sc[:, :, :, 1], ALU.min))
        a, b, gs = (x[n][:, :, :].rearrange("p t g -> p (t g)") for n in ("a", "b", "gs"))
        step(v.tensor_tensor(a, hi[:, :, 0], hi[:, :, 1], ALU.min))
        step(v.tensor_tensor(b, lo[:, :, 0], lo[:, :, 1], ALU.max))
        step(v.tensor_tensor(b, a, b, ALU.max))
        step(v.tensor_tensor(a, hi[:, :, 0], hi[:, :, 1], ALU.max))
        step(v.tensor_tensor(gs, a, b, ALU.add))
        mine = x["gs"][:, :, :, None].broadcast_to([P, NT, 8, 8])
        other = x["gs"][:, :, None, :].broadcast_to([P, NT, 8, 8])
        step(v.tensor_tensor(x["gt"][:, :, :, :], other, mine, ALU.is_gt))
        step(v.tensor_tensor(x["eq"][:, :, :, :], other, mine, ALU.is_equal))
        step(v.tensor_tensor(x["eq"][:, :, :, :], x["eq"][:, :, :, :], x["before"][:, None, :, :].broadcast_to([P, NT, 8, 8]), ALU.mult))
        step(v.tensor_tensor(x["gt"][:, :, :, :], x["gt"][:, :, :, :], x["eq"][:, :, :, :], ALU.add))
        step(v.tensor_reduce(x["a"][:, :, :], x["gt"][:, :, :, :], AX.X, ALU.add))
        step(v.tensor_scalar(x["b"][:, :, :], x["a"][:, :, :], float(R.TOPG) - 0.5, None, ALU.is_lt))
        step(v.tensor_tensor(x["sc"][:, :, :].rearrange("p t (g k) -> p (t g) k", k=R.PER), x["sc"][:, :, :].rearrange("p t (g k) -> p (t g) k", k=R.PER),
                             b[:, :, None].broadcast_to([P, NT * 8, R.PER]), ALU.mult))
        for t in range(NT):
            r = v.max(x["m8"][:, t, :], x["sc"][:, t, :])
        step(r)
        for t in range(NT):
            r = v.match_replace(x["left"][:, t, :], x["m8"][:, t, :], x["sc"][:, t, :], R.TAKEN)
        step(r)
        step(v.tensor_scalar(x["left"][:, :, :], x["left"][:, :, :], R.TAKEN / 2, None, ALU.is_lt))
        step(v.tensor_tensor(x["w"][:, :, :], x["left"][:, :, :], sg[:, :, :], ALU.mult))
        step(v.tensor_reduce(x["sum"][:, :], x["w"][:, :, :], AX.X, ALU.add))
        step(v.tensor_scalar(x["sum"][:, :], x["sum"][:, :], 1e-20, 1.0 / R.SCALE, ALU.add, ALU.mult))
        step(v.reciprocal(x["inv"][:, :], x["sum"][:, :]))
        step(v.tensor_tensor(comb[:, :, 0:E], x["w"][:, :, :], x["inv"][:, :, None].broadcast_to([P, NT, E]), ALU.mult))
        step(v.memset(comb[:, :, E:E + 1], 1.0))


ONLY = None


class Resident:
    pass


def network(nc, a, out, stop=99):
    with ExitStack() as c:
        sb = lambda n, s, d=F32: c.enter_context(nc.sbuf_tensor(n, s, d))
        g = Resident()
        g.x = sb("x_sb", [P, NT, D])
        g.x4 = g.x[:, :, :].rearrange("p (i k) d -> p i k d", k=4)
        g.xb = g.x[:, :, :].rearrange("p (b q) d -> p b (q d)", q=QT)
        g.xnT = sb("xnT", [P, B, S])
        g.xnT4 = g.xnT[:, :, :].rearrange("p (i k) s -> p i (k s)", k=2)
        g.mv = sb("mv", [P, NT, 2])
        g.mean4 = g.mv[:, :, 0].rearrange("p (i k) -> p i k", k=4)
        g.std, g.rstd = sb("std", [P, NT]), sb("rstd", [P, NT])
        g.rstd4 = g.rstd[:, :].rearrange("p (i k) -> p i k", k=4)
        g.ident, g.sel, g.ones = sb("ident", [P, P]), sb("sel", [P, P]), sb("ones", [P, P])
        g.cols = sb("cols", [P, 8])
        g.blocks32 = sb("blocks32", [P, 4])
        g.blocks = sb("blocks", [P, 4], F16)
        g.xt = g.x[:, :, :].rearrange("p (b q) d -> p q b d", q=QT)
        g.xb3 = g.x[:, :, :].rearrange("p (b q) d -> p b q d", q=QT)
        g.xb4 = g.x[:, :, :].rearrange("p (j k) d -> p j (k d)", k=4)
        g.xnTb = g.xnT4
        g.meant = g.mv[:, :, 0].rearrange("p (b q) -> p q b", q=QT)
        g.rstdt = g.rstd[:, :].rearrange("p (b q) -> p q b", q=QT)
        g.rms, g.rrms = sb("rms", [P, NT]), sb("rrms", [P, NT])
        g.ones2 = sb("ones2", [1, S])
        g.ident16 = sb("ident16", [P, P], F16)
        g.ctx_a = nc.dram_tensor("ctx_a", (P, B, LK), F16, kind="Internal").ap()
        g.ctx_b = nc.dram_tensor("ctx_b", (CB, B, LK), F16, kind="Internal").ap()
        g.ctxT_dram, g.ctxV_dram = a["ctxT"], a["ctxV"]
        arrived, made, copied = (c.enter_context(nc.semaphore(n)) for n in ("arrived", "made", "copied"))
        with nc.Block() as block:
            @block.sync
            def _(sp):
                sp.dma_start(g.x[:, :, :], a["x"]).then_inc(arrived, 16)
                sp.dma_start(g.ident[:, :], a["ident"]).then_inc(arrived, 16)
                sp.dma_start(g.sel[:, :], a["sel"]).then_inc(arrived, 16)
                sp.dma_start(g.cols[:, :], a["cols"]).then_inc(arrived, 16)
                sp.dma_start(g.blocks32[:, :], a["blocks"]).then_inc(arrived, 16)
                sp.wait_ge(arrived, 80)

            @block.vector
            def _(dve):
                nc.vector.memset(g.ones2[:, :], 1.0)
                nc.vector.memset(g.ones[:, :], 1.0).then_inc(made, 1)
                dve.wait_ge(arrived, 80)
                nc.vector.tensor_copy(g.blocks[:, :], g.blocks32[:, :]).then_inc(made, 1)
                nc.vector.tensor_copy(g.ident16[:, :], g.ident[:, :]).then_inc(made, 1)
                dve.wait_ge(made, 3)
        split_context(nc, g, "c")
        phases = [
            lambda: (layer_norm(nc, g, "n0"), small_attention(nc, g, "a0", a["a0"], 8 ** -0.5, True)),
            lambda: (moments(nc, g, "n1", rms=True), head_mix_ffn(nc, g, "f0", a["f0"])),
            lambda: (layer_norm(nc, g, "n2"), wide_attention(nc, g, "a1", a["a1"], 16, 2, 64, 64 ** -0.5, 2, True, False)),
            lambda: (moments(nc, g, "n3"), conv_ffn(nc, g, "f1", a["f1"])),
            lambda: (layer_norm(nc, g, "n4"), wide_attention(nc, g, "a2", a["a2"], 1, 1, 128, 1.0, 4, False, True)),
            lambda: (layer_norm(nc, g, "n5"), expert_ffn(nc, g, "f2", a["f2"], 2048, 256, False, PairedRouting)),
            lambda: (layer_norm(nc, g, "n6"), small_attention(nc, g, "a3", a["a3"], 8 ** -0.5, False)),
            lambda: (layer_norm(nc, g, "n7"), expert_ffn(nc, g, "f3", a["f3"], 2176, 64, True, GroupedRouting)),
        ]
        if ONLY is not None:
            phases = [phases[k] for k in ONLY]
        for p in phases[:stop]:
            p()
        with nc.Block() as block:
            @block.sync
            def _(sp):
                sp.dma_start(out, g.x[:, :, :]).then_inc(copied, 16)
                sp.wait_ge(copied, 16)


def laid_out(inputs):
    import numpy as np
    f = {k: np.asarray(v) for k, v in inputs.items()}
    a = {}
    a["x"] = f["x"].reshape(NT, P, D).transpose(1, 0, 2)
    ctx = f["ctx_512"]
    a["ctxT"] = ctx.transpose(2, 0, 1)
    ctxv = np.zeros((B, KT * P, DC), np.float32)
    ctxv[:, :LK] = ctx
    a["ctxV"] = ctxv.reshape(B, KT, P, DC).transpose(2, 0, 1, 3)
    a["ident"] = np.eye(P, dtype=np.float32)
    part = np.arange(P)
    a["sel"] = (part[:, None] == part[None, :] // 32 * 32 + 8).astype(np.float32)
    cols = np.zeros((P, 8), np.float32)
    cols[:, 0] = LN_EPS
    cols[:, 1] = np.where(part % 32 == 24, 1.0, 8 ** -0.5)
    cols[:, 2] = np.where(part % 32 // 8 == 1, -1.0, 0.0)
    cols[:, 3] = np.where(part % 32 // 8 == 2, -1.0, 0.0)
    cols[:, 4] = np.where(part < DC, 0.0, -1.0)
    cols[:, 5] = np.where(part < DC, -1.0, 0.0)
    cols[:, 6] = 1e-6
    cols[:, 7] = np.where(part == DC, 0.0, -1.0)
    a["cols"] = cols
    a["blocks"] = (part[:, None] // 32 == np.arange(4)[None, :]).astype(np.float32)

    def small(name, Wq, bq, Wk, bk, Wv, bv, Wo, bo):
        wq = np.zeros((P, 16, 32), np.float32)
        wk = np.zeros((CB, 16, 32), np.float32)
        wv = np.zeros((CB, 16, 32), np.float32)
        b = np.zeros((4, 32, 4), np.float32)
        for r in range(3):
            wq[:, :, 8 * r:8 * r + 8] = Wq.reshape(D, 16, 8)
            wk[:DC, :, 8 * r:8 * r + 8] = Wk.reshape(DC, 16, 8)
            if bk is not None:
                wk[DC:, :, 8 * r:8 * r + 8] = bk.reshape(16, 8)
                b[:, 8 * r:8 * r + 8, :] = bq.reshape(4, 4, 8).transpose(1, 2, 0)
        wk[DC:, :, 24] = 1
        wv[:DC, :, 0:8] = Wv.reshape(DC, 16, 8)
        if bv is not None:
            wv[DC:, :, 0:8] = bv.reshape(16, 8)
        wv[DC:, :, 8] = 1
        twice = lambda m: np.concatenate([m[:DC], m[:DC]])
        for n, v, s in (("wq", wq, (P, 4, P)), ("wk_a", twice(wk), (P, 4, P)), ("wk_b", wk, (CB, 4, P)),
                        ("wv_a", twice(wv), (P, 4, P)), ("wv_b", wv, (CB, 4, P)), ("wo", Wo, (P, D)),
                        ("bq", b, (P, 4)), ("bo", bo if bo is not None else np.zeros(D, np.float32), (1, D))):
            a[f"{name}.{n}"] = v.reshape(s)

    small("a0", *(f[f"L0_xattn_{n}"] for n in ("Wq", "bq", "Wk", "bk", "Wv", "bv", "Wo", "bo")))
    Wkv = f["L3_xattn_Wkv"]
    small("a3", f["L3_xattn_Wq"].T, None, Wkv[:D].T, None, Wkv[D:].T, None, f["L3_xattn_Wo"].T, None)
    heads = lambda m: m.reshape(m.shape[0], 16, 64).transpose(2, 1, 0)
    a["a1.wq"], a["a1.wk"], a["a1.wv"] = (heads(f["L1_xattn_" + n]) for n in ("Wq", "Wk", "Wv"))
    a["a1.wo"] = f["L1_xattn_Wo"].reshape(16, 64, D).transpose(1, 0, 2)
    a["a1.bo"] = f["L1_xattn_bo"][None]
    a["a2.wq"], a["a2.wk"] = f["L2_xattn_Wq"].T[:, None], f["L2_xattn_Wk"].T[:, None]
    a["a2.wv"] = f["L2_xattn_Wv"][:, None]
    a["a2.bq"], a["a2.bo"] = f["L2_xattn_bq"][:, None], f["L2_xattn_bv"][None]
    h = {k[7:]: v for k, v in f.items() if k.startswith("L0_ffn_")}
    a["f0.wq"], a["f0.wdT"], a["f0.wup"], a["f0.wo"] = h["Wq"], h["Wdown"].T, h["Wup"], h["Wo"]
    a["f0.bdown"], a["f0.bo"] = h["bdown"][:, None], h["bo"][None]
    a["f0.brow"] = np.concatenate([h["bq"], h["bup"]])[None]
    a["f0.gamma1"], a["f0.gamma2"] = h["gamma1"][:, None], h["gamma2"][:, None]
    a["f0.wg"], a["f0.bg"] = h["Wg"], np.broadcast_to(h["bg"], (P, 8))
    a["f0.we"] = h["We"].transpose(1, 0, 2).reshape(D, 8 * D)
    h = {k[7:]: v for k, v in f.items() if k.startswith("L1_ffn_")}
    a["f1.w1"] = h["w1"].T
    a["f1.w2"] = h["w2"].T.reshape(4, P, D).transpose(1, 0, 2).reshape(P, 512)
    a["f1.convw"] = h["conv_w"].reshape(4, P, 3).transpose(1, 0, 2)
    a["f1.convb"] = h["conv_b"].reshape(4, P).T
    h = {k[7:]: v for k, v in f.items() if k.startswith("L2_ffn_")}
    a["f2.wr"] = np.concatenate([h["macro_w"], h["micro_w"].transpose(1, 0, 2).reshape(D, 8)], 1)
    a["f2.wg"], a["f2.wu"] = (h[n].transpose(1, 0, 2).reshape(D, 16, P) for n in ("gate_w", "up_w"))
    a["f2.wd"] = h["down_w"].reshape(16, P, D).transpose(1, 0, 2)
    a["f2.sel"] = (np.arange(8)[:, None] == np.arange(2048)[None] // 256).astype(np.float32).reshape(8, 16, P)
    a["f2.order"] = np.broadcast_to(np.arange(4, 0, -1, dtype=np.float32), (P, 4))
    h = {k[7:]: v for k, v in f.items() if k.startswith("L3_ffn_")}
    a["f3.wr"] = h["gate_w"].T
    a["f3.wg"], a["f3.wu"] = (np.concatenate([h[n].reshape(2048, D), h[m]]).T.reshape(D, 17, P)
                              for n, m in (("w_gate", "sh_gate"), ("w_up", "sh_up")))
    a["f3.wd"] = np.concatenate([h["w_down"].transpose(0, 2, 1).reshape(2048, D), h["sh_down"].T]).reshape(17, P, D).transpose(1, 0, 2)
    a["f3.sel"] = (np.arange(33)[:, None] == np.minimum(np.arange(2176)[None] // 64, 32)).astype(np.float32).reshape(33, 17, P)
    a["f3.bias"] = np.broadcast_to(h["gate_bias"], (P, 32))
    a["f3.before"] = np.broadcast_to(np.tril(np.ones((8, 8), np.float32), -1), (P, 8, 8))
    return a


def kernel(**inputs):
    import numpy as np
    import concourse.bacc as bacc
    from concourse.bass_utils import run_bass_kernel_spmd

    nc = bacc.Bacc("TRN2", target_bir_lowering=False, num_devices=1)
    arrays, a = {}, {}
    for name, v in laid_out(inputs).items():
        v = np.ascontiguousarray(v)
        arrays["in_" + name.replace(".", "_")] = v
        t = nc.dram_tensor("in_" + name.replace(".", "_"), v.shape, F32, kind="ExternalInput").ap()
        if "." in name:
            a.setdefault(name.split(".")[0], {})[name.split(".")[1]] = t
        else:
            a[name] = t
    out = nc.dram_tensor("out", (P, NT, D), F32, kind="ExternalOutput").ap()
    network(nc, a, out)
    r = run_bass_kernel_spmd(nc, [arrays], core_ids=[0])
    return r.results[0]["out"].transpose(1, 0, 2).reshape(B, S, D)
```

```python
import math
from contextlib import ExitStack

import concourse.bass as bass
from concourse import mybir

F32 = mybir.dt.float32
F16 = mybir.dt.float16
BF16 = mybir.dt.bfloat16
ALU = mybir.AluOpType
ACT = mybir.ActivationFunctionType
AX = mybir.AxisListType

P = 128
B, S, D, DC, LK = 8, 256, 128, 64, 1601
NT = B * S // P
QT = S // P
KT = -(-LK // P)
LAST = LK - (KT - 1) * P
PIECES = [(0, 401), (401, 400), (801, 400), (1201, 400)]
NP_ = len(PIECES)
CB = DC + 2
LN_EPS = 1e-5


def rows(t):
    return P if t < KT - 1 else LAST


class Plan:

    def __init__(self, ahead, body, times, behind, incs, credits):
        self.ahead, self.body, self.times, self.behind, self.incs = ahead, body, times, behind, incs
        count = dict(credits)
        for op in ahead:
            self.number(op, count, None)
        start = dict(count)
        for op in body:
            self.number(op, count, None)
        self.step = {n: count[n] - start[n] for n in count}
        for n in count:
            count[n] = start[n] + times * self.step[n]
        for op in behind:
            self.number(op, count, None)

    def number(self, op, count, _):
        for n, k in self.incs[op["kind"]].items():
            count[n] += k
        op["count"] = dict(count)
        op["by"] = self.incs[op["kind"]]

    def at(self, op, name, i, less=0):
        v = op["count"][name] - less
        return v if i is None else i * self.step[name] + v

    def all(self):
        return ([(op, None) for op in self.ahead] + [(op, i) for i in range(self.times) for op in self.body]
                + [(op, None) for op in self.behind])

    def run(self, engine, emit):
        for op in self.ahead:
            emit(op, None)
        if self.times:
            with engine.Fori(0, self.times) as i:
                for op in self.body:
                    emit(op, i)
        for op in self.behind:
            emit(op, None)


def semaphores(nc, stack, name):
    taken = []

    def clear():
        first = last = None
        for k, handle in enumerate(sorted(taken, key=lambda h: h.num)):
            first = handle.num if k == 0 or handle.num != last + 1 else first
            last = handle.num
            runs[first] = last
        for first, last in runs.items():
            nc.gpsimd.sem_clear(range(first, last + 1))
        nc.all_engine_barrier()

    def sem(n):
        handle = stack.enter_context(nc.semaphore(f"{name}_{n}"))
        taken.append(handle)
        return handle

    runs = {}
    stack.callback(clear)
    return sem


class ContextSplit:

    def __init__(self, nc, g, stack, sem, name):
        sb = lambda n, s, d: stack.enter_context(nc.sbuf_tensor(f"{name}_{n}", s, d))
        self.nc, self.g = nc, g
        self.stage = sb("stage", [P, B, LK], F32)
        self.cast, self.parts, self.ones = sb("cast", [P, B, LK], F16), sb("parts", [P, B, LK], F16), sb("one", [CB - DC, LK], F16)
        self.landed, self.stored = [sem(f"landed{b}") for b in range(B)], sem("stored")
        self.cast_done, self.split_done, self.ones_done = sem("cast"), sem("split"), sem("ones")

    def load(self, sp):
        for b in range(B):
            sp.dma_start(self.stage[0:DC, b, :], self.g.ctxT_dram[:, b, :]).then_inc(self.landed[b], 16)
            sp.dma_start(self.stage[DC:P, b, :], self.g.ctxT_dram[:, b, :]).then_inc(self.landed[b], 16)

    def casts(self, act):
        for b in range(B):
            act.wait_ge(self.landed[b], 32)
            self.nc.scalar.activation(self.cast[:, b, :], self.stage[:, b, :], ACT.Copy).then_inc(self.cast_done, 1)

    def splits(self, dve):
        self.nc.vector.memset(self.ones[:, :], 1.0).then_inc(self.ones_done, 1)
        for b in range(B):
            dve.wait_ge(self.cast_done, b + 1)
            self.nc.vector.scalar_tensor_tensor(self.parts[:, b, :], self.cast[:, b, :], self.g.cols[:, 4:5], self.stage[:, b, :],
                                                ALU.mult, ALU.add).then_inc(self.split_done, 1)

    def store(self, sp):
        g = self.g
        sp.wait_ge(self.ones_done, 1)
        sp.dma_start(g.ctx_b[DC:CB, :, :], self.ones[:, None, :].broadcast_to([CB - DC, B, LK])).then_inc(self.stored, 16)
        for b in range(B):
            sp.wait_ge(self.cast_done, b + 1)
            sp.dma_start(g.ctx_b[0:DC, b, :], self.cast[0:DC, b, :]).then_inc(self.stored, 16)
            sp.wait_ge(self.split_done, b + 1)
            sp.dma_start(g.ctx_a[:, b, :], self.parts[:, b, :]).then_inc(self.stored, 16)
        sp.wait_ge(self.stored, 16 * (2 * B + 1))


def layer_norm(nc, g, name, loads=(), loaded=None, context=False):
    with ExitStack() as c:
        sem = semaphores(nc, c, name)
        sb = lambda n, s, d=F32: c.enter_context(nc.sbuf_tensor(f"{name}_{n}", s, d))
        stats = sb("stats", [P, NT, 6])
        xn = sb("xn", [P, 2, 4, D])
        ps = [c.enter_context(nc.psum_tensor(f"{name}_ps{k}", [P, 512], F32)) for k in range(2)]
        stats_done, moments_done, std_done = sem("stats_done"), sem("moments_done"), sem("std_done")
        rstd_done, xn_done, turned, xnT_done = sem("rstd_done"), sem("xn_done"), sem("turned"), sem("xnT_done")
        ctx = ContextSplit(nc, g, c, sem, name) if context else None
        block = c.enter_context(nc.Block())

        @block.sync
        def _(sp):
            for dst, src in loads:
                sp.dma_start(dst, src).then_inc(loaded, 16)
            if ctx:
                ctx.load(sp)
                ctx.store(sp)

        @block.vector
        def _(dve):
            for t in range(NT):
                nc.vector.bn_stats(stats[:, t, :], g.x[:, t, :]).then_inc(stats_done, 1)
            for t in range(NT):
                dve.wait_ge(stats_done, t + 1)
                nc.vector.bn_aggr(g.mv[:, t, :], stats[:, t, :]).then_inc(moments_done, 1)
            dve.wait_ge(std_done, 1)
            nc.vector.reciprocal(g.rstd[:, :], g.std[:, :]).then_inc(rstd_done, 1)
            dve.wait_ge(rstd_done, 1)
            with dve.Fori(0, NT // 8) as i:
                for h in range(2):
                    dve.wait_ge(turned, i * 2 + (h + 1))
                    for k in range(4):
                        t = 4 * h + k
                        r = nc.vector.tensor_scalar(xn[:, h, k, :], g.x8[:, i, t, :], g.mean8[:, i, t:t + 1],
                                                    g.rstd8[:, i, t:t + 1], ALU.subtract, ALU.mult)
                    r.then_inc(xn_done, 1)
            if ctx:
                ctx.splits(dve)

        @block.scalar
        def _(act):
            act.wait_ge(moments_done, NT)
            nc.scalar.activation(g.std[:, :], g.mv[:, :, 1], ACT.Sqrt, bias=g.cols[:, 0:1]).then_inc(std_done, 1)
            with act.Fori(0, NT // 8) as i:
                for h in range(2):
                    act.wait_ge(turned, i * 2 + (h + 3))
                    nc.scalar.activation(g.xnT8[:, i, h * 4 * P:(h + 1) * 4 * P], ps[h][:, :], ACT.Copy).then_inc(xnT_done, 1)
            if ctx:
                ctx.casts(act)

        @block.tensor
        def _(pe):
            pe.sem_inc(turned, 2)
            with pe.Fori(0, NT // 8) as i:
                for h in range(2):
                    pe.wait_ge(xn_done, i * 2 + (h + 1))
                    pe.wait_ge(xnT_done, i * 2 + (h + 1))
                    for k in range(4):
                        r = nc.tensor.transpose(ps[h][:, k * P:(k + 1) * P], xn[:, h, k, :], g.ident[:, :])
                    r.then_inc(turned, 1)

        @block.gpsimd
        def _(pool):
            pool.sem_inc(xnT_done, 2)


def small_attention(nc, g, name, w, scale, has_bo, normed=False):
    H, DH, HG, W = 16, 8, 4, 32
    G = H // HG
    MROW, SUM = 24, 8
    with ExitStack() as c:
        sem = semaphores(nc, c, name)
        sb = lambda n, s, d=F32: c.enter_context(nc.sbuf_tensor(f"{name}_{n}", s, d))
        pb = lambda n, s: c.enter_context(nc.psum_tensor(f"{name}_{n}", s, F32))
        wq, wo = sb("wq", [P, G, P]), sb("wo", [P, D])
        wk_a, wk_b, wv_a, wv_b = (sb(n, [r, G, P], F16) for n, r in (("wk_a", P), ("wk_b", CB), ("wv_a", P), ("wv_b", CB)))
        raw_a, raw_b = [sb(f"raw_a{k}", [P, G, P]) for k in range(2)], [sb(f"raw_b{k}", [CB, G, P]) for k in range(2)]
        wcast = sb("wcast", [CB, 2, G, P], F16)
        bq = sb("bq", [P, G])
        bqs, bqn = sb("bqs", [P, G]), sb("bqn", [P, G])
        bo = sb("bo", [1, D])
        ctx_a, ctx_b = sb("ctx_a", [P, LK], F16), sb("ctx_b", [CB, LK], F16)
        k16 = sb("k16", [P, G, LK], F16)
        kf, kneg = sb("kf", [P, 2, 401]), sb("kneg", [P, 2, 401], F16)
        v = sb("v", [P, G, KT, P])
        qf, qneg, q16 = sb("qf", [P, S]), sb("qneg", [P, S], F16), sb("q16", [P, S], F16)
        q_max = sb("q_max", [P, 2, HG, S], F16)
        q_exp = sb("q_exp", [P, 2, HG, S], F16)
        mx = sb("mx", [P, QT, HG, NP_])
        negm = sb("negm", [P, QT, HG, W], F16)
        prob = sb("prob", [P, 4, HG * S])
        acc = sb("acc", [P, G, S])
        rec, on, onT = sb("rec", [P, QT, H]), sb("on", [P, QT, D]), sb("onT", [P, S])
        loaded, ctx_loaded = sem("loaded"), sem("ctx_loaded")
        loads = [(dst[:, :, :], src) for dst, src in ((wq, w["wq"]), (raw_a[0], w["wk_a"]), (raw_b[0], w["wk_b"]),
                                                      (raw_a[1], w["wv_a"]), (raw_b[1], w["wv_b"]))]
        loads += [(dst[:, :], src) for dst, src in ((wo, w["wo"]), (bq, w["bq"]), (bo, w["bo"]))]
        if not normed:
            layer_norm(nc, g, name + "n", loads, loaded)
        ps_s, ps_m = [pb(f"ps_s{i}", [P, 1024]) for i in range(2)], [pb(f"ps_m{i}", [P, 512]) for i in range(2)]
        ps_o, ps_w = pb("ps_o", [P, 512]), pb("ps_w", [P, 512])
        qk, ex, pv, mm, mr, nm = sem("scores"), sem("exped"), sem("pv"), sem("maxmm"), sem("maxed"), sem("negmax")
        mj, mf, kc, qs, qb = sem("side"), sem("side_free"), sem("k_split"), sem("q_split"), sem("q_blocks")
        ac, init, wsplit, rc = sem("acc_out"), sem("init"), sem("wsplit"), sem("recip")
        qc = sem("q_out")

        def step(s, total=None):
            ok = lambda k: total is None or 0 <= s + k < total
            gr = lambda k: (s + k) % G
            db = lambda k: (s + k) // G
            pieces = [(j, q, k) for j in range(HG) for q in range(QT) for k in range(NP_)]
            side = {}
            if ok(1):
                side[1] = dict(kind="Q2", g=gr(1), db=db(1), par=(s + 1) % 2)
            if ok(3):
                side[6] = dict(kind="Q1", g=gr(3), db=db(3), par=(s + 3) % 2)
                for k in range(4):
                    side[2 + k] = dict(kind="K", g=gr(3), db=db(3), piece=k, first=gr(3) == 0 and k == 0)
                    side[7 + k] = dict(kind="V", g=gr(3), db=db(3), quad=k, last=gr(3) == G - 1 and k == 3)
            if gr(0) == 0 and (total is None or s > 0) and s >= G:
                side[0] = dict(kind="T", q=0, db=db(0) - 1)
                side[11] = dict(kind="T", q=1, db=db(0) - 1)
                side[12] = dict(kind="W", db=db(0) - 1)
            ops = []
            for t in range(KT):
                n, t2 = divmod(t + 2, KT)
                m = []
                if ok(2):
                    for k, (j, q, p) in enumerate(pieces[3 * t:3 * t + 3]):
                        m.append(dict(kind="M", g=gr(2), j=j, q=q, piece=p, par=(s + 2) % 2, first=t == 0 and k == 0))
                ops += m[0:1]
                if ok(n):
                    ops.append(dict(kind="S", g=gr(n), t=t2, par=(s + n) % 2))
                ops += m[1:2]
                if ok(0):
                    ops.append(dict(kind="PV", g=gr(0), t=t))
                ops += m[2:3]
                if t == 11 and ok(2):
                    ops.append(dict(kind="MF"))
                if t in side:
                    ops.append(side[t])
                    if side[t]["kind"] in ("K", "Q1", "Q2"):
                        ops.append(dict(side[t], kind=side[t]["kind"] + "D"))
            if ok(0):
                ops.append(dict(kind="N", g=gr(0)))
            if side.get(12, {}).get("kind") == "W":
                ops.append(dict(kind="O", db=db(0) - 1))
            return ops

        total = B * G
        ahead = [o for s in (-3, -2, -1, 0) for o in step(s, total)]
        body = [o for s in range(1, G + 1) for o in step(s)]
        behind = [o for s in range(total - G + 1, total) for o in step(s, total)]
        behind += [dict(kind="T", q=0, db=B - 1), dict(kind="T", q=1, db=B - 1), dict(kind="W", db=B - 1), dict(kind="O", db=B - 1)]
        incs = {"S": dict(qk=1, ex=1), "PV": dict(pv=1), "M": dict(mm=1, mr=1), "MF": dict(nm=1),
                "K": dict(mj=1, mf=1), "KD": dict(kc=1), "V": dict(mj=1, mf=1), "Q1": dict(mj=1, mf=1), "Q2": dict(mj=1, mf=1),
                "Q1D": dict(qs=1, qb=1), "Q2D": dict(qs=1, qb=1), "N": dict(ac=1),
                "T": dict(mj=1, mf=1, rc=1), "W": dict(mj=1, mf=1), "O": dict(mj=1, mf=1)}
        plan = Plan(ahead, body, B - 1, behind, incs,
                    dict(qk=0, ex=2, pv=4, mm=0, mr=2, nm=0, mj=0, mf=1, kc=2, qs=1, qb=0, ac=0, rc=0))
        assert plan.step["ex"] % 4 == 0 and plan.step["mr"] % 2 == 0
        at = plan.at

        def batch(op, i):
            return op["db"] if i is None else i + op["db"]

        last_use = {batch(op, i): at(op, "mf", i) for op, i in plan.all() if op.get("last")}
        block = c.enter_context(nc.Block())

        @block.sync
        def _(sp):
            if normed:
                for dst, src in loads:
                    sp.dma_start(dst, src).then_inc(loaded, 16)
            for b in range(B):
                if b:
                    sp.wait_ge(mf, last_use[b - 1])
                sp.dma_start(ctx_a[:, :], g.ctx_a[:, b, :]).then_inc(ctx_loaded, 16)
                sp.dma_start(ctx_b[:, :], g.ctx_b[:, b, :]).then_inc(ctx_loaded, 16)

        @block.tensor
        def _(pe):
            pe.sem_inc(pv, 4)
            pe.wait_ge(loaded, len(loads) * 16)
            pe.wait_ge(wsplit, 2)

            def emit(op, i):
                k = op["kind"]
                if k == "S":
                    t, n = op["t"], rows(op["t"])
                    if t == 0:
                        pe.wait_ge(qb, at(op, "qb", i))
                    pe.wait_ge(ex, at(op, "ex", i, 2))
                    slot = ps_s[op["count"]["qk"] % 2 ^ 1]
                    for h in range(2):
                        r = nc.tensor.matmul(slot[0:n, h * 512:h * 512 + 512], k16[:, op["g"], t * P:t * P + n],
                                             q_exp[:, op["par"], 2 * h:2 * h + 2, :], start=True, stop=True)
                    r.then_inc(qk, 1)
                elif k == "PV":
                    t, n = op["t"], rows(op["t"])
                    m = op["count"]["pv"] - 5
                    if t == 0 and (i is not None or op["count"]["ac"] > 0):
                        pe.wait_ge(ac, at(op, "ac", i))
                    pe.wait_ge(ex, at(op, "pv", i, 2))
                    for j in range(HG):
                        r = nc.tensor.matmul(ps_o[W * j:W * j + W, 0:S], v[0:n, op["g"], t, W * j:W * j + W],
                                             prob[0:n, m % 4, j * S:(j + 1) * S], start=t == 0, stop=t == KT - 1)
                    r.then_inc(pv, 1)
                elif k == "M":
                    if op["first"]:
                        pe.wait_ge(qb, at(op, "qb", i))
                    pe.wait_ge(mr, at(op, "mr", i, 2))
                    k0, n = PIECES[op["piece"]]
                    q = op["q"]
                    nc.tensor.matmul(ps_m[op["count"]["mm"] % 2 ^ 1][:, 0:n], q_max[:, op["par"], op["j"], q * P:(q + 1) * P],
                                     k16[:, op["g"], k0:k0 + n], start=True, stop=True).then_inc(mm, 1)
                elif k not in ("MF", "N", "KD", "Q1D", "Q2D"):
                    pe.wait_ge(mf, at(op, "mf", i, 1))
                    if k == "K":
                        if op["first"]:
                            b = batch(op, i)
                            pe.wait_ge(ctx_loaded, b * 32 + 32)
                        k0, n = PIECES[op["piece"]]
                        nc.tensor.matmul(ps_w[:, 0:n], wk_a[:, op["g"], :], ctx_a[:, k0:k0 + n], start=True, stop=False)
                        r = nc.tensor.matmul(ps_w[:, 0:n], wk_b[:, op["g"], :], ctx_b[:, k0:k0 + n], start=False, stop=True)
                    elif k == "V":
                        for t in range(4 * op["quad"], min(4 * op["quad"] + 4, KT)):
                            n = rows(t)
                            o = ps_w[0:n, (t % 4) * P:(t % 4) * P + P]
                            nc.tensor.matmul(o, ctx_a[:, t * P:t * P + n], wv_a[:, op["g"], :], start=True, stop=False)
                            r = nc.tensor.matmul(o, ctx_b[:, t * P:t * P + n], wv_b[:, op["g"], :], start=False, stop=True)
                    elif k in ("Q1", "Q2"):
                        r = nc.tensor.matmul(ps_w[:, 0:S], wq[:, op["g"], :], g.xnT[:, batch(op, i), :],
                                             start=True, stop=k == "Q1")
                        if k == "Q2":
                            pe.wait_ge(nm, at(op, "nm", i))
                            for q in range(QT):
                                r = nc.tensor.matmul(ps_w[:, q * P:(q + 1) * P], negm[:, q, :, :].rearrange("p a b -> p (a b)"),
                                                     g.ident16[:, :], start=False, stop=q == QT - 1)
                    elif k == "T":
                        pe.wait_ge(ac, at(op, "ac", i))
                        for gg in range(G):
                            r = nc.tensor.transpose(ps_w[:, gg * P:(gg + 1) * P], acc[:, gg, op["q"] * P:(op["q"] + 1) * P], g.ident[:, :])
                    elif k == "W":
                        for q in range(QT):
                            r = nc.tensor.transpose(ps_w[:, q * P:(q + 1) * P], on[:, q, :], g.ident[:, :])
                    elif k == "O":
                        for q in range(QT):
                            if has_bo:
                                nc.tensor.matmul(ps_w[:, q * D:(q + 1) * D], g.ones[0:1, :], bo[:, :], start=True, stop=False)
                            r = nc.tensor.matmul(ps_w[:, q * D:(q + 1) * D], onT[:, q * P:(q + 1) * P], wo[:, :], start=not has_bo, stop=True)
                    r.then_inc(mj, 1)

            plan.run(pe, emit)

        @block.scalar
        def _(act):
            act.sem_inc(ex, 2)
            act.wait_ge(loaded, len(loads) * 16)
            nc.scalar.activation(bqs[:, :], bq[:, :], ACT.Copy, scale=scale).then_inc(qc, 1)
            act.wait_ge(qc, 1)
            nc.scalar.activation(bqn[:, :], bqs[:, :], ACT.Identity, scale=g.cols[:, 3:4]).then_inc(qc, 1)
            act.wait_ge(qc, 2)

            def emit(op, i):
                k = op["kind"]
                if k == "S":
                    t, n = op["t"], rows(op["t"])
                    act.wait_ge(qk, at(op, "qk", i))
                    act.wait_ge(pv, at(op, "qk", i))
                    nc.scalar.activation(prob[0:n, (op["count"]["qk"] - 1) % 4, :], ps_s[op["count"]["qk"] % 2 ^ 1][0:n, :],
                                         ACT.Exp).then_inc(ex, 1)
                elif k == "K":
                    act.wait_ge(mj, at(op, "mj", i))
                    act.wait_ge(kc, at(op, "kc", i, 1))
                    n, h = PIECES[op["piece"]][1], op["piece"] % 2
                    nc.scalar.activation(kf[:, h, 0:n], ps_w[:, 0:n], ACT.Copy)
                    nc.scalar.activation(kneg[:, h, 0:n], ps_w[:, 0:n], ACT.Identity, scale=g.cols[:, 2:3]).then_inc(mf, 1)
                elif k == "V":
                    act.wait_ge(mj, at(op, "mj", i))
                    if op["quad"] < 3:
                        dst = v[:, op["g"], 4 * op["quad"]:4 * op["quad"] + 4, :].rearrange("p a b -> p (a b)")
                        r = nc.scalar.activation(dst, ps_w[:, :], ACT.Copy)
                    else:
                        r = nc.scalar.activation(v[0:LAST, op["g"], KT - 1, :], ps_w[0:LAST, 0:P], ACT.Copy)
                    r.then_inc(mf, 1)
                elif k in ("Q1", "Q2"):
                    act.wait_ge(mj, at(op, "mj", i))
                    act.wait_ge(qs, at(op, "qs", i))
                    nc.scalar.activation(qf[:, :], ps_w[:, 0:S], ACT.Identity, bias=bqs[:, op["g"]:op["g"] + 1],
                                         scale=g.cols[:, 1:2])
                    nc.scalar.activation(qneg[:, :], ps_w[:, 0:S], ACT.Identity, bias=bqn[:, op["g"]:op["g"] + 1],
                                         scale=g.cols[:, 9:10]).then_inc(mf, 1)
                elif k == "N":
                    act.wait_ge(pv, at(op, "pv", i))
                    act.wait_ge(mj, at(op, "mj", i))
                    nc.scalar.activation(acc[:, op["g"], :], ps_o[:, 0:S], ACT.Copy).then_inc(ac, 1)
                elif k == "W":
                    act.wait_ge(mj, at(op, "mj", i))
                    nc.scalar.activation(onT[:, :], ps_w[:, 0:S], ACT.Copy).then_inc(mf, 1)

            plan.run(act, emit)

        @block.vector
        def _(dve):
            nc.vector.memset(negm[:, :, :, :], 0.0).then_inc(init, 1)
            dve.sem_inc(mr, 2)
            dve.sem_inc(mf, 1)
            dve.sem_inc(qs, 1)
            dve.sem_inc(kc, 2)
            dve.wait_ge(loaded, len(loads) * 16)
            for k, (w_a, w_b) in enumerate(((wk_a, wk_b), (wv_a, wv_b))):
                nc.vector.tensor_copy(w_a[:, :, :], raw_a[k][:, :, :])
                nc.vector.tensor_copy(wcast[:, k, :, :], raw_b[k][:, :, :]).then_inc(init, 1)
            dve.wait_ge(init, 3)
            for k, w_b in enumerate((wk_b, wv_b)):
                nc.vector.scalar_tensor_tensor(w_b[:, :, :], wcast[:, k, :, :], g.cols[0:CB, 7:8], raw_b[k][:, :, :], ALU.mult, ALU.add).then_inc(wsplit, 1)

            def emit(op, i):
                k = op["kind"]
                if k == "M":
                    if op["first"] and (i is not None or op["count"]["nm"] > 0):
                        dve.wait_ge(nm, at(op, "nm", i))
                    dve.wait_ge(mm, at(op, "mm", i))
                    n = PIECES[op["piece"]][1]
                    nc.vector.reduce_max(mx[:, op["q"], op["j"], op["piece"]:op["piece"] + 1],
                                         ps_m[op["count"]["mm"] % 2 ^ 1][:, 0:n], AX.X).then_inc(mr, 1)
                elif k == "MF":
                    dve.wait_ge(mr, at(op, "mr", i))
                    nc.vector.tensor_reduce(negm[:, :, :, MROW], mx[:, :, :, :], AX.X, ALU.max, negate=True).then_inc(nm, 1)
                elif k == "T":
                    dve.wait_ge(mj, at(op, "mj", i))
                    heads = ps_w[:, :].rearrange("p (h r) -> p h r", r=W)
                    nc.vector.reciprocal(rec[:, op["q"], :], heads[:, :, SUM]).then_inc(rc, 1)
                    dve.wait_ge(rc, at(op, "rc", i))
                    nc.vector.tensor_tensor(on[:, op["q"], :].rearrange("p (h d) -> p h d", d=DH), heads[:, :, 0:DH],
                                            rec[:, op["q"], :, None].broadcast_to([P, H, DH]), ALU.mult).then_inc(mf, 1)
                elif k == "O":
                    dve.wait_ge(mj, at(op, "mj", i))
                    xb = g.xb[:, batch(op, i), :]
                    nc.vector.tensor_tensor(xb, ps_w[:, 0:S], xb, ALU.add).then_inc(mf, 1)

            plan.run(dve, emit)

        @block.gpsimd
        def _(pool):
            def emit(op, i):
                k = op["kind"]
                if k == "KD":
                    pool.wait_ge(mf, at(op, "mf", i))
                    (k0, n), h = PIECES[op["piece"]], op["piece"] % 2
                    nc.gpsimd.tensor_tensor(k16[:, op["g"], k0:k0 + n], kf[:, h, 0:n], kneg[:, h, 0:n], ALU.add).then_inc(kc, 1)
                elif k in ("Q1D", "Q2D"):
                    pool.wait_ge(mf, at(op, "mf", i))
                    if op["count"]["qb"] > 1 or i is not None:
                        pool.wait_ge(qb, at(op, "qb", i, 1))
                    nc.gpsimd.tensor_tensor(q16[:, :], qf[:, :], qneg[:, :], ALU.add).then_inc(qs, 1)
                    pool.wait_ge(qs, at(op, "qs", i))
                    dst = (q_max if k == "Q1D" else q_exp)[:, op["par"], :, :]
                    nc.gpsimd.tensor_tensor(dst, q16[:, None, :].broadcast_to([P, HG, S]), g.blocks[:, :, None].broadcast_to([P, HG, S]), ALU.mult).then_inc(qb, 1)

            plan.run(pool, emit)


def wide_attention(nc, g, name, w, H, HG, DH, scale, KB, combined, biased):
    G = H // HG
    C1 = DC + 1
    N = HG * S
    PAIR = 2 // HG
    PB = 8
    POOLED = 9
    SV = KT - POOLED + 1
    total = B * G
    BODY = 2 * G if G > 1 else total
    with ExitStack() as c:
        sem = semaphores(nc, c, name)
        sb = lambda n, s, d=F32: c.enter_context(nc.sbuf_tensor(f"{name}_{n}", s, d))
        pb = lambda n, s: c.enter_context(nc.psum_tensor(f"{name}_{n}", s, F32))
        wq, wk = sb("wq", [DH, H, D]), sb("wk", [DH, H, DC])
        wv = sb("wv", [DH if combined else P, H, DC if combined else D])
        wo = sb("wo", [DH, H, D]) if combined else None
        bq = sb("bq", [DH, 1]) if biased else None
        bo = sb("bo", [1, D])
        wqk = sb("wqk", [P, H, P])
        bqk = sb("bqk", [1, P]) if biased else None
        wvo = sb("wvo", [P, G, D])
        k_a, k_b = sb("k_a", [P, KB, LK], F16), sb("k_b", [C1, KB, LK], F16)
        v = sb("v", [P, KB, KT, DC])
        q_a, q_b = sb("q_a", [P, 4, N], F16), sb("q_b", [C1, 4, N], F16)
        mx, negm = sb("mx", [P, QT, HG, NP_]), sb("negm", [P, QT, HG], F16)
        prob = sb("prob", [P, PB, N])
        sum_p, sum_v = sb("sum_p", [P, 2, N]), sb("sum_v", [P, 2, N])
        acc, rec, on = sb("acc", [P, S]), sb("rec", [P, S]), sb("on", [P, G, S])
        loaded, ctx_in = sem("loaded"), [sem(f"ctx_in{k}") for k in range(KB)]
        loads = [(wq[:, :, :], w["wq"]), (wk[:, :, :], w["wk"]), (bo[:, :], w["bo"])]
        loads += [(wv[:, :, :], w["wv"])] if combined else [(wv[k * DC:(k + 1) * DC, :, :], w["wv"]) for k in range(2)]
        loads += [(wo[:, :, :], w["wo"])] if combined else []
        loads += [(bq[:, :], w["bq"])] if biased else []
        layer_norm(nc, g, name + "n", loads, loaded)
        ps_s, ps_m = [pb(f"ps_s{i}", [P, 512]) for i in range(4)], [pb(f"ps_m{i}", [P, 512]) for i in range(2)]
        ps_o, ps_w = pb("ps_o", [P, 512]), pb("ps_w", [P, 512])
        qk, ex, pv, mm, mr, nm = sem("scores"), sem("exped"), sem("pv"), sem("maxmm"), sem("maxed"), sem("negmax")
        mj, mf, qc = sem("side"), sem("side_free"), sem("q_cast")
        ac, od = sem("acc_out"), sem("normed")
        sp_, sv = sem("sum_pool"), sem("sum_vector")
        folded, fold_out = sem("folded"), sem("fold_out")

        def step(s, total=None):
            ok = lambda k: total is None or 0 <= s + k < total
            f = lambda k: dict(s=s + k, g=(s + k) % G, db=(s + k) // G, kb=(s + k) // G % KB, par=(s + k) % 2, par4=(s + k) % 4)
            pieces = [(j, q, k) for j in range(HG) for q in range(QT) for k in range(NP_)]
            side = {}
            if ok(1):
                side[1] = [dict(kind="Q2", **f(1))]
            if ok(3):
                side[3] = [dict(kind="Q1", **f(3))]
                side[4] = [dict(kind="Q1D", **f(3))]
            if (total is None or s > 0) and ok(-1):
                side[2] = [dict(kind="C", **f(-1))]
                side[8] = [dict(kind="N", **f(-1))]
                side[9] = [dict(kind="ND", **f(-1))]
                if s % G == 0:
                    side[11] = [dict(kind="O", **f(-1))]
                    side[12] = [dict(kind="OD", **f(-1))]
            since = 0 if s < 2 else 1 + ((s - 1) % G == 0)
            ops = []
            for t in range(KT):
                n, t2 = divmod(t + 3, KT)
                m = []
                if ok(2):
                    for k, (j, q, p) in enumerate(pieces[2 * t - 2:2 * t] if t else []):
                        m.append(dict(kind="M", j=j, q=q, piece=p, first=t == 1 and k == 0, since=since, **f(2)))
                ops += m[0:1]
                if ok(n):
                    ops.append(dict(kind="S", t=t2, queries=side[1][0] if n and t2 == 0 else None, **f(n)))
                ops += [o for o in side.get(t, []) if o["kind"] in ("Q1D", "ND", "OD", "C")]
                ops += m[1:2]
                if ok(0) and (PAIR == 1 or t % 2 or t == KT - 1):
                    for u in ([t - 1, t] if PAIR == 2 and t % 2 else [t]):
                        ops.append(dict(kind="PV", t=u, **f(0)))
                if t == 9 and ok(2):
                    ops.append(dict(kind="MF"))
                ops += [o for o in side.get(t, []) if o["kind"] not in ("Q1D", "ND", "OD", "C")]
            if ok(0):
                ops.append(dict(kind="A", **f(0)))
            return ops

        ahead = [o for s in (-3, -2, -1, 0) for o in step(s, total)]
        times = total // BODY - 1
        body = [o for s in range(1, BODY + 1) for o in step(s)] if times else []
        behind = [o for s in range(total - BODY + 1, total) for o in step(s, total)]
        behind += [dict(kind=k, s=total - 1, g=G - 1, db=B - 1, par=(total - 1) % 2) for k in ("C", "N", "ND", "O", "OD")]
        incs = {"S": dict(qk=1, ex=1), "PV": dict(pv=1), "M": dict(mm=1, mr=1), "MF": dict(nm=1),
                "Q1": dict(mj=1, mf=1, qc=1), "Q1D": {}, "Q2": dict(mj=1, mf=1), "A": dict(ac=1),
                "N": dict(mj=1, mf=1), "ND": dict(od=1), "C": {}, "O": dict(mj=1, mf=1), "OD": {}}
        plan = Plan(ahead, body, times, behind, incs,
                    dict(qk=0, ex=4, pv=PB, mm=0, mr=2, nm=0, mj=0, mf=1, qc=0, ac=0, od=1))
        at = plan.at
        if times:
            assert plan.step["ex"] % PB == 0 and plan.step["mr"] % 2 == 0

        def step_of(op, i):
            return op["s"] if i is None else i * BODY + op["s"]

        def batch(op, i):
            return op["db"] if i is None else i * (BODY // G) + op["db"]

        attended = {batch(op, i): at(op, "pv", i) for op, i in plan.all() if op["kind"] == "PV" and op["t"] == KT - 1}
        block = c.enter_context(nc.Block())

        @block.sync
        def _(sp):
            for b in range(B):
                if b >= KB:
                    sp.wait_ge(pv, attended[b - KB])
                sp.dma_start(k_a[:, b % KB, :], g.ctx_a[:, b, :]).then_inc(ctx_in[b % KB], 16)
                sp.dma_start(k_b[:, b % KB, :], g.ctx_b[0:C1, b, :]).then_inc(ctx_in[b % KB], 16)
                sp.dma_start(v[:, b % KB, :, :], g.ctxV_dram[:, b, :, :]).then_inc(ctx_in[b % KB], 16)

        @block.tensor
        def _(pe):
            pe.sem_inc(pv, PB)
            pe.wait_ge(loaded, len(loads) * 16)
            for h in range(H):
                if h >= 4:
                    pe.wait_ge(fold_out, h - 3)
                bank = ps_s[h % 4]
                r = nc.tensor.matmul(bank[:, 0:DC], wq[:, h, :], wk[:, h, :], start=True, stop=True)
                if combined:
                    r = nc.tensor.matmul(bank[0:DC, 256:256 + D], wv[:, h, :], wo[:, h, :], start=True, stop=True)
                r.then_inc(folded, 1)
            if biased:
                nc.tensor.matmul(ps_m[0][0:1, 0:DC], bq[:, :], wk[:, 0, :], start=True, stop=True).then_inc(folded, 1)
            pe.wait_ge(fold_out, H + biased + (not combined))

            def emit(op, i):
                k = op["kind"]
                if k == "S":
                    t, n = op["t"], rows(op["t"])
                    if t == 0:
                        q2 = op["queries"] or op
                        pe.wait_ge(mf, at(q2, "mf", i))
                    pe.wait_ge(ex, at(op, "ex", i, 4))
                    bank = ps_s[(op["count"]["qk"] - 1) % 4]
                    nc.tensor.matmul(bank[0:n, 0:N], k_a[:, op["kb"], t * P:t * P + n], q_a[:, op["par4"], :], start=True, stop=False)
                    nc.tensor.matmul(bank[0:n, 0:N], k_b[:, op["kb"], t * P:t * P + n], q_b[:, op["par4"], :],
                                     start=False, stop=True).then_inc(qk, 1)
                elif k == "PV":
                    t, n = op["t"], rows(op["t"])
                    m = op["count"]["pv"] - PB - 1
                    if t == 0 and (i is not None or op["count"]["ac"] > 0):
                        pe.wait_ge(ac, at(op, "ac", i))
                    pe.wait_ge(ex, at(op, "pv", i, PB - 4))
                    for j in range(HG):
                        r0 = DC * (t % 2 if PAIR == 2 else j)
                        r = nc.tensor.matmul(ps_o[r0:r0 + DC, 0:S], v[0:n, op["kb"], t, :],
                                             prob[0:n, m % PB, j * S:(j + 1) * S], start=t < PAIR, stop=t >= KT - PAIR)
                    r.then_inc(pv, 1)
                elif k == "M":
                    if op["first"]:
                        pe.wait_ge(mf, at(op, "mf", i, op["since"]))
                        if op["g"] == 0:
                            n = op["db"] // KB * 48 + 48
                            pe.wait_ge(ctx_in[op["kb"]], n if i is None else i * (BODY // G // KB * 48) + n)
                    pe.wait_ge(mr, at(op, "mr", i, 2))
                    k0, n = PIECES[op["piece"]]
                    q0 = op["j"] * S + op["q"] * P
                    nc.tensor.matmul(ps_m[(op["count"]["mm"] - 1) % 2][:, 0:n], q_a[:, op["par4"], q0:q0 + P],
                                     k_a[:, op["kb"], k0:k0 + n], start=True, stop=True).then_inc(mm, 1)
                elif k in ("Q1", "Q2", "N", "O"):
                    pe.wait_ge(mf, at(op, "mf", i, 1))
                    if k == "Q1":
                        for j in range(HG):
                            if biased:
                                nc.tensor.matmul(ps_w[:, j * S:(j + 1) * S], bqk[:, :], g.ones2[0:1, :], start=True, stop=False)
                            r = nc.tensor.matmul(ps_w[:, j * S:(j + 1) * S], wqk[:, op["g"] * HG + j, :], g.xnT[:, batch(op, i), :],
                                                 start=not biased, stop=True)
                    elif k == "Q2":
                        pe.wait_ge(nm, at(op, "nm", i))
                        for j in range(HG):
                            for q in range(QT):
                                c0 = j * S + q * P
                                r = nc.tensor.matmul(ps_w[DC:C1, c0:c0 + P], negm[:, q, j:j + 1], g.ident16[:, :], start=True, stop=True)
                    elif k == "N":
                        pe.wait_ge(sv, step_of(op, i) * SV + 2 * SV)
                        rows_ = DC * PAIR
                        for j in range(HG):
                            r = nc.tensor.matmul(ps_w[rows_ * j:rows_ * j + rows_, 0:S], g.ones[:, 0:rows_], sum_v[:, op["par"], j * S:(j + 1) * S],
                                                 start=True, stop=True)
                    elif k == "O":
                        pe.wait_ge(od, at(op, "od", i))
                        for q in range(QT):
                            nc.tensor.matmul(ps_w[:, q * D:(q + 1) * D], g.ones[0:1, :], bo[:, :], start=True, stop=False)
                            for gg in range(G):
                                r = nc.tensor.matmul(ps_w[:, q * D:(q + 1) * D], on[:, gg, q * P:(q + 1) * P], wvo[:, gg, :],
                                                     start=False, stop=gg == G - 1)
                    r.then_inc(mj, 1)

            plan.run(pe, emit)

        @block.scalar
        def _(act):
            act.sem_inc(ex, 4)
            for h in range(H):
                act.wait_ge(folded, h + 1)
                bank = ps_s[h % 4]
                if combined:
                    nc.scalar.activation(wvo[h % HG * DC:h % HG * DC + DC, h // HG, :], bank[0:DC, 256:256 + D], ACT.Copy)
                for k in range(2):
                    r = nc.scalar.activation(wqk[:, h, k * DC:(k + 1) * DC], bank[:, 0:DC], ACT.Copy, scale=scale)
                r.then_inc(fold_out, 1)
            if not combined:
                act.wait_ge(loaded, len(loads) * 16)
                nc.scalar.activation(wvo[:, 0, :], wv[:, 0, :], ACT.Copy).then_inc(fold_out, 1)
            if biased:
                act.wait_ge(folded, H + 1)
                for k in range(2):
                    r = nc.scalar.activation(bqk[:, k * DC:(k + 1) * DC], ps_m[0][0:1, 0:DC], ACT.Copy, scale=scale)
                r.then_inc(fold_out, 1)

            def emit(op, i):
                k = op["kind"]
                if k == "S":
                    t, n = op["t"], rows(op["t"])
                    act.wait_ge(qk, at(op, "qk", i))
                    act.wait_ge(pv, at(op, "qk", i))
                    st = step_of(op, i)
                    if t >= PB:
                        act.wait_ge(sp_, st * POOLED + (POOLED + t - PB + 1))
                    elif t + KT - PB < POOLED:
                        act.wait_ge(sp_, st * POOLED + (t + KT - PB + 1))
                    else:
                        act.wait_ge(sv, st * SV + (t + KT - PB - POOLED + 1))
                    m = op["count"]["qk"] - 1
                    nc.scalar.activation(prob[0:n, m % PB, :], ps_s[m % 4][0:n, 0:N], ACT.Exp).then_inc(ex, 1)
                elif k == "Q1":
                    act.wait_ge(mj, at(op, "mj", i))
                    nc.scalar.activation(q_a[:, op["par4"], :], ps_w[:, 0:N], ACT.Copy).then_inc(qc, 1)
                elif k == "Q2":
                    act.wait_ge(mj, at(op, "mj", i))
                    nc.scalar.activation(q_b[DC:C1, op["par4"], :], ps_w[DC:C1, 0:N], ACT.Copy).then_inc(mf, 1)
                elif k == "A":
                    act.wait_ge(pv, at(op, "pv", i))
                    act.wait_ge(od, at(op, "od", i))
                    nc.scalar.activation(acc[:, :], ps_o[:, 0:S], ACT.Copy).then_inc(ac, 1)

            plan.run(act, emit)

        @block.vector
        def _(dve):
            dve.sem_inc(mr, 2)
            dve.sem_inc(mf, 1)
            dve.sem_inc(od, 1)
            dve.sem_inc(sv, SV)

            def emit(op, i):
                k = op["kind"]
                if k == "PV" and op["t"] > POOLED:
                    t, n = op["t"], rows(op["t"])
                    m = op["count"]["pv"] - PB - 1
                    dve.wait_ge(ex, at(op, "pv", i, PB - 4))
                    dst = sum_v[0:n, op["par"], :]
                    if t == POOLED + 1:
                        nc.vector.tensor_tensor(dst, prob[:, (m - 1) % PB, :], prob[:, m % PB, :], ALU.add).then_inc(sv, 2)
                    else:
                        dve.wait_ge(sv, step_of(op, i) * SV + (t - POOLED + SV))
                        nc.vector.tensor_tensor(dst, dst, prob[0:n, m % PB, :], ALU.add).then_inc(sv, 1)
                elif k == "C":
                    dve.wait_ge(sp_, step_of(op, i) * POOLED + 2 * POOLED)
                    dve.wait_ge(sv, step_of(op, i) * SV + 2 * SV - 1)
                    dst = sum_v[:, op["par"], :]
                    nc.vector.tensor_tensor(dst, dst, sum_p[:, op["par"], :], ALU.add).then_inc(sv, 1)
                elif k == "M":
                    if op["first"] and (i is not None or op["count"]["nm"] > 0):
                        dve.wait_ge(nm, at(op, "nm", i))
                    dve.wait_ge(mm, at(op, "mm", i))
                    n = PIECES[op["piece"]][1]
                    nc.vector.reduce_max(mx[:, op["q"], op["j"], op["piece"]:op["piece"] + 1],
                                         ps_m[(op["count"]["mm"] - 1) % 2][:, 0:n], AX.X).then_inc(mr, 1)
                elif k == "MF":
                    dve.wait_ge(mr, at(op, "mr", i))
                    nc.vector.tensor_reduce(negm[:, :, :], mx[:, :, :, :], AX.X, ALU.max, negate=True).then_inc(nm, 1)
                elif k == "Q1D":
                    dve.wait_ge(qc, at(op, "qc", i))
                    nc.vector.scalar_tensor_tensor(q_b[0:DC, op["par4"], :], q_a[0:DC, op["par4"], :], g.cols[0:DC, 5:6],
                                                   ps_w[0:DC, 0:N], ALU.mult, ALU.add).then_inc(mf, 1)
                elif k == "ND":
                    dve.wait_ge(mj, at(op, "mj", i))
                    nc.vector.reciprocal(rec[:, :], ps_w[:, 0:S]).then_inc(mf, 1)
                    dve.wait_ge(mf, at(op, "mf", i))
                    dve.wait_ge(ac, at(op, "ac", i))
                    nc.vector.tensor_tensor(on[:, op["g"], :], acc[:, :], rec[:, :], ALU.mult).then_inc(od, 1)
                elif k == "OD":
                    dve.wait_ge(mj, at(op, "mj", i))
                    xb = g.xb[:, batch(op, i), :]
                    nc.vector.tensor_tensor(xb, ps_w[:, 0:S], xb, ALU.add).then_inc(mf, 1)

            plan.run(dve, emit)

        @block.gpsimd
        def _(pool):
            pool.sem_inc(sp_, POOLED)

            def emit(op, i):
                if op["kind"] == "PV" and 0 < op["t"] < POOLED:
                    m = op["count"]["pv"] - PB - 1
                    pool.wait_ge(ex, at(op, "pv", i, PB - 4))
                    dst = sum_p[:, op["par"], :]
                    if op["t"] == 1:
                        if op["s"] >= 2 or i is not None:
                            pool.wait_ge(sv, step_of(op, i) * SV)
                        nc.gpsimd.tensor_tensor(dst, prob[:, (m - 1) % PB, :], prob[:, m % PB, :], ALU.add).then_inc(sp_, 2)
                    else:
                        pool.wait_ge(sp_, step_of(op, i) * POOLED + (op["t"] + POOLED))
                        nc.gpsimd.tensor_tensor(dst, dst, prob[:, m % PB, :], ALU.add).then_inc(sp_, 1)

            plan.run(pool, emit)


class Flow:

    def __init__(self, n, nbuf, order):
        self.n, self.nbuf, self.order = n, nbuf, order

    def run(self, engine, emit):
        n, nb = self.n, self.nbuf
        for s in range(nb):
            for kind, off in self.order:
                if 0 <= s - off < n:
                    emit(kind, s - off, (s - off) % nb)
        if n > nb:
            with engine.Fori(0, n // nb - 1) as i:
                for k in range(nb):
                    for kind, off in self.order:
                        emit(kind, i * nb + (nb + k - off), (k - off) % nb)
        for s in range(n, n + nb):
            for kind, off in self.order:
                if s - off < n:
                    emit(kind, s - off, (s - off) % nb)

    def done(self, engine, sem, t):
        engine.wait_ge(sem, t + (1 + self.nbuf))

    def free(self, engine, sem, t):
        engine.wait_ge(sem, t + 1)

    def free1(self, engine, sem, t):
        engine.wait_ge(sem, t + self.nbuf)


def moments(nc, g, name, loads, loaded, rms=False):
    with ExitStack() as c:
        sem = semaphores(nc, c, name)
        stats = c.enter_context(nc.sbuf_tensor(f"{name}_stats", [P, NT, 6], F32))
        sq = c.enter_context(nc.sbuf_tensor(f"{name}_sq", [P, NT, 2], F32))
        stats_done, moments_done, std_done, rstd_done = sem("stats_done"), sem("moments_done"), sem("std_done"), sem("rstd_done")
        with nc.Block() as block:
            @block.sync
            def _(sp):
                for dst, src in loads:
                    sp.dma_start(dst, src).then_inc(loaded, 16)

            @block.vector
            def _(dve):
                for t in range(NT):
                    nc.vector.bn_stats(stats[:, t, :], g.x[:, t, :]).then_inc(stats_done, 1)
                for t in range(NT):
                    dve.wait_ge(stats_done, t + 1)
                    nc.vector.bn_aggr(g.mv[:, t, :], stats[:, t, :]).then_inc(moments_done, 1)
                dve.wait_ge(std_done, 1)
                nc.vector.reciprocal(g.rstd[:, :], g.std[:, :]).then_inc(rstd_done, 1)
                if rms:
                    dve.wait_ge(rstd_done, 1)
                    nc.vector.tensor_tensor(sq[:, :, 0], g.rstd[:, :], g.rstd[:, :], ALU.mult).then_inc(rstd_done, 1)
                    dve.wait_ge(rstd_done, 2)
                    nc.vector.tensor_tensor(sq[:, :, 1], sq[:, :, 0], g.mv[:, :, 1], ALU.mult).then_inc(rstd_done, 1)
                    dve.wait_ge(std_done, 2)
                    nc.vector.reciprocal(g.rrms[:, :], g.rms[:, :]).then_inc(rstd_done, 1)

            @block.scalar
            def _(act):
                act.wait_ge(moments_done, NT)
                nc.scalar.activation(g.std[:, :], g.mv[:, :, 1], ACT.Sqrt, bias=g.cols[:, 0:1]).then_inc(std_done, 1)
                if rms:
                    act.wait_ge(rstd_done, 3)
                    nc.scalar.activation(g.rms[:, :], sq[:, :, 1], ACT.Sqrt, bias=g.cols[:, 6:7]).then_inc(std_done, 1)


def head_mix_ffn(nc, g, name, w):
    H, DH, E = 16, 8, 8
    C3 = 3 * D
    with ExitStack() as c:
        sem = semaphores(nc, c, name)
        sb = lambda n, s, d=F32: c.enter_context(nc.sbuf_tensor(f"{name}_{n}", s, d))
        pb = lambda n, s, d=F32: c.enter_context(nc.psum_tensor(f"{name}_{n}", s, d))
        z2 = sb("z2", [P, NT, D])
        ms2, rms2, rr2 = sb("ms2", [P, NT]), sb("rms2", [P, NT]), sb("rr2", [P, NT])
        with ExitStack() as c1:
            sb1 = lambda n, s, d=F32: c1.enter_context(nc.sbuf_tensor(f"{name}_{n}", s, d))
            pb1 = lambda n, s, d=F32: c1.enter_context(nc.psum_tensor(f"{name}_{n}", s, d))
            wqkv, wdT, wup, wo = sb1("wqkv", [P, C3]), sb1("wdT", [DC, D]), sb1("wup", [DC, 2 * D]), sb1("wo", [P, D])
            bdown, bdb = sb1("bdown", [DC, 1]), sb1("bdb", [DC, P])
            brow, bo, bias = sb1("brow", [1, C3]), sb1("bo", [1, D]), sb1("bias", [P, C3])
            gamma = sb1("gamma", [P, 1])
            NB = 4
            z, zT, qkv = sb1("z", [P, NB, D]), sb1("zT", [P, NB, D]), sb1("qkv", [P, NB, C3])
            prod, att, eatt = sb1("prod", [P, NB, H * H * DH]), sb1("att", [P, NB, H * H]), sb1("eatt", [P, NB, H * H])
            top, esum, einv = sb1("top", [P, H]), sb1("esum", [P, H]), sb1("einv", [P, H])
            prod2, o_raw = sb1("prod2", [P, 2, H * DH * H]), sb1("o_raw", [P, D])
            o, oT, zz, sqr = sb1("o", [P, NB, D]), sb1("oT", [P, NB, D]), sb1("zz", [P, D]), sb1("sqr", [P, D])
            ps_t, ps_q = [pb1(f"ps_t{k}", [P, 512]) for k in range(2)], [pb1(f"ps_q{k}", [P, 512]) for k in range(2)]
            ps_u, ps_y = [pb1(f"ps_u{k}", [P, 512]) for k in range(2)], [pb1(f"ps_y{k}", [P, 512]) for k in range(2)]
            loaded, folded, ready, biased = sem("loaded"), sem("folded"), sem("ready"), sem("biased")
            loads = [(wqkv[:, 0:D], w["wq"]), (wdT[:, :], w["wdT"]), (wup[:, :], w["wup"]), (wo[:, :], w["wo"]),
                     (bdown[:, :], w["bdown"]), (brow[:, :], w["brow"]), (bo[:, :], w["bo"]), (gamma[:, :], w["gamma1"])]
            moments(nc, g, name + "m", loads, loaded, rms=True)
            names = ["z", "turn", "zT", "qkvmm", "qkv", "prod", "att", "exp", "weigh", "rest", "mix", "oturn", "oT", "omm", "z2", "sq"]
            s = {n: sem("s_" + n) for n in names}
            r_step, v_step, y_step = sem("r_step"), sem("v_step"), sem("y_step")
            POOLED = 12
            order = [("qkvmm", 1), ("oturn", 4), ("oT", 4), ("weigh", 3), ("qkv", 1), ("prod", 1), ("att", 2), ("exp", 2),
                     ("z", 0), ("turn", 0), ("zT", 0), ("omm", 4), ("rest", 3), ("z2", 4), ("sq", 4), ("mix", 3)]
            flow = Flow(NT, NB, order)
            done, free = flow.done, flow.free

            def weighted(b, h0, h1):
                e = eatt[:, b, :].rearrange("p (h k) -> p h k", h=H)[:, h0:h1, None, :].broadcast_to([P, h1 - h0, DH, H])
                v = qkv[:, b, D:C3].rearrange("p (k d) -> p d k", d=2 * DH)[:, None, DH:2 * DH, :].broadcast_to([P, h1 - h0, DH, H])
                return prod2[:, b % 2, :].rearrange("p (h d k) -> p h d k", h=H, d=DH)[:, h0:h1, :, :], e, v

            block = c1.enter_context(nc.Block())

            @block.tensor
            def _(pe):
                for n in ("turn", "qkvmm", "oturn", "omm"):
                    pe.sem_inc(s[n], NB)
                pe.wait_ge(loaded, 8 * 16)
                pe.wait_ge(ready, 1)
                nc.tensor.matmul(ps_q[0][:, 0:2 * D], wdT[:, :], wup[:, :], start=True, stop=True).then_inc(folded, 1)
                nc.tensor.matmul(ps_q[1][:, 0:C3], g.ones[0:1, :], brow[:, :], start=True, stop=False)
                nc.tensor.matmul(ps_q[1][:, D:C3], bdb[:, :], wup[:, :], start=False, stop=True).then_inc(folded, 1)
                pe.wait_ge(biased, 2)

                def emit(kind, t, b):
                    if kind == "turn":
                        done(pe, s["z"], t)
                        free(pe, s["zT"], t + 2)
                        nc.tensor.transpose(ps_t[b % 2][:, 0:P], z[:, b, :], g.ident[:, :]).then_inc(s[kind], 1)
                    elif kind == "qkvmm":
                        done(pe, s["zT"], t)
                        free(pe, s["qkv"], t + 2)
                        nc.tensor.matmul(ps_q[b % 2][:, 0:C3], zT[:, b, :], wqkv[:, :], start=True, stop=True).then_inc(s[kind], 1)
                    elif kind == "oturn":
                        done(pe, s["mix"], t)
                        free(pe, s["oT"], t + 2)
                        nc.tensor.transpose(ps_u[b % 2][:, 0:P], o[:, b, :], g.ident[:, :]).then_inc(s[kind], 1)
                    elif kind == "omm":
                        done(pe, s["oT"], t)
                        free(pe, s["z2"], t + 2)
                        nc.tensor.matmul(ps_y[b % 2][:, 0:D], g.ones[0:1, :], bo[:, :], start=True, stop=False)
                        nc.tensor.matmul(ps_y[b % 2][:, 0:D], oT[:, b, :], wo[:, :], start=False, stop=True).then_inc(s[kind], 1)

                flow.run(pe, emit)

            @block.scalar
            def _(act):
                for n in ("zT", "exp", "oT", "sq"):
                    act.sem_inc(s[n], NB)

                def emit(kind, t, b):
                    if kind == "zT":
                        done(act, s["turn"], t)
                        free(act, s["qkvmm"], t)
                        nc.scalar.activation(zT[:, b, :], ps_t[b % 2][:, 0:P], ACT.Copy).then_inc(s[kind], 1)
                    elif kind == "exp":
                        done(act, s["att"], t)
                        free(act, s["mix"], t)
                        nc.scalar.activation(eatt[:, b, :], att[:, b, :], ACT.Exp, scale=DH ** -0.5).then_inc(s[kind], 1)
                    elif kind == "oT":
                        done(act, s["oturn"], t)
                        free(act, s["omm"], t)
                        nc.scalar.activation(oT[:, b, :], ps_u[b % 2][:, 0:P], ACT.Copy).then_inc(s[kind], 1)
                    elif kind == "sq":
                        done(act, s["z2"], t)
                        flow.free1(act, s["sq"], t)
                        nc.scalar.activation(sqr[:, :], z2[:, t, :], ACT.Square, accum_out=ms2[:, bass.ds(t, 1)]).then_inc(s[kind], 1)

                flow.run(act, emit)

            @block.gpsimd
            def _(pool):
                pool.sem_inc(s["prod"], NB)
                pool.sem_inc(s["weigh"], NB)

                def emit(kind, t, b):
                    if kind == "prod":
                        done(pool, s["qkv"], t)
                        free(pool, s["att"], t)
                        q = qkv[:, b, 0:D].rearrange("p (h d) -> p h d", d=DH)[:, :, None, :].broadcast_to([P, H, H, DH])
                        k = qkv[:, b, D:C3].rearrange("p (h d) -> p h d", d=2 * DH)[:, None, :, 0:DH].broadcast_to([P, H, H, DH])
                        nc.gpsimd.tensor_tensor(prod[:, b, :].rearrange("p (h k d) -> p h k d", h=H, k=H), q, k, ALU.mult).then_inc(s[kind], 1)
                    elif kind == "weigh":
                        done(pool, s["exp"], t)
                        free(pool, s["mix"], t + 2)
                        nc.gpsimd.tensor_tensor(*weighted(b, 0, POOLED), ALU.mult).then_inc(s[kind], 1)

                flow.run(pool, emit)

            @block.vector
            def _(dve):
                for n in ("z", "qkv", "att", "rest", "mix", "z2"):
                    dve.sem_inc(s[n], NB)
                dve.wait_ge(loaded, 8 * 16)
                nc.vector.tensor_copy(bdb[:, :], bdown[:, 0:1].broadcast_to([DC, P])).then_inc(ready, 1)
                dve.wait_ge(folded, 2)
                nc.vector.tensor_scalar(wqkv[:, D:C3], ps_q[0][:, 0:2 * D], gamma[:, 0:1], None, ALU.mult)
                nc.vector.tensor_scalar(wqkv[:, 0:D], wqkv[:, 0:D], gamma[:, 0:1], None, ALU.mult).then_inc(biased, 1)
                nc.vector.tensor_copy(bias[:, :], ps_q[1][:, 0:C3]).then_inc(biased, 1)
                dve.wait_ge(biased, 2)

                def emit(kind, t, b):
                    if kind == "z":
                        free(dve, s["turn"], t)
                        nc.vector.tensor_scalar(z[:, b, :], g.x[:, t, :], g.mv[:, t, 0:1], g.rstd[:, bass.ds(t, 1)],
                                                ALU.subtract, ALU.mult).then_inc(s[kind], 1)
                    elif kind == "qkv":
                        done(dve, s["qkvmm"], t)
                        free(dve, s["mix"], t)
                        nc.vector.scalar_tensor_tensor(qkv[:, b, :], ps_q[b % 2][:, 0:C3], g.rrms[:, bass.ds(t, 1)], bias[:, :],
                                                       ALU.mult, ALU.add).then_inc(s[kind], 1)
                    elif kind == "att":
                        L = 3
                        done(dve, s["prod"], t)
                        free(dve, s["exp"], t)
                        a = att[:, b, :].rearrange("p (h k) -> p h k", h=H)
                        nc.vector.tensor_reduce(a, prod[:, b, :].rearrange("p (h k d) -> p h k d", h=H, k=H), AX.X, ALU.add).then_inc(r_step, 1)
                        dve.wait_ge(r_step, t * 2 + 1)
                        nc.vector.tensor_reduce(top[:, :], a, AX.X, ALU.max).then_inc(r_step, 1)
                        dve.wait_ge(r_step, t * 2 + 2)
                        nc.vector.tensor_tensor(a, a, top[:, :, None].broadcast_to([P, H, H]), ALU.subtract).then_inc(s[kind], 1)
                    elif kind == "rest":
                        done(dve, s["exp"], t)
                        nc.vector.tensor_tensor(*weighted(b, POOLED, H), ALU.mult).then_inc(s[kind], 1)
                    elif kind == "mix":
                        done(dve, s["rest"], t)
                        done(dve, s["weigh"], t)
                        free(dve, s["oturn"], t)
                        flow.free1(dve, s["mix"], t)
                        e = eatt[:, b, :].rearrange("p (h k) -> p h k", h=H)
                        pr = prod2[:, b % 2, :].rearrange("p (h d k) -> p h d k", h=H, d=DH)
                        nc.vector.tensor_reduce(esum[:, :], e, AX.X, ALU.add).then_inc(v_step, 1)
                        dve.wait_ge(v_step, t * 3 + 1)
                        nc.vector.reciprocal(einv[:, :], esum[:, :]).then_inc(v_step, 1)
                        nc.vector.tensor_reduce(o_raw[:, :].rearrange("p (h d) -> p h d", h=H), pr, AX.X, ALU.add).then_inc(v_step, 1)
                        dve.wait_ge(v_step, t * 3 + 3)
                        nc.vector.tensor_tensor(o[:, b, :].rearrange("p (h d) -> p h d", h=H), o_raw[:, :].rearrange("p (h d) -> p h d", h=H),
                                                einv[:, :, None].broadcast_to([P, H, DH]), ALU.mult).then_inc(s[kind], 1)
                    elif kind == "z2":
                        done(dve, s["omm"], t)
                        flow.free1(dve, s["z2"], t)
                        nc.vector.tensor_scalar(zz[:, :], g.x[:, t, :], g.mv[:, t, 0:1], g.rstd[:, bass.ds(t, 1)],
                                                ALU.subtract, ALU.mult).then_inc(y_step, 1)
                        dve.wait_ge(y_step, t + 1)
                        nc.vector.tensor_tensor(z2[:, t, :], ps_y[b % 2][:, 0:D], zz[:, :], ALU.add).then_inc(s[kind], 1)

                flow.run(dve, emit)

        with ExitStack() as c1:
            sb1 = lambda n, s, d=F32: c1.enter_context(nc.sbuf_tensor(f"{name}b_{n}", s, d))
            pb1 = lambda n, s, d=F32: c1.enter_context(nc.psum_tensor(f"{name}b_{n}", s, d))
            NB = 2
            wg, we, bg, gamma = sb1("wg", [P, E]), sb1("we", [P, E * D]), sb1("bg", [P, E]), sb1("gamma", [P, 1])
            zc, zT = sb1("zc", [P, NB, D]), sb1("zT", [P, NB, D])
            lg, eg = sb1("lg", [P, NB, E]), sb1("eg", [P, NB, E])
            lraw, ltop, esum, einv = sb1("lraw", [P, E]), sb1("ltop", [P, 1]), sb1("esum", [P, 1]), sb1("einv", [P, 1])
            gate, mixed, comb, xz = sb1("gate", [P, E]), sb1("mixed", [P, E, D]), sb1("comb", [P, D]), sb1("xz", [P, D])
            ps_t, ps_g = pb1("ps_t", [P, 512]), pb1("ps_g", [P, 512])
            ps_e = [pb1(f"ps_e{k}", [P, 1024]) for k in range(2)]
            loaded, rms_in, rms_out, scaled = sem("b_loaded"), sem("b_rms_in"), sem("b_rms_out"), sem("b_scaled")
            s = {n: sem("b_" + n) for n in ("copy", "turn", "zT", "mm", "logit", "exp", "mix")}
            l_step, m_step = sem("b_l_step"), sem("b_m_step")
            order = [("copy", 0), ("turn", 0), ("zT", 0), ("mm", 1), ("mix", 2), ("logit", 1), ("exp", 1)]
            flow = Flow(NT, NB, order)
            done, free, free1 = flow.done, flow.free, flow.free1
            block = c1.enter_context(nc.Block())

            @block.sync
            def _(sp):
                for dst, src in ((wg, w["wg"]), (we, w["we"]), (bg, w["bg"]), (gamma, w["gamma2"])):
                    sp.dma_start(dst[:, :], src).then_inc(loaded, 16)

            @block.tensor
            def _(pe):
                for n in ("turn", "mm"):
                    pe.sem_inc(s[n], NB)
                pe.wait_ge(scaled, 1)

                def emit(kind, t, b):
                    if kind == "turn":
                        done(pe, s["copy"], t)
                        free1(pe, s["zT"], t)
                        nc.tensor.transpose(ps_t[:, 0:P], zc[:, b, :], g.ident[:, :]).then_inc(s[kind], 1)
                    elif kind == "mm":
                        done(pe, s["zT"], t)
                        free1(pe, s["logit"], t)
                        free(pe, s["mix"], t)
                        nc.tensor.matmul(ps_g[:, 0:E], zT[:, b, :], wg[:, :], start=True, stop=True)
                        for k in range(2):
                            r = nc.tensor.matmul(ps_e[b][:, k * 512:(k + 1) * 512], zT[:, b, :], we[:, k * 512:(k + 1) * 512], start=True, stop=True)
                        r.then_inc(s[kind], 1)

                flow.run(pe, emit)

            @block.scalar
            def _(act):
                for n in ("copy", "zT", "exp"):
                    act.sem_inc(s[n], NB)
                nc.scalar.activation(rms2[:, :], ms2[:, :], ACT.Sqrt, bias=g.cols[:, 6:7], scale=1.0 / D).then_inc(rms_in, 1)

                def emit(kind, t, b):
                    if kind == "copy":
                        free(act, s["turn"], t)
                        nc.scalar.activation(zc[:, b, :], z2[:, t, :], ACT.Copy).then_inc(s[kind], 1)
                    elif kind == "zT":
                        done(act, s["turn"], t)
                        free(act, s["mm"], t)
                        nc.scalar.activation(zT[:, b, :], ps_t[:, 0:P], ACT.Copy).then_inc(s[kind], 1)
                    elif kind == "exp":
                        done(act, s["logit"], t)
                        free(act, s["mix"], t)
                        nc.scalar.activation(eg[:, b, :], lg[:, b, :], ACT.Exp).then_inc(s[kind], 1)

                flow.run(act, emit)

            @block.vector
            def _(dve):
                for n in ("logit", "mix"):
                    dve.sem_inc(s[n], NB)
                dve.wait_ge(loaded, 4 * 16)
                nc.vector.tensor_scalar(we[:, :], we[:, :], gamma[:, 0:1], None, ALU.mult)
                nc.vector.tensor_scalar(wg[:, :], wg[:, :], gamma[:, 0:1], None, ALU.mult).then_inc(scaled, 1)
                dve.wait_ge(rms_in, 1)
                nc.vector.reciprocal(rr2[:, :], rms2[:, :]).then_inc(rms_out, 1)
                dve.wait_ge(rms_out, 1)

                def emit(kind, t, b):
                    if kind == "logit":
                        done(dve, s["mm"], t)
                        free(dve, s["exp"], t)
                        free1(dve, s["logit"], t)
                        nc.vector.scalar_tensor_tensor(lraw[:, :], ps_g[:, 0:E], rr2[:, bass.ds(t, 1)], bg[:, :], ALU.mult, ALU.add).then_inc(l_step, 1)
                        dve.wait_ge(l_step, t * 2 + 1)
                        nc.vector.tensor_reduce(ltop[:, :], lraw[:, :], AX.X, ALU.max).then_inc(l_step, 1)
                        dve.wait_ge(l_step, t * 2 + 2)
                        nc.vector.tensor_scalar(lg[:, b, :], lraw[:, :], ltop[:, 0:1], None, ALU.subtract).then_inc(s[kind], 1)
                    elif kind == "mix":
                        done(dve, s["exp"], t)
                        done(dve, s["mm"], t)
                        free1(dve, s["mix"], t)
                        nc.vector.tensor_reduce(esum[:, :], eg[:, b, :], AX.X, ALU.add).then_inc(m_step, 1)
                        dve.wait_ge(m_step, t * 6 + 1)
                        nc.vector.reciprocal(einv[:, :], esum[:, :]).then_inc(m_step, 1)
                        dve.wait_ge(m_step, t * 6 + 2)
                        nc.vector.tensor_scalar(gate[:, :], eg[:, b, :], einv[:, 0:1], rr2[:, bass.ds(t, 1)], ALU.mult, ALU.mult).then_inc(m_step, 1)
                        dve.wait_ge(m_step, t * 6 + 3)
                        nc.vector.tensor_tensor(mixed[:, :, :], ps_e[b][:, :].rearrange("p (e f) -> p e f", e=E),
                                                gate[:, :, None].broadcast_to([P, E, D]), ALU.mult).then_inc(m_step, 1)
                        nc.vector.tensor_tensor(xz[:, :], g.x[:, t, :], z2[:, t, :], ALU.add).then_inc(m_step, 1)
                        dve.wait_ge(m_step, t * 6 + 5)
                        nc.vector.tensor_reduce(comb[:, :], mixed[:, :, :].rearrange("p e f -> p f e"), AX.X, ALU.add).then_inc(m_step, 1)
                        dve.wait_ge(m_step, t * 6 + 6)
                        nc.vector.tensor_tensor(g.x[:, t, :], comb[:, :], xz[:, :], ALU.add).then_inc(s[kind], 1)

                flow.run(dve, emit)


MAGIC = 1.5 * 2.0 ** 23
QMAX = 127.0


def conv_ffn(nc, g, name, w):
    F = 512
    FC = F // P
    with ExitStack() as c:
        sem = semaphores(nc, c, name)
        sb = lambda n, s, d=F32: c.enter_context(nc.sbuf_tensor(f"{name}_{n}", s, d))
        pb = lambda n, s, d=F32: c.enter_context(nc.psum_tensor(f"{name}_{n}", s, d))
        NB = 4
        wt = [sb(f"wt{k}", [P, F]) for k in range(2)]
        wa = sb("wa", [P, F])
        wb = [sb(f"wb{k}", [P, F], BF16) for k in range(2)]
        wsum, wmean, wscale = sb("wsum", [P, 2]), sb("wmean", [P, 2]), sb("wscale", [P, 2])
        convw, convb = sb("convw", [P, FC, 3]), sb("convb", [P, FC])
        z = sb("z", [P, QT, D])
        amax, inv, scl = sb("amax", [P, QT]), sb("inv", [P, NB, QT]), sb("scl", [P, QT])
        za, zi, diag = sb("za", [P, QT, D]), sb("zi", [P, NB, QT, D], BF16), sb("diag", [P, NB, QT, P])
        xiT, invb = sb("xiT", [P, NB, S], BF16), sb("invb", [P, NB, S])
        hd, y0, y1 = sb("hd", [P, FC, S + 2]), sb("y0", [P, NB, FC, S]), sb("y1", [P, NB, FC, S])
        hs = sb("hs", [P, NB, FC, S])
        amax2, inv2, scl2 = sb("amax2", [P, QT]), sb("inv2", [P, NB, QT]), sb("scl2", [P, QT])
        ha2 = sb("ha2", [P, QT, D])
        ha, hi, hiT = sb("ha", [P, QT * F]), sb("hi", [P, NB, QT * F], BF16), sb("hiT", [P, NB, FC, S], BF16)
        identb = sb("identb", [P, P], BF16)
        loaded = sem("loaded")
        moments(nc, g, name + "m", [(wt[0][:, :], w["w1"]), (wt[1][:, :], w["w2"]), (convw[:, :, :], w["convw"]), (convb[:, :], w["convb"])], loaded)
        ps_t, ps_b = pb("ps_t", [P, 512], BF16), pb("ps_b", [P, 512])
        ps_h, ps_u, ps_v, ps_y = pb("ps_h", [P, 1024]), pb("ps_u", [P, 1024]), pb("ps_v", [P, 1024], BF16), pb("ps_y", [P, 512])
        wstep, wsummed, prepared = sem("wstep"), sem("wsummed"), sem("prepared")
        names = ["quant", "turn", "turned", "up", "deq", "conv0", "conv", "silu", "back", "quant2", "turn2", "turned2", "down", "add"]
        s = {n: sem("s_" + n) for n in names}
        q_step, c_step, r_step, a_step = sem("q_step"), sem("c_step"), sem("r_step"), sem("a_step")
        order = [("add", 4), ("conv", 2), ("silu", 2), ("back", 3), ("quant2", 3), ("up", 1), ("deq", 1), ("turn2", 3), ("turned2", 3),
                 ("conv0", 1), ("down", 3), ("quant", 0), ("turn", 0), ("turned", 0)]
        flow = Flow(B, NB, order)
        done, free, free1 = flow.done, flow.free, flow.free1
        block = c.enter_context(nc.Block())

        @block.tensor
        def _(pe):
            for n in ("turn", "up", "back", "turn2", "down"):
                pe.sem_inc(s[n], NB)
            pe.wait_ge(wstep, 2)
            nc.tensor.matmul(ps_y[:, 0:2], g.ones[:, :], wsum[:, :], start=True, stop=True).then_inc(wsummed, 1)
            pe.wait_ge(prepared, 1)

            def emit(kind, t, b):
                if kind == "turn":
                    done(pe, s["quant"], t)
                    free1(pe, s["turned"], t)
                    for q in range(QT):
                        nc.tensor.transpose(ps_t[:, q * P:(q + 1) * P], zi[:, b, q, :], identb[:, :])
                        r = nc.tensor.matmul(ps_b[:, q * P:(q + 1) * P], g.ones[:, :], diag[:, b, q, :], start=True, stop=True)
                    r.then_inc(s[kind], 1)
                elif kind == "up":
                    done(pe, s["turned"], t)
                    free1(pe, s["deq"], t)
                    for f in range(FC):
                        r = nc.tensor.matmul(ps_h[:, f * S:(f + 1) * S], wb[0][:, f * P:(f + 1) * P], xiT[:, b, :], start=True, stop=True)
                    r.then_inc(s[kind], 1)
                elif kind == "back":
                    done(pe, s["silu"], t)
                    free1(pe, s["quant2"], t)
                    for q in range(QT):
                        for f in range(FC):
                            r = nc.tensor.transpose(ps_u[:, q * F + f * P:q * F + (f + 1) * P], hs[:, b, f, q * P:(q + 1) * P], g.ident[:, :])
                    r.then_inc(s[kind], 1)
                elif kind == "turn2":
                    done(pe, s["quant2"], t)
                    free1(pe, s["turned2"], t)
                    for q in range(QT):
                        for f in range(FC):
                            r = nc.tensor.transpose(ps_v[:, f * S + q * P:f * S + (q + 1) * P], hi[:, b, q * F + f * P:q * F + (f + 1) * P], identb[:, :])
                    r.then_inc(s[kind], 1)
                elif kind == "down":
                    done(pe, s["turned2"], t)
                    free1(pe, s["add"], t)
                    for q in range(QT):
                        for f in range(FC):
                            r = nc.tensor.matmul(ps_y[:, q * D:(q + 1) * D], hiT[:, b, f, q * P:(q + 1) * P], wb[1][:, f * D:(f + 1) * D],
                                                 start=f == 0, stop=f == FC - 1)
                    r.then_inc(s[kind], 1)

            flow.run(pe, emit)

        @block.scalar
        def _(act):
            for n in ("turned", "conv0", "silu", "turned2"):
                act.sem_inc(s[n], NB)
            act.wait_ge(prepared, 1)

            def emit(kind, t, b):
                if kind == "turned":
                    done(act, s["turn"], t)
                    free(act, s["up"], t)
                    free(act, s["deq"], t)
                    nc.scalar.activation(xiT[:, b, :], ps_t[:, 0:S], ACT.Copy)
                    nc.scalar.activation(invb[:, b, :], ps_b[:, 0:S], ACT.Copy).then_inc(s[kind], 1)
                elif kind == "conv0":
                    done(act, s["deq"], t)
                    free(act, s["conv"], t)
                    for f in range(FC):
                        r = nc.scalar.activation(y0[:, b, f, :], hd[:, f, 1:S + 1], ACT.Identity, bias=convb[:, f:f + 1], scale=convw[:, f, 1:2])
                    r.then_inc(s[kind], 1)
                elif kind == "silu":
                    done(act, s["conv"], t)
                    free(act, s["back"], t)
                    nc.scalar.activation(hs[:, b, :, :], y0[:, b, :, :], ACT.Silu).then_inc(s[kind], 1)
                elif kind == "turned2":
                    done(act, s["turn2"], t)
                    free(act, s["down"], t)
                    nc.scalar.activation(hiT[:, b, :, :].rearrange("p f s -> p (f s)"), ps_v[:, :], ACT.Copy).then_inc(s[kind], 1)

            flow.run(act, emit)

        @block.vector
        def _(dve):
            for n in ("quant", "deq", "conv", "quant2", "add"):
                dve.sem_inc(s[n], NB)
            dve.wait_ge(loaded, 64)
            nc.vector.memset(hd[:, :, :], 0.0)
            nc.vector.tensor_copy(identb[:, :], g.ident[:, :])
            for k in range(2):
                nc.vector.tensor_reduce(wsum[:, k:k + 1], wt[k][:, :], AX.X, ALU.add, apply_absolute_value=True).then_inc(wstep, 1)
            dve.wait_ge(wsummed, 1)
            nc.vector.tensor_scalar(wmean[:, :], ps_y[:, 0:2], 1.0 / (F * D), 1e-5, ALU.mult, ALU.max).then_inc(wstep, 1)
            dve.wait_ge(wstep, 3)
            nc.vector.reciprocal(wscale[:, :], wmean[:, :]).then_inc(wstep, 1)
            nc.vector.tensor_scalar(convw[:, :, :], convw[:, :, :], wmean[:, 0:1], None, ALU.mult)
            for k in range(2):
                dve.wait_ge(wstep, 4 + 3 * k)
                nc.vector.tensor_scalar(wa[:, :], wt[k][:, :], wscale[:, k:k + 1], MAGIC, ALU.mult, ALU.add).then_inc(wstep, 1)
                dve.wait_ge(wstep, 5 + 3 * k)
                nc.vector.tensor_scalar(wt[k][:, :], wa[:, :], MAGIC - 1, MAGIC + 1, ALU.max, ALU.min).then_inc(wstep, 1)
                dve.wait_ge(wstep, 6 + 3 * k)
                nc.vector.tensor_scalar(wb[k][:, :], wt[k][:, :], MAGIC, None, ALU.subtract).then_inc(wstep, 1)
            dve.wait_ge(wstep, 10)
            nc.vector.tensor_copy(wa[:, 0:1], wmean[:, 0:1]).then_inc(prepared, 1)

            def scales(src, top, i_b, scl_, step, at, width):
                nc.vector.tensor_reduce(top[:, :], src, AX.X, ALU.max, apply_absolute_value=True).then_inc(step, 1)
                dve.wait_ge(step, at(1))
                nc.vector.tensor_scalar(i_b, top[:, :], 1e-5, 1.0 / QMAX, ALU.max, ALU.mult).then_inc(step, 1)
                dve.wait_ge(step, at(2))
                nc.vector.reciprocal(scl_[:, :], i_b).then_inc(step, 1)
                dve.wait_ge(step, at(3))

            def emit(kind, t, b):
                if kind == "quant":
                    free(dve, s["turn"], t)
                    free1(dve, s["quant"], t)
                    N = 7
                    at = lambda k: t * N + k
                    for q in range(QT):
                        nc.vector.tensor_scalar(z[:, q, :], g.xt[:, q, t, :], g.meant[:, q, bass.ds(t, 1)], g.rstdt[:, q, bass.ds(t, 1)],
                                                ALU.subtract, ALU.mult).then_inc(q_step, 1)
                    dve.wait_ge(q_step, at(2))
                    scales(z[:, :, :], amax, inv[:, b, :], scl, q_step, lambda k: at(2 + k), D)
                    for q in range(QT):
                        r = nc.vector.tensor_scalar(za[:, q, :], z[:, q, :], scl[:, q:q + 1], MAGIC, ALU.mult, ALU.add)
                    r.then_inc(q_step, 1)
                    dve.wait_ge(q_step, at(6))
                    nc.vector.tensor_scalar(z[:, :, :], za[:, :, :], MAGIC - 128, MAGIC + 127, ALU.max, ALU.min).then_inc(q_step, 1)
                    dve.wait_ge(q_step, at(7))
                    for q in range(QT):
                        nc.vector.tensor_scalar(diag[:, b, q, :], g.ident[:, :], inv[:, b, q:q + 1], None, ALU.mult)
                    nc.vector.tensor_scalar(zi[:, b, :, :], z[:, :, :], MAGIC, None, ALU.subtract).then_inc(s[kind], 1)
                elif kind == "deq":
                    done(dve, s["up"], t)
                    done(dve, s["turned"], t)
                    free1(dve, s["conv0"], t)
                    free1(dve, s["conv"], t)
                    nc.vector.tensor_tensor(hd[:, :, 1:S + 1], ps_h[:, :].rearrange("p (f s) -> p f s", f=FC),
                                            invb[:, b, None, :].broadcast_to([P, FC, S]), ALU.mult).then_inc(s[kind], 1)
                elif kind == "conv":
                    done(dve, s["conv0"], t)
                    free(dve, s["silu"], t)
                    for f in range(FC):
                        r = nc.vector.scalar_tensor_tensor(y1[:, b, f, :], hd[:, f, 0:S], convw[:, f, 0:1], y0[:, b, f, :], ALU.mult, ALU.add)
                    r.then_inc(c_step, 1)
                    dve.wait_ge(c_step, t + 1)
                    for f in range(FC):
                        r = nc.vector.scalar_tensor_tensor(y0[:, b, f, :], hd[:, f, 2:S + 2], convw[:, f, 2:3], y1[:, b, f, :], ALU.mult, ALU.add)
                    r.then_inc(s[kind], 1)
                elif kind == "quant2":
                    done(dve, s["back"], t)
                    free(dve, s["turn2"], t)
                    free1(dve, s["quant2"], t)
                    N = 5
                    at = lambda k: t * N + k
                    src = ps_u[:, :].rearrange("p (q f) -> p q f", q=QT)
                    scales(src, amax2, inv2[:, b, :], scl2, r_step, at, F)
                    for q in range(QT):
                        r = nc.vector.tensor_scalar(ha[:, q * F:(q + 1) * F], src[:, q, :], scl2[:, q:q + 1], MAGIC, ALU.mult, ALU.add)
                    r.then_inc(r_step, 1)
                    dve.wait_ge(r_step, at(4))
                    nc.vector.tensor_scalar(ha[:, :], ha[:, :], MAGIC - 128, MAGIC + 127, ALU.max, ALU.min).then_inc(r_step, 1)
                    dve.wait_ge(r_step, at(5))
                    nc.vector.tensor_scalar(hi[:, b, :], ha[:, :], MAGIC, None, ALU.subtract).then_inc(s[kind], 1)
                elif kind == "add":
                    done(dve, s["down"], t)
                    free1(dve, s["add"], t)
                    for q in range(QT):
                        r = nc.vector.tensor_scalar(ha2[:, q, :], ps_y[:, q * D:(q + 1) * D], inv2[:, b, q:q + 1], wmean[:, 1:2], ALU.mult, ALU.mult)
                    r.then_inc(a_step, 1)
                    dve.wait_ge(a_step, t + 1)
                    nc.vector.tensor_tensor(g.xb3[:, t, :, :], ha2[:, :, :], g.xb3[:, t, :, :], ALU.add).then_inc(s[kind], 1)

            flow.run(dve, emit)


def expert_ffn(nc, g, name, w, NF, FE, shared, routing):
    WS = 128.0
    NC = NF // P
    NR = w["wr"].shape[1]
    NE = 32 if shared else 8
    NX = NE + shared
    BLK = 512
    NBLK = B * S // BLK
    REP = max(1, FE // P)
    with ExitStack() as c:
        sem = semaphores(nc, c, name)
        sb = lambda n, s, d=F32: c.enter_context(nc.sbuf_tensor(f"{name}_{n}", s, d))
        pb = lambda n, s, d=F32: c.enter_context(nc.psum_tensor(f"{name}_{n}", s, d))
        w16 = [[sb(f"w{k}_{h}", [P, NC, P], F16) for h in range(2)] for k in range(3)]
        z16 = [sb(f"z{h}", [P, NBLK, BLK], F16) for h in range(2)]
        sel = sb("sel", [2 * NX, NC, P], F16)
        combT = sb("combT", [2 * NX, NBLK, BLK], F16)
        with ExitStack() as c1:
            sb1 = lambda n, s, d=F32: c1.enter_context(nc.sbuf_tensor(f"{name}_{n}", s, d))
            pb1 = lambda n, s, d=F32: c1.enter_context(nc.psum_tensor(f"{name}_{n}", s, d))
            wr = sb1("wr", [P, NR])
            lT = sb1("lT", [NR, NBLK, BLK])
            sg, comb, comb16 = sb1("sg", [P, NT, NR]), sb1("comb", [P, NT, NX]), sb1("comb16", [P, NT, 2, NX], F16)
            raw, raw_sel = [sb1(f"raw{k}", [P, NC, P]) for k in range(3)], sb1("raw_sel", [2 * NX, NC, P])
            arrived, extra = sem("arrived"), routing.tiles(sb1)
            loads = [(wr[:, :], w["wr"])] + routing.loads(extra, w)
            layer_norm(nc, g, name + "n", loads, arrived)
            ps_l, ps_k = [pb1(f"ps_l{k}", [P, 512]) for k in range(4)], pb1("ps_k", [P, 512])
            mm, out, turned, sig = sem("mm"), sem("out"), sem("turned"), sem("sig")
            routed, back, st = sem("routed"), sem("back"), sem("route_step")
            loaded, taken, cast = [sem(f"loaded{k}") for k in range(4)], sem("taken"), sem("cast")
            block = c1.enter_context(nc.Block())

            @block.sync
            def _(sp):
                for k, (dst, src) in enumerate(zip(raw + [raw_sel], (w["wg"], w["wu"], w["wd"], w["sel"]))):
                    sp.dma_start(dst[:, :, :], src).then_inc(loaded[k], 16)

            @block.tensor
            def _(pe):
                pe.wait_ge(arrived, 16 * len(loads))
                for k in range(NBLK):
                    nc.tensor.matmul(ps_l[k][0:NR, :], wr[:, :], g.xnT[:, 2 * k:2 * k + 2, :], start=True, stop=True).then_inc(mm, 1)
                pe.wait_ge(out, NBLK)
                for t in range(NT):
                    r = nc.tensor.transpose(ps_k[:, t * NR:(t + 1) * NR], lT[:, t // 4, t % 4 * P:(t % 4 + 1) * P], g.ident[0:NR, 0:NR])
                r.then_inc(turned, 1)
                pe.wait_ge(routed, 1)
                for t in range(NT):
                    r = nc.tensor.matmul(ps_l[t // 4][0:2 * NX, t % 4 * P:(t % 4 + 1) * P], comb16[:, t, :, :].rearrange("p h n -> p (h n)"),
                                         g.ident16[:, :], start=True, stop=True)
                    if t % 4 == 3:
                        r.then_inc(back, 1)

            @block.scalar
            def _(act):
                for k in range(NBLK):
                    act.wait_ge(mm, k + 1)
                    nc.scalar.activation(lT[:, k, :], ps_l[k][0:NR, :], ACT.Copy).then_inc(out, 1)
                act.wait_ge(turned, 1)
                nc.scalar.activation(sg[:, :, :], ps_k[:, 0:NT * NR].rearrange("p (t n) -> p t n", n=NR), ACT.Sigmoid).then_inc(sig, 1)
                for k in range(NBLK):
                    nc.scalar.activation(z16[0][:, k, :], g.xnTb[:, k, :], ACT.Copy).then_inc(cast, 1)
                for k in range(3):
                    act.wait_ge(loaded[k], 16)
                    nc.scalar.activation(w16[k][0][:, :, :], raw[k][:, :, :], ACT.Copy, scale=WS).then_inc(taken, 1)
                    act.wait_ge(taken, k + 1)
                    nc.scalar.activation(raw[k][:, :, :], raw[k][:, :, :], ACT.Copy, scale=WS).then_inc(cast, 1)
                act.wait_ge(loaded[3], 16)
                nc.scalar.activation(sel[:, :, :], raw_sel[:, :, :], ACT.Copy)
                for k in range(NBLK):
                    act.wait_ge(back, k + 1)
                    nc.scalar.activation(combT[:, k, :], ps_l[k][0:2 * NX, :], ACT.Copy).then_inc(out, 1)

            @block.gpsimd
            def _(pool):
                for k in range(NBLK):
                    pool.wait_ge(cast, k + 1)
                    nc.gpsimd.tensor_tensor(z16[1][:, k, :], g.xnTb[:, k, :], z16[0][:, k, :], ALU.subtract)
                for k in range(3):
                    pool.wait_ge(cast, NBLK + k + 1)
                    nc.gpsimd.tensor_tensor(w16[k][1][:, :, :], raw[k][:, :, :], w16[k][0][:, :, :], ALU.subtract)

            @block.vector
            def _(dve):
                count = [0]

                def step(r):
                    r.then_inc(st, 1)
                    count[0] += 1
                    dve.wait_ge(st, count[0])

                dve.wait_ge(sig, 1)
                dve.wait_ge(arrived, 16 * len(loads))
                routing.route(nc, step, sg, comb, extra)
                step(nc.vector.tensor_copy(comb16[:, :, 0, :], comb[:, :, :]))
                nc.vector.tensor_tensor(comb16[:, :, 1, :], comb[:, :, :], comb16[:, :, 0, :], ALU.subtract).then_inc(routed, 1)

        with ExitStack() as c1:
            sb1 = lambda n, s, d=F32: c1.enter_context(nc.sbuf_tensor(f"{name}b_{n}", s, d))
            pb1 = lambda n, s, d=F32: c1.enter_context(nc.psum_tensor(f"{name}b_{n}", s, d))
            HB = 4
            LAG = 3
            sg, su, h = sb1("sg", [P, 2, BLK]), sb1("su", [P, 2, BLK]), sb1("h", [P, 2, BLK])
            h1, h2 = sb1("h1", [P, HB, BLK], F16), sb1("h2", [P, HB, BLK], F16)
            oT = sb1("oT", [P, 2, BLK])
            ps_g, ps_u, ps_c, ps_o = ([pb1(f"ps_{n}{k}", [P, BLK]) for k in range(2)] for n in "guco")
            ins, silu, su_done, hid, down = sem("b_ins"), sem("b_silu"), sem("b_su"), sem("b_hidden"), sem("b_down")
            cast, split = sem("b_cast"), sem("b_split")
            o_out, o_turned, added = sem("b_o_out"), sem("b_o_turned"), sem("b_added")
            block = c1.enter_context(nc.Block())
            M = 2 * NC
            SLOTS = M + LAG + 3
            last_down = {j * NC + NC - 1 + LAG: j for j in range(2)}

            @block.tensor
            def _(pe):
                pe.sem_inc(down, HB)

                def products(bank, weights, cc, parts, first, last):
                    for k, (a, b) in enumerate(((0, 0), (1, 0), (0, 1))):
                        r = nc.tensor.matmul(bank[:, :], weights[a][:, cc, :], parts[b], start=first and k == 0, stop=last and k == 2)
                    return r

                with pe.Fori(0, NBLK // 2) as i:
                    for slot in range(SLOTS):
                        if slot < M:
                            j, cc = divmod(slot, NC)
                            z = [z16[k][:, i * 2 + j, :] for k in range(2)]
                            pe.wait_ge(hid, i * M + (slot + 1))
                            products(ps_g[slot % 2], w16[0], cc, z, True, True)
                            r = products(ps_u[slot % 2], w16[1], cc, z, True, True)
                            if slot % REP == 0:
                                r = nc.tensor.matmul(ps_c[slot // REP % 2][:, :], sel[:, cc, :], combT[:, i * 2 + j, :], start=True, stop=True)
                            r.then_inc(ins, 1)
                        m = slot - LAG
                        if 0 <= m < M:
                            j, cc = divmod(m, NC)
                            pe.wait_ge(split, i * M + (m + 3))
                            if cc == 0:
                                pe.wait_ge(added, i * 2 + (j + 1))
                            products(ps_o[j], w16[2], cc, [h1[:, m % HB, :], h2[:, m % HB, :]], cc == 0, cc == NC - 1).then_inc(down, 1)
                        if slot - 1 in last_down:
                            j = last_down[slot - 1]
                            pe.wait_ge(o_out, i * 2 + (j + 1))
                            for q in range(BLK // P):
                                r = nc.tensor.transpose(ps_o[j][:, q * P:(q + 1) * P], oT[:, j, q * P:(q + 1) * P], g.ident[:, :])
                            r.then_inc(o_turned, 1)

            @block.scalar
            def _(act):
                with act.Fori(0, NBLK // 2) as i:
                    for slot in range(SLOTS):
                        if slot < M:
                            act.wait_ge(ins, i * M + (slot + 1))
                            act.wait_ge(su_done, i * M + (slot + 1))
                            nc.scalar.activation(sg[:, slot % 2, :], ps_g[slot % 2][:, :], ACT.Silu, scale=1 / WS).then_inc(silu, 1)
                        m = slot - 1
                        if 0 <= m < M:
                            act.wait_ge(hid, i * M + (m + 3))
                            act.wait_ge(down, i * M + (m + 1))
                            nc.scalar.activation(h1[:, m % HB, :], h[:, m % 2, :], ACT.Copy).then_inc(cast, 1)
                        if slot in last_down:
                            j = last_down[slot]
                            act.wait_ge(down, i * M + (j * NC + NC + HB))
                            act.wait_ge(added, i * 2 + (j + 1))
                            nc.scalar.activation(oT[:, j, :], ps_o[j][:, :], ACT.Copy, scale=1 / WS).then_inc(o_out, 1)

            @block.gpsimd
            def _(pool):
                pool.sem_inc(split, 2)
                with pool.Fori(0, NBLK // 2) as i:
                    for m in range(M):
                        pool.wait_ge(cast, i * M + (m + 1))
                        nc.gpsimd.tensor_tensor(h2[:, m % HB, :], h[:, m % 2, :], h1[:, m % HB, :], ALU.subtract).then_inc(split, 1)

            @block.vector
            def _(dve):
                dve.sem_inc(hid, 2)
                dve.sem_inc(su_done, 2)
                dve.sem_inc(added, 2)
                with dve.Fori(0, NBLK // 2) as i:
                    for slot in range(SLOTS):
                        if slot < M:
                            dve.wait_ge(silu, i * M + (slot + 1))
                            nc.vector.tensor_tensor(su[:, slot % 2, :], sg[:, slot % 2, :], ps_u[slot % 2][:, :], ALU.mult).then_inc(su_done, 1)
                            dve.wait_ge(su_done, i * M + (slot + 3))
                            dve.wait_ge(split, i * M + (slot + 1))
                            nc.vector.scalar_tensor_tensor(h[:, slot % 2, :], su[:, slot % 2, :], g.cols[:, 8:9], ps_c[slot // REP % 2][:, :],
                                                           ALU.mult, ALU.mult).then_inc(hid, 1)
                        if slot - 2 in last_down:
                            j = last_down[slot - 2]
                            dve.wait_ge(o_turned, i * 2 + (j + 1))
                            xb = g.xb4[:, i * 2 + j, :]
                            nc.vector.tensor_tensor(xb, ps_o[j][:, :], xb, ALU.add).then_inc(added, 1)


class PairedRouting:

    G, EPS = 4, 1e-9

    @staticmethod
    def tiles(sb):
        return dict(top=sb("r_top", [P, NT]), eq=sb("r_eq", [P, NT, 4]), den=sb("r_den", [P, NT]), inv=sb("r_inv", [P, NT]),
                    us=sb("r_us", [P, NT, 4]), ui=sb("r_ui", [P, NT, 4]), order=sb("r_order", [P, 4]), done=sb("r_done", [P, 1]))

    @staticmethod
    def loads(x, w):
        return [(x["order"][:, :], w["order"])]

    @staticmethod
    def route(nc, step, sg, comb, x):
        G = PairedRouting.G
        v, T = nc.vector, [P, NT, G]
        macro, micro = sg[:, :, 0:G], sg[:, :, G:3 * G].rearrange("p t (g e) -> p t g e", e=2)
        step(v.tensor_reduce(x["top"][:, :], macro, AX.X, ALU.max))
        step(v.tensor_tensor(x["eq"][:, :, :], macro, x["top"][:, :, None].broadcast_to(T), ALU.is_equal))
        step(v.tensor_tensor(x["eq"][:, :, :], x["eq"][:, :, :], x["order"][:, None, :].broadcast_to(T), ALU.mult))
        step(v.tensor_reduce(x["inv"][:, :], x["eq"][:, :, :], AX.X, ALU.max))
        step(v.tensor_tensor(x["eq"][:, :, :], x["eq"][:, :, :], x["inv"][:, :, None].broadcast_to(T), ALU.is_equal))
        step(v.tensor_scalar(x["den"][:, :], x["top"][:, :], PairedRouting.EPS, None, ALU.add))
        step(v.reciprocal(x["inv"][:, :], x["den"][:, :]))
        step(v.tensor_tensor(x["top"][:, :], x["top"][:, :], x["inv"][:, :], ALU.mult))
        step(v.tensor_tensor(x["eq"][:, :, :], x["eq"][:, :, :], x["top"][:, :, None].broadcast_to(T), ALU.mult))
        step(v.tensor_tensor(x["us"][:, :, :], micro[:, :, :, 0], micro[:, :, :, 1], ALU.add))
        step(v.tensor_scalar(x["us"][:, :, :], x["us"][:, :, :], PairedRouting.EPS, None, ALU.add))
        step(v.reciprocal(x["ui"][:, :, :], x["us"][:, :, :]))
        step(v.tensor_tensor(x["ui"][:, :, :], x["ui"][:, :, :], x["eq"][:, :, :], ALU.mult))
        for e in range(2):
            step(v.tensor_tensor(comb[:, :, :].rearrange("p t (g e) -> p t g e", e=2)[:, :, :, e], micro[:, :, :, e], x["ui"][:, :, :], ALU.mult))


class GroupedRouting:

    G, PER, TOPG, SCALE, TAKEN = 8, 4, 4, 2.5, -3.0e38

    @staticmethod
    def tiles(sb):
        E = 32
        return dict(bias=sb("r_bias", [P, E]), sc=sb("r_sc", [P, NT, E]), hi=sb("r_hi", [P, NT, 8, 2]), lo=sb("r_lo", [P, NT, 8, 2]),
                    a=sb("r_a", [P, NT, 8]), b=sb("r_b", [P, NT, 8]), gs=sb("r_gs", [P, NT, 8]),
                    gt=sb("r_gt", [P, NT, 8, 8]), eq=sb("r_eq", [P, NT, 8, 8]), before=sb("r_before", [P, 8, 8]),
                    m8=sb("r_m8", [P, NT, 8]), left=sb("r_left", [P, NT, E]), w=sb("r_w", [P, NT, E]), sum=sb("r_sum", [P, NT]),
                    inv=sb("r_inv", [P, NT]), done=sb("r_done", [P, 1]))

    @staticmethod
    def loads(x, w):
        return [(x["bias"][:, :], w["bias"]), (x["before"][:, :, :], w["before"])]

    @staticmethod
    def route(nc, step, sg, comb, x):
        R, v, E = GroupedRouting, nc.vector, 32
        step(v.tensor_tensor(x["sc"][:, :, :], sg[:, :, :], x["bias"][:, None, :].broadcast_to([P, NT, E]), ALU.add))
        sc = x["sc"][:, :, :].rearrange("p t (g k two) -> p (t g) k two", g=R.G, two=2)
        hi, lo = (x[n][:, :, :, :].rearrange("p t g k -> p (t g) k") for n in ("hi", "lo"))
        step(v.tensor_tensor(hi, sc[:, :, :, 0], sc[:, :, :, 1], ALU.max))
        step(v.tensor_tensor(lo, sc[:, :, :, 0], sc[:, :, :, 1], ALU.min))
        a, b, gs = (x[n][:, :, :].rearrange("p t g -> p (t g)") for n in ("a", "b", "gs"))
        step(v.tensor_tensor(a, hi[:, :, 0], hi[:, :, 1], ALU.min))
        step(v.tensor_tensor(b, lo[:, :, 0], lo[:, :, 1], ALU.max))
        step(v.tensor_tensor(b, a, b, ALU.max))
        step(v.tensor_tensor(a, hi[:, :, 0], hi[:, :, 1], ALU.max))
        step(v.tensor_tensor(gs, a, b, ALU.add))
        mine = x["gs"][:, :, :, None].broadcast_to([P, NT, 8, 8])
        other = x["gs"][:, :, None, :].broadcast_to([P, NT, 8, 8])
        step(v.tensor_tensor(x["gt"][:, :, :, :], other, mine, ALU.is_gt))
        step(v.tensor_tensor(x["eq"][:, :, :, :], other, mine, ALU.is_equal))
        step(v.tensor_tensor(x["eq"][:, :, :, :], x["eq"][:, :, :, :], x["before"][:, None, :, :].broadcast_to([P, NT, 8, 8]), ALU.mult))
        step(v.tensor_tensor(x["gt"][:, :, :, :], x["gt"][:, :, :, :], x["eq"][:, :, :, :], ALU.add))
        step(v.tensor_reduce(x["a"][:, :, :], x["gt"][:, :, :, :], AX.X, ALU.add))
        step(v.tensor_scalar(x["b"][:, :, :], x["a"][:, :, :], float(R.TOPG) - 0.5, None, ALU.is_lt))
        step(v.tensor_tensor(x["sc"][:, :, :].rearrange("p t (g k) -> p (t g) k", k=R.PER), x["sc"][:, :, :].rearrange("p t (g k) -> p (t g) k", k=R.PER),
                             b[:, :, None].broadcast_to([P, NT * 8, R.PER]), ALU.mult))
        for t in range(NT):
            r = v.max(x["m8"][:, t, :], x["sc"][:, t, :])
        step(r)
        for t in range(NT):
            r = v.match_replace(x["left"][:, t, :], x["m8"][:, t, :], x["sc"][:, t, :], R.TAKEN)
        step(r)
        step(v.tensor_scalar(x["left"][:, :, :], x["left"][:, :, :], R.TAKEN / 2, None, ALU.is_lt))
        step(v.tensor_tensor(x["w"][:, :, :], x["left"][:, :, :], sg[:, :, :], ALU.mult))
        step(v.tensor_reduce(x["sum"][:, :], x["w"][:, :, :], AX.X, ALU.add))
        step(v.tensor_scalar(x["sum"][:, :], x["sum"][:, :], 1e-20, 1.0 / R.SCALE, ALU.add, ALU.mult))
        step(v.reciprocal(x["inv"][:, :], x["sum"][:, :]))
        step(v.tensor_tensor(comb[:, :, 0:E], x["w"][:, :, :], x["inv"][:, :, None].broadcast_to([P, NT, E]), ALU.mult))
        step(v.memset(comb[:, :, E:E + 1], 1.0))


ONLY = None


class Resident:
    pass


def network(nc, a, out, stop=99):
    with ExitStack() as c:
        sb = lambda n, s, d=F32: c.enter_context(nc.sbuf_tensor(n, s, d))
        g = Resident()
        g.x = sb("x_sb", [P, NT, D])
        g.x8 = g.x[:, :, :].rearrange("p (i k) d -> p i k d", k=8)
        g.xb = g.x[:, :, :].rearrange("p (b q) d -> p b (q d)", q=QT)
        g.xnT = sb("xnT", [P, B, S])
        g.xnT8 = g.xnT[:, :, :].rearrange("p (i k) s -> p i (k s)", k=4)
        g.xnTb = g.xnT[:, :, :].rearrange("p (i k) s -> p i (k s)", k=2)
        g.mv = sb("mv", [P, NT, 2])
        g.mean8 = g.mv[:, :, 0].rearrange("p (i k) -> p i k", k=8)
        g.std, g.rstd = sb("std", [P, NT]), sb("rstd", [P, NT])
        g.rstd8 = g.rstd[:, :].rearrange("p (i k) -> p i k", k=8)
        g.ident, g.sel, g.ones = sb("ident", [P, P]), sb("sel", [P, P]), sb("ones", [P, P])
        g.cols = sb("cols", [P, 10])
        g.blocks32 = sb("blocks32", [P, 4])
        g.blocks = sb("blocks", [P, 4], F16)
        g.xt = g.x[:, :, :].rearrange("p (b q) d -> p q b d", q=QT)
        g.xb3 = g.x[:, :, :].rearrange("p (b q) d -> p b q d", q=QT)
        g.xb4 = g.x[:, :, :].rearrange("p (j k) d -> p j (k d)", k=4)
        g.meant = g.mv[:, :, 0].rearrange("p (b q) -> p q b", q=QT)
        g.rstdt = g.rstd[:, :].rearrange("p (b q) -> p q b", q=QT)
        g.rms, g.rrms = sb("rms", [P, NT]), sb("rrms", [P, NT])
        g.ones2 = sb("ones2", [1, S])
        g.ident16 = sb("ident16", [P, P], F16)
        g.ctx_a = nc.dram_tensor("ctx_a", (P, B, LK), F16, kind="Internal").ap()
        g.ctx_b = nc.dram_tensor("ctx_b", (CB, B, LK), F16, kind="Internal").ap()
        g.ctxT_dram, g.ctxV_dram = a["ctxT"], a["ctxV"]
        arrived, made, copied = (c.enter_context(nc.semaphore(n)) for n in ("arrived", "made", "copied"))
        with nc.Block() as block:
            @block.sync
            def _(sp):
                sp.dma_start(g.x[:, :, :], a["x"]).then_inc(arrived, 16)
                sp.dma_start(g.ident[:, :], a["ident"]).then_inc(arrived, 16)
                sp.dma_start(g.sel[:, :], a["sel"]).then_inc(arrived, 16)
                sp.dma_start(g.cols[:, :], a["cols"]).then_inc(arrived, 16)
                sp.dma_start(g.blocks32[:, :], a["blocks"]).then_inc(arrived, 16)
                sp.wait_ge(arrived, 80)

            @block.vector
            def _(dve):
                nc.vector.memset(g.ones2[:, :], 1.0)
                nc.vector.memset(g.ones[:, :], 1.0).then_inc(made, 1)
                dve.wait_ge(arrived, 80)
                nc.vector.tensor_copy(g.blocks[:, :], g.blocks32[:, :]).then_inc(made, 1)
                nc.vector.tensor_copy(g.ident16[:, :], g.ident[:, :]).then_inc(made, 1)
                dve.wait_ge(made, 3)
        phases = [
            lambda: (layer_norm(nc, g, "n0", context=True), small_attention(nc, g, "a0", a["a0"], 8 ** -0.5, True, normed=True)),
            lambda: head_mix_ffn(nc, g, "f0", a["f0"]),
            lambda: wide_attention(nc, g, "a1", a["a1"], 16, 2, 64, 64 ** -0.5, 2, True, False),
            lambda: conv_ffn(nc, g, "f1", a["f1"]),
            lambda: wide_attention(nc, g, "a2", a["a2"], 1, 1, 128, 1.0, 4, False, True),
            lambda: expert_ffn(nc, g, "f2", a["f2"], 2048, 256, False, PairedRouting),
            lambda: small_attention(nc, g, "a3", a["a3"], 8 ** -0.5, False),
            lambda: expert_ffn(nc, g, "f3", a["f3"], 2176, 64, True, GroupedRouting),
        ]
        if ONLY is not None:
            phases = [phases[k] for k in ONLY]
        for p in phases[:stop]:
            p()
        with nc.Block() as block:
            @block.sync
            def _(sp):
                sp.dma_start(out, g.x[:, :, :]).then_inc(copied, 16)
                sp.wait_ge(copied, 16)


def laid_out(inputs):
    import numpy as np
    f = {k: np.asarray(v) for k, v in inputs.items()}
    a = {}
    a["x"] = f["x"].reshape(NT, P, D).transpose(1, 0, 2)
    ctx = f["ctx_512"]
    a["ctxT"] = ctx.transpose(2, 0, 1)
    ctxv = np.zeros((B, KT * P, DC), np.float32)
    ctxv[:, :LK] = ctx
    a["ctxV"] = ctxv.reshape(B, KT, P, DC).transpose(2, 0, 1, 3)
    a["ident"] = np.eye(P, dtype=np.float32)
    part = np.arange(P)
    a["sel"] = (part[:, None] == part[None, :] // 32 * 32 + 8).astype(np.float32)
    cols = np.zeros((P, 10), np.float32)
    cols[:, 0] = LN_EPS
    cols[:, 1] = np.where(part % 32 == 24, 1.0, 8 ** -0.5)
    cols[:, 2] = np.where(part % 32 // 8 == 1, -1.0, 0.0)
    cols[:, 3] = np.where(part % 32 // 8 == 2, -1.0, 0.0)
    cols[:, 4] = np.where(part < DC, 0.0, -1.0)
    cols[:, 5] = np.where(part < DC, -1.0, 0.0)
    cols[:, 6] = 1e-6
    cols[:, 7] = np.where(part == DC, 0.0, -1.0)
    cols[:, 8] = 1 / 128
    cols[:, 9] = cols[:, 1] * cols[:, 3]
    a["cols"] = cols
    a["blocks"] = (part[:, None] // 32 == np.arange(4)[None, :]).astype(np.float32)

    def small(name, Wq, bq, Wk, bk, Wv, bv, Wo, bo):
        wq = np.zeros((P, 16, 32), np.float32)
        wk = np.zeros((CB, 16, 32), np.float32)
        wv = np.zeros((CB, 16, 32), np.float32)
        b = np.zeros((4, 32, 4), np.float32)
        for r in range(3):
            wq[:, :, 8 * r:8 * r + 8] = Wq.reshape(D, 16, 8)
            wk[:DC, :, 8 * r:8 * r + 8] = Wk.reshape(DC, 16, 8)
            if bk is not None:
                wk[DC:, :, 8 * r:8 * r + 8] = bk.reshape(16, 8)
                b[:, 8 * r:8 * r + 8, :] = bq.reshape(4, 4, 8).transpose(1, 2, 0)
        wk[DC:, :, 24] = 1
        wv[:DC, :, 0:8] = Wv.reshape(DC, 16, 8)
        if bv is not None:
            wv[DC:, :, 0:8] = bv.reshape(16, 8)
        wv[DC:, :, 8] = 1
        twice = lambda m: np.concatenate([m[:DC], m[:DC]])
        for n, v, s in (("wq", wq, (P, 4, P)), ("wk_a", twice(wk), (P, 4, P)), ("wk_b", wk, (CB, 4, P)),
                        ("wv_a", twice(wv), (P, 4, P)), ("wv_b", wv, (CB, 4, P)), ("wo", Wo, (P, D)),
                        ("bq", b, (P, 4)), ("bo", bo if bo is not None else np.zeros(D, np.float32), (1, D))):
            a[f"{name}.{n}"] = v.reshape(s)

    small("a0", *(f[f"L0_xattn_{n}"] for n in ("Wq", "bq", "Wk", "bk", "Wv", "bv", "Wo", "bo")))
    Wkv = f["L3_xattn_Wkv"]
    small("a3", f["L3_xattn_Wq"].T, None, Wkv[:D].T, None, Wkv[D:].T, None, f["L3_xattn_Wo"].T, None)
    heads = lambda m: m.reshape(m.shape[0], 16, 64).transpose(2, 1, 0)
    a["a1.wq"], a["a1.wk"], a["a1.wv"] = (heads(f["L1_xattn_" + n]) for n in ("Wq", "Wk", "Wv"))
    a["a1.wo"] = f["L1_xattn_Wo"].reshape(16, 64, D).transpose(1, 0, 2)
    a["a1.bo"] = f["L1_xattn_bo"][None]
    a["a2.wq"], a["a2.wk"] = f["L2_xattn_Wq"].T[:, None], f["L2_xattn_Wk"].T[:, None]
    a["a2.wv"] = f["L2_xattn_Wv"][:, None]
    a["a2.bq"], a["a2.bo"] = f["L2_xattn_bq"][:, None], f["L2_xattn_bv"][None]
    h = {k[7:]: v for k, v in f.items() if k.startswith("L0_ffn_")}
    a["f0.wq"], a["f0.wdT"], a["f0.wup"], a["f0.wo"] = h["Wq"], h["Wdown"].T, h["Wup"], h["Wo"]
    a["f0.bdown"], a["f0.bo"] = h["bdown"][:, None], h["bo"][None]
    a["f0.brow"] = np.concatenate([h["bq"], h["bup"]])[None]
    a["f0.gamma1"], a["f0.gamma2"] = h["gamma1"][:, None], h["gamma2"][:, None]
    a["f0.wg"], a["f0.bg"] = h["Wg"], np.broadcast_to(h["bg"], (P, 8))
    a["f0.we"] = h["We"].transpose(1, 0, 2).reshape(D, 8 * D)
    h = {k[7:]: v for k, v in f.items() if k.startswith("L1_ffn_")}
    a["f1.w1"] = h["w1"].T
    a["f1.w2"] = h["w2"].T.reshape(4, P, D).transpose(1, 0, 2).reshape(P, 512)
    a["f1.convw"] = h["conv_w"].reshape(4, P, 3).transpose(1, 0, 2)
    a["f1.convb"] = h["conv_b"].reshape(4, P).T
    h = {k[7:]: v for k, v in f.items() if k.startswith("L2_ffn_")}
    a["f2.wr"] = np.concatenate([h["macro_w"], h["micro_w"].transpose(1, 0, 2).reshape(D, 8)], 1)
    a["f2.wg"], a["f2.wu"] = (h[n].transpose(1, 0, 2).reshape(D, 16, P) for n in ("gate_w", "up_w"))
    a["f2.wd"] = h["down_w"].reshape(16, P, D).transpose(1, 0, 2)
    a["f2.sel"] = (np.arange(8)[:, None] == np.arange(2048)[None] // 256).astype(np.float32).reshape(8, 16, P)
    a["f2.sel"] = np.concatenate([a["f2.sel"]] * 2)
    a["f2.order"] = np.broadcast_to(np.arange(4, 0, -1, dtype=np.float32), (P, 4))
    h = {k[7:]: v for k, v in f.items() if k.startswith("L3_ffn_")}
    a["f3.wr"] = h["gate_w"].T
    a["f3.wg"], a["f3.wu"] = (np.concatenate([h[n].reshape(2048, D), h[m]]).T.reshape(D, 17, P)
                              for n, m in (("w_gate", "sh_gate"), ("w_up", "sh_up")))
    a["f3.wd"] = np.concatenate([h["w_down"].transpose(0, 2, 1).reshape(2048, D), h["sh_down"].T]).reshape(17, P, D).transpose(1, 0, 2)
    a["f3.sel"] = (np.arange(33)[:, None] == np.minimum(np.arange(2176)[None] // 64, 32)).astype(np.float32).reshape(33, 17, P)
    a["f3.sel"] = np.concatenate([a["f3.sel"]] * 2)
    a["f3.bias"] = np.broadcast_to(h["gate_bias"], (P, 32))
    a["f3.before"] = np.broadcast_to(np.tril(np.ones((8, 8), np.float32), -1), (P, 8, 8))
    return a


def kernel(**inputs):
    import numpy as np
    import concourse.bacc as bacc
    from concourse.bass_utils import run_bass_kernel_spmd

    nc = bacc.Bacc("TRN2", target_bir_lowering=False, num_devices=1)
    arrays, a = {}, {}
    for name, v in laid_out(inputs).items():
        v = np.ascontiguousarray(v)
        arrays["in_" + name.replace(".", "_")] = v
        t = nc.dram_tensor("in_" + name.replace(".", "_"), v.shape, F32, kind="ExternalInput").ap()
        if "." in name:
            a.setdefault(name.split(".")[0], {})[name.split(".")[1]] = t
        else:
            a[name] = t
    out = nc.dram_tensor("out", (P, NT, D), F32, kind="ExternalOutput").ap()
    network(nc, a, out)
    r = run_bass_kernel_spmd(nc, [arrays], core_ids=[0])
    return r.results[0]["out"].transpose(1, 0, 2).reshape(B, S, D)
```
